# Optimizing a Trainium2 kernel written in Bass

```python
import numpy as np
import jax
import jax.numpy as jnp

def _softmax(x, axis=-1):
    return jax.nn.softmax(x, axis=axis)

def _gelu(x):
    return jax.nn.gelu(x, approximate=True)

def _silu(x):
    return jax.nn.silu(x)

def _sigmoid(x):
    return jax.nn.sigmoid(x)

def _layernorm(x, axis=-1, eps=1e-05):
    m = jnp.mean(x, axis=axis, keepdims=True)
    v = jnp.var(x, axis=axis, keepdims=True)
    return (x - m) / jnp.sqrt(v + eps)

def _scatter_add(tgt, idx, src, axis=0):
    return tgt.at[idx].add(src)

def _segment_sum(src, seg, n):
    return jax.ops.segment_sum(src, seg, n)
kernel_name = 'mk_adaln_ffn_d1_seqx_r8_f12fe8'

def setup_inputs(seed: int=0):
    np.random.seed(seed)
    _w = jnp.asarray

    def _rec_inputs():
        import jax
        import jax.numpy as jnp
        _rk = jax.random.key(seed)
        x = -0.0002928 + 1 * jax.random.normal(jax.random.fold_in(_rk, 1), (4, 256, 128), jnp.float32)
        _lenS = 256 - jax.random.randint(jax.random.fold_in(_rk, 7), (4,), 0, max(1, 256 // 4) + 1, jnp.int32)
        _lenS2 = 256 - jax.random.randint(jax.random.fold_in(_rk, 8), (4,), 0, max(1, 256 // 4) + 1, jnp.int32)
        fside_16xSxS_0 = -5.72187e-05 + 0.999849 * jax.random.normal(jax.random.fold_in(_rk, 11), (16, 256, 256), jnp.float32)
        cond_64 = -0.0265395 + 0.99382 * jax.random.normal(jax.random.fold_in(_rk, 13), (4, 64), jnp.float32)
        _validS = jnp.arange(256)[None, :] < _lenS[:, None]
        _validS2 = jnp.arange(256)[None, :] < _lenS2[:, None]
        _causal = jnp.tril(jnp.ones((256, 256), dtype=bool))
        mask_BxS_bk0 = jnp.logical_not(jnp.broadcast_to(_validS[:, :], (4, 256)))
        return (x, fside_16xSxS_0, cond_64, mask_BxS_bk0)
    x, fside_16xSxS_0, cond_64, mask_BxS_bk0 = _rec_inputs()

    def _L0_cond_setup():
        import jax, jax.numpy as jnp
        import numpy as np
        B, N, DIM, H, DH = (2, 256, 128, 16, 64)
        INNER = H * DH
        EPS = 1e-05

        def layernorm(x, g):
            mean = jnp.mean(x, axis=-1, keepdims=True)
            var = jnp.var(x, axis=-1, keepdims=True)
            return (x - mean) * jax.lax.rsqrt(var + EPS) * g
        key = jax.random.key(seed)
        ks = jax.random.split(key, 10)
        x = jax.random.normal(ks[0], (B, N, DIM), dtype=jnp.float32)
        attn_bias = jax.random.normal(ks[1], (H, N, N), dtype=jnp.float32)
        mask = jax.random.randint(ks[2], (B, N), 0, 2).astype(bool)
        g_in = jnp.ones((DIM,), dtype=jnp.float32)
        null_attn_bias = jax.random.normal(ks[3], (H,), dtype=jnp.float32)
        null_kv = jax.random.normal(ks[4], (2, DH), dtype=jnp.float32)
        Wq = jax.random.normal(ks[5], (DIM, INNER), dtype=jnp.float32) * 0.02
        Wkv = jax.random.normal(ks[6], (DIM, 2 * DH), dtype=jnp.float32) * 0.02
        Wo = jax.random.normal(ks[7], (INNER, DIM), dtype=jnp.float32) * 0.02
        g_out = jnp.ones((DIM,), dtype=jnp.float32)
        return {'x': x, 'attn_bias': attn_bias, 'mask': mask, 'g_in': g_in, 'null_attn_bias': null_attn_bias, 'null_kv': null_kv, 'Wq': Wq, 'Wkv': Wkv, 'Wo': Wo, 'g_out': g_out}
    _L0_cond_all = _L0_cond_setup()
    _L0_cond_in = {k: v for k, v in _L0_cond_all.items() if k in ('g_in', 'null_attn_bias', 'Wq', 'Wkv', 'Wo', 'g_out')}
    del _L0_cond_all

    def _L0_ffn_setup():
        import jax, jax.numpy as jnp
        import numpy as np
        H, KVH, HD, D = (8, 2, 128, 128)
        E, TOPK, FFN = (8, 2, 448)
        THETA, EPS = (1000000.0, 1e-05)
        NBITS, GS = (4, 128)
        QMAX = float(2 ** NBITS - 1)
        NEG = -1e+30

        def qgroup(w):
            shp = w.shape
            w2 = w.reshape(-1, GS)
            wmax = jnp.max(w2, -1, keepdims=True)
            wmin = jnp.min(w2, -1, keepdims=True)
            scales = jnp.clip(wmax - wmin, 1e-05, None) / QMAX
            base = jnp.clip(jnp.round(-wmin / scales), 0.0, QMAX)
            wq = (jnp.clip(jnp.round(w2 / scales) + base, 0.0, QMAX) - base) * scales
            return wq.reshape(shp)

        def rms(x, g):
            return x * jax.lax.rsqrt(jnp.mean(x * x, -1, keepdims=True) + EPS) * g

        def rot_half(x):
            h = x.shape[-1] // 2
            return jnp.concatenate([-x[..., h:], x[..., :h]], axis=-1)
        key = jax.random.key(seed)
        ks = jax.random.split(key, 12)
        B, S = (2, 128)
        n = lambda k, s: 0.02 * jax.random.normal(k, s, dtype=jnp.float32)
        return {'hidden_states': jax.random.normal(ks[0], (B, S, D), dtype=jnp.float32), 'w_q': n(ks[1], (H * HD, D)), 'w_k': n(ks[2], (KVH * HD, D)), 'w_v': n(ks[3], (KVH * HD, D)), 'w_o': n(ks[4], (D, H * HD)), 'g1': jnp.ones((D,), jnp.float32), 'g2': jnp.ones((D,), jnp.float32), 'w_gate': n(ks[5], (E, D)), 'w1': n(ks[6], (E, FFN, D)), 'w3': n(ks[7], (E, FFN, D)), 'w2': n(ks[8], (E, D, FFN))}
    _L0_ffn_all = _L0_ffn_setup()
    _L0_ffn_in = {k: v for k, v in _L0_ffn_all.items() if k in ('w_q', 'w_k', 'w_v', 'w_o', 'g1', 'g2', 'w_gate', 'w1', 'w3', 'w2')}
    del _L0_ffn_all
    return {'x': x, 'fside_16xSxS_0': fside_16xSxS_0, 'cond_64': cond_64, 'mask_BxS_bk0': mask_BxS_bk0, 'L0_cond_g_in': _L0_cond_in['g_in'], 'L0_cond_null_attn_bias': _L0_cond_in['null_attn_bias'], 'L0_cond_Wq': _L0_cond_in['Wq'], 'L0_cond_Wkv': _L0_cond_in['Wkv'], 'L0_cond_Wo': _L0_cond_in['Wo'], 'L0_cond_g_out': _L0_cond_in['g_out'], 'L0_ffn_w_q': _L0_ffn_in['w_q'], 'L0_ffn_w_k': _L0_ffn_in['w_k'], 'L0_ffn_w_v': _L0_ffn_in['w_v'], 'L0_ffn_w_o': _L0_ffn_in['w_o'], 'L0_ffn_g1': _L0_ffn_in['g1'], 'L0_ffn_g2': _L0_ffn_in['g2'], 'L0_ffn_w_gate': _L0_ffn_in['w_gate'], 'L0_ffn_w1': _L0_ffn_in['w1'], 'L0_ffn_w3': _L0_ffn_in['w3'], 'L0_ffn_w2': _L0_ffn_in['w2']}

def reference(x, fside_16xSxS_0, cond_64, mask_BxS_bk0, L0_cond_g_in, L0_cond_null_attn_bias, L0_cond_Wq, L0_cond_Wkv, L0_cond_Wo, L0_cond_g_out, L0_ffn_w_q, L0_ffn_w_k, L0_ffn_w_v, L0_ffn_w_o, L0_ffn_g1, L0_ffn_g2, L0_ffn_w_gate, L0_ffn_w1, L0_ffn_w3, L0_ffn_w2):
    import jax
    import jax.numpy as jnp

    def _L0_cond_ref(x, attn_bias, mask, g_in, null_attn_bias, null_kv, Wq, Wkv, Wo, g_out):
        import jax, jax.numpy as jnp
        import numpy as np
        B, N, DIM, H, DH = (2, 256, 128, 16, 64)
        INNER = H * DH
        EPS = 1e-05

        def layernorm(x, g):
            mean = jnp.mean(x, axis=-1, keepdims=True)
            var = jnp.var(x, axis=-1, keepdims=True)
            return (x - mean) * jax.lax.rsqrt(var + EPS) * g
        b, n, _ = x.shape
        scale = DH ** (-0.5)
        xn = layernorm(x, g_in)
        q = (xn @ Wq).reshape(b, n, H, DH).transpose(0, 2, 1, 3) * scale
        kv = xn @ Wkv
        k, v = (kv[..., :DH], kv[..., DH:])
        nk = jnp.broadcast_to(null_kv[0], (b, 1, DH))
        nv = jnp.broadcast_to(null_kv[1], (b, 1, DH))
        k = jnp.concatenate([nk, k], axis=1)
        v = jnp.concatenate([nv, v], axis=1)
        sim = jnp.einsum('bhid,bjd->bhij', q, k)
        null_col = jnp.broadcast_to(null_attn_bias[:, None, None], (H, n, 1))
        bias = jnp.concatenate([null_col, attn_bias], axis=-1)
        sim = sim + bias
        neg = -jnp.finfo(sim.dtype).max
        j = n + 1
        causal_mask = jnp.triu(jnp.ones((n, j), dtype=bool), k=j - n + 1)
        sim = jnp.where(causal_mask, neg, sim)
        mask_p = jnp.pad(mask, ((0, 0), (1, 0)), constant_values=True)
        sim = jnp.where(mask_p[:, None, None, :], sim, neg)
        attn = jax.nn.softmax(sim, axis=-1)
        out = jnp.einsum('bhij,bjd->bhid', attn, v)
        out = out.transpose(0, 2, 1, 3).reshape(b, n, INNER)
        out = out @ Wo
        return layernorm(out, g_out)

    def _L0_ffn_ref(hidden_states, w_q, w_k, w_v, w_o, g1, g2, w_gate, w1, w3, w2):
        import jax, jax.numpy as jnp
        import numpy as np
        H, KVH, HD, D = (8, 2, 128, 128)
        E, TOPK, FFN = (8, 2, 448)
        THETA, EPS = (1000000.0, 1e-05)
        NBITS, GS = (4, 128)
        QMAX = float(2 ** NBITS - 1)
        NEG = -1e+30

        def qgroup(w):
            shp = w.shape
            w2 = w.reshape(-1, GS)
            wmax = jnp.max(w2, -1, keepdims=True)
            wmin = jnp.min(w2, -1, keepdims=True)
            scales = jnp.clip(wmax - wmin, 1e-05, None) / QMAX
            base = jnp.clip(jnp.round(-wmin / scales), 0.0, QMAX)
            wq = (jnp.clip(jnp.round(w2 / scales) + base, 0.0, QMAX) - base) * scales
            return wq.reshape(shp)

        def rms(x, g):
            return x * jax.lax.rsqrt(jnp.mean(x * x, -1, keepdims=True) + EPS) * g

        def rot_half(x):
            h = x.shape[-1] // 2
            return jnp.concatenate([-x[..., h:], x[..., :h]], axis=-1)
        B, S, _ = hidden_states.shape
        T = B * S
        xn = rms(hidden_states, g1)
        q = (xn @ qgroup(w_q).T).reshape(B, S, H, HD).transpose(0, 2, 1, 3)
        k = (xn @ qgroup(w_k).T).reshape(B, S, KVH, HD).transpose(0, 2, 1, 3)
        v = (xn @ qgroup(w_v).T).reshape(B, S, KVH, HD).transpose(0, 2, 1, 3)
        k = qgroup(k)
        pos = jnp.arange(S, dtype=jnp.float32)
        inv = 1.0 / THETA ** (jnp.arange(0, HD, 2, dtype=jnp.float32) / HD)
        freqs = pos[:, None] * inv[None, :]
        emb = jnp.concatenate([freqs, freqs], axis=-1)
        cos = jnp.cos(emb)[None, None]
        sin = jnp.sin(emb)[None, None]
        q = q * cos + rot_half(q) * sin
        k = k * cos + rot_half(k) * sin
        rep = H // KVH
        k = jnp.repeat(k, rep, axis=1)
        v = jnp.repeat(v, rep, axis=1)
        v = qgroup(v)
        scores = jnp.einsum('bhqd,bhkd->bhqk', q, k) / np.float32(np.sqrt(HD))
        causal = jnp.tril(jnp.ones((S, S), dtype=bool))
        scores = jnp.where(causal[None, None], scores, NEG)
        attn = jax.nn.softmax(scores, axis=-1)
        o = jnp.einsum('bhqk,bhkd->bhqd', attn, v).transpose(0, 2, 1, 3).reshape(B, S, H * HD)
        h = hidden_states + o @ qgroup(w_o).T
        hn = rms(h, g2).reshape(T, D)
        logits = hn @ w_gate.T
        probs = jax.nn.softmax(logits, axis=-1)
        tv, ti = jax.lax.top_k(probs, TOPK)
        tv = tv / jnp.sum(tv, axis=-1, keepdims=True)
        rw = jnp.zeros((T, E), hn.dtype).at[jnp.arange(T)[:, None], ti].set(tv)
        moe = jnp.zeros((T, D), hn.dtype)
        for e in range(E):
            up = jax.nn.silu(hn @ qgroup(w1[e]).T) * (hn @ qgroup(w3[e]).T)
            moe = moe + rw[:, e:e + 1] * (up @ qgroup(w2[e]).T)
        return h + moe.reshape(B, S, D)
    x = x + _L0_ffn_ref(_L0_cond_ref(x, fside_16xSxS_0, mask_BxS_bk0, L0_cond_g_in, L0_cond_null_attn_bias, cond_64, L0_cond_Wq, L0_cond_Wkv, L0_cond_Wo, L0_cond_g_out), L0_ffn_w_q, L0_ffn_w_k, L0_ffn_w_v, L0_ffn_w_o, L0_ffn_g1, L0_ffn_g2, L0_ffn_w_gate, L0_ffn_w1, L0_ffn_w3, L0_ffn_w2)
    return x

_drawn_inputs = setup_inputs


def setup_inputs(seed=0):
    import zlib

    import numpy as np

    out = dict(_drawn_inputs(seed))
    spreads = {'L0_cond_g_in': (1.0, 0.2),
     'L0_cond_g_out': (1.0, 0.2),
     'L0_ffn_g1': (1.0, 0.2),
     'L0_ffn_g2': (1.0, 0.6)}
    factors = {'L0_ffn_w_q': 8.0,
     'L0_ffn_w_k': 8.0,
     'L0_ffn_w_gate': 8.0,
     'L0_ffn_w1': 8.0,
     'L0_ffn_w3': 8.0,
     'L0_ffn_w2': 8.0}
    for name, (base, spread) in spreads.items():
        noise = np.random.default_rng([zlib.crc32(name.encode()), seed]).standard_normal(out[name].shape)
        drawn = base * np.exp(spread * noise) if base else spread * noise
        out[name] = jnp.asarray(drawn.astype(out[name].dtype))
    for name, factor in factors.items():
        out[name] = (out[name] * factor).astype(out[name].dtype)
    return out
```

```python
from contextlib import ExitStack

import numpy as np

import concourse.bass as bass
from concourse import mybir

F32 = mybir.dt.float32
F32R = mybir.dt.float32r
BF16 = mybir.dt.bfloat16
U8 = mybir.dt.uint8
ALU = mybir.AluOpType
ACT = mybir.ActivationFunctionType
AX = mybir.AxisListType

P = 128
EPS = 1e-5
MASKED = -1e30
MAGIC = 1.5 * 2.0**23
QMAX = 15.0


def build(nc, x, bias, cond, mask, g_in, null_bias, Wq, Wkv, Wo, g_out, w_q, w_k, w_v, w_o,
          g1, g2, w_gate, w1, w3, w2, rope_tok, rope_feat, out, dbg=None):
    B, N, D = x.shape
    T = B * N // P
    NT = B * N
    DH = cond.shape[1]
    HA = bias.shape[0]
    PAIRS_A = HA // 2
    HB = w_q.shape[0] // D
    KVH = w_k.shape[0] // D
    PAIRS_B = HB // 2
    E, FFN, _ = w1.shape
    HALF = NT // 2
    FC = 4
    FP = FFN // FC
    assert (B, N, D, DH) == (4, 256, P, 64) and FP == 112

    ctx = ExitStack()
    with ctx:
        def sb(name, shape, dt=F32):
            return ctx.enter_context(nc.sbuf_tensor(name, shape, dt))

        def sem(name):
            return ctx.enter_context(nc.semaphore(name))

        ps = ctx.enter_context(nc.psum_tensor("ps", [P, 8, 512], F32))

        identf = sb("identf", [P, P])
        identb = sb("identb", [P, P], BF16)
        gin_c = sb("gin_c", [P, 1])
        gout_b = sb("gout_b", [P, D])
        nk_b = sb("nk_b", [P, DH])
        vn_b = sb("vn_b", [P, DH])
        vn_c = sb("vn_c", [P, 1])
        nb_b = sb("nb_b", [P, HA])
        mask_u = sb("mask_u", [P, B, N], U8)
        mask_i1 = sb("mask_i1", [P, B, N], BF16)
        mask_i0 = sb("mask_i0", [P, B, P], BF16)
        x_sb = sb("x_sb", [P, T, D])
        xh = sb("xh", [P, T, D])
        xnT = sb("xnT", [P, NT])
        stats = sb("stats", [P, T, 6])
        mv = sb("mv", [P, T, 2])
        std = sb("std", [P, T])
        rstd = sb("rstd", [P, T])
        wkv_sb = sb("wkv_sb", [P, 2 * DH])
        wkk = sb("wkk", [P, P])
        kT = sb("kT", [P, 2, NT])
        kz = [kT[:, h, :] for h in range(2)]
        v_sb = sb("v_sb", [P, T, DH])
        wq_full = sb("wq_full", [P, HA * DH])
        u_sb = sb("u_sb", [P, HA])
        snull = sb("snull", [P, T, HA])
        wq_p = sb("wq_p", [P, P])
        bias_sb = [sb(f"bias{i}", [P, 2, (i + 1) * P]) for i in range(2)]
        qT = sb("qT", [P, NT])
        px = [sb(f"px{u}", [P, 4, N + 1]) for u in range(4)]
        negm = [sb(f"negm{u}", [P, 4]) for u in range(4)]
        sums = [sb(f"sums{u}", [P, 4]) for u in range(4)]
        rec = [sb(f"rec{u}", [P, 4]) for u in range(4)]
        pt = [sb(f"pt{k}", [P, 8, P]) for k in range(2)]
        oT = sb("oT", [P, PAIRS_A, NT])
        wo_sb = sb("wo_sb", [P, PAIRS_A, D])

        y_sb = sb("y_sb", [P, T, D])
        tmp = px[3][:].rearrange("p k c -> p (k c)")[:, 0:T * D].rearrange("p (t d) -> p t d", t=T)
        ssq = sb("ssq", [P, T])
        g1_c = sb("g1_c", [P, 1])
        g2_c = sb("g2_c", [P, 1])
        x_hi = sb("x_hi", [P, NT], F32R)
        x_lo = sb("x_lo", [P, NT], F32R)
        GB = HB + 2 * KVH + HB
        wraw = sb("wraw", [P, GB, D])
        wint = sb("wint", [P, HB, D], BF16)
        q_stat = sb("q_stat", [P, 8, 32])
        wqT = sb("wqT", [P, HB, D], F32R)
        wqrT = sb("wqrT", [P, HB, D], F32R)
        sq_swap = sb("sq_swap", [P, HB])
        wkvT = sb("wkvT", [P, 2 * KVH * D])
        woT = sb("woT", [P, HB, D])
        kv_sb = sb("kv_sb", [P, T, 2 * KVH, D])
        k_rot = sb("k_rot", [P, T, KVH, D])
        cs_tok = sb("cs_tok", [P, 2, 2, D])
        cs_feat = sb("cs_feat", [P, 2, N])
        causal = sb("causal", [P, P], BF16)
        qa = [sb(f"qa{k}", [P, HALF]) for k in range(2)]
        qb = [sb(f"qb{k}", [P, HALF]) for k in range(2)]
        qrT = [sb(f"qrT{k}", [P, 2, NT]) for k in range(2)]
        wg = sb("wg", [E, D])
        wgT = sb("wgT", [P, E])
        lg = sb("lg", [P, T, E])
        lgm = sb("lgm", [P, T])
        spare = wraw[:].rearrange("p g d -> p (g d)")
        cmp = spare[:, 0:512].rearrange("p (t e f) -> p t e f", t=T, e=E)
        cmq = spare[:, 512:1024].rearrange("p (t e f) -> p t e f", t=T, e=E)
        below = sb("below", [P, E, E])
        rank = sb("rank", [P, T, E])
        rw = sb("rw", [P, T, E])
        rsm = sb("rsm", [P, T])
        hx = wq_full[:].rearrange("p (t d) -> p t d", t=T)
        w13 = spare[0:FP, 1024:1024 + 2 * FC * D].rearrange("p (g d) -> p g d", g=2 * FC)
        w2r = kv_sb[0:DH].rearrange("p t g d -> p (t g) d")[:, 0:7, :]
        i13 = sb("i13", [FP, 2 * FC, D], BF16)
        st13 = sb("st13", [P, 8, 16])
        s13 = sb("s13", [FP, 2 * FC])
        w13T = sb("w13T", [P, 2 * FC, FP], F32R)
        w2T = sb("w2T", [FP, FC, D])
        hr = k_rot[:, :, 0, :]
        hr_hi = wqT[:].rearrange("p h d -> p (h d)")
        hr_lo = wqrT[:].rearrange("p h d -> p (h d)")
        gate = [qa[k][0:FP, :] for k in range(2)]
        up = [qb[k][0:FP, :] for k in range(2)]
        zrow = sb("zrow", [P, P])
        moeT = qrT[0][:, 0, :]

        sems = {}

        def ev(name):
            if name not in sems:
                sems[name] = sem(name)
            return sems[name]

        s_x, s_small, s_wkv, s_wqf, s_wo, s_mask = (sem(n) for n in
                                                    ("x_in", "small_in", "wkv_in", "wqf_in", "wo_in", "mask_in"))
        s_wqp, s_bias1, s_bias0 = sem("wqp_in"), sem("bias1_in"), sem("bias0_in")
        s_ident, s_pool0 = sem("ident_ready"), sem("pool_setup")
        s_dve0, s_act0, s_pe0 = sem("dve_setup"), sem("act_setup"), sem("pe_setup")
        s_q, s_qev = sem("q_product"), sem("q_copied")
        s_scored, s_added, s_max, s_exp = sem("scored"), sem("bias_added"), sem("max_taken"), sem("exp_done")
        s_rec, s_norm, s_turn = sem("sum_inverted"), sem("probs_normalised"), sem("probs_turned")
        s_pta, s_ptd, s_pv, s_oev = sem("turned_copied_act"), sem("turned_copied_dve"), sem("values_mixed"), sem("mix_copied")
        s_wod, s_ln2 = sem("wo_done"), sem("ln2_chain")
        s_out = sem("out_written")
        s_zero = sem("key_rows_zeroed")

        block = ctx.enter_context(nc.Block())

        def unit(u):
            i = 1 if u < 2 else 0
            return i, u % 2, (i + 1) * P

        def blk(i, hd, b2, jt):
            return (hd * 2 + b2) * (i + 1) + jt

        def pt_banks(u):
            return (4, 5) if u < 2 else ((4,) if u == 2 else (5,))

        DV = dict(ln=1)
        dve_marks = {}
        mark = dve_marks.__setitem__

        @block.sync
        def _(sp):
            sp.dma_start(x_sb[:], x.rearrange("b (i p) d -> p (b i) d", p=P)).then_inc(s_x, 16)
            sp.dma_start(wkv_sb[:], Wkv).then_inc(s_wkv, 16)
            sp.dma_start(wq_full[:], Wq).then_inc(s_wqf, 16)
            small = [
                (gin_c[:], g_in.rearrange("(d o) -> d o", o=1)),
                (gout_b[:], g_out.partition_broadcast(P)),
                (nk_b[:], cond[0].partition_broadcast(P)),
                (vn_b[:], cond[1].partition_broadcast(P)),
                (vn_c[0:DH, :], cond[1].rearrange("(d o) -> d o", o=1)),
                (vn_c[DH:P, :], cond[1].rearrange("(d o) -> d o", o=1)),
                (nb_b[:], null_bias.partition_broadcast(P)),
            ]
            for dst, src in small:
                sp.dma_start(dst, src).then_inc(s_small, 16)
            sp.dma_start(mask_u[:], mask.partition_broadcast(P)).then_inc(s_mask, 16)

            def load_pair(hp, s_in=None):
                sp.dma_start(wq_p[:], Wq[:, bass.ts(hp, P)]).then_inc(s_wqp, 16)
                sp.dma_start(bias_sb[1][:], bias[bass.ts(hp, 2), P:N, :].rearrange("h q k -> q h k")).then_inc(s_bias1, 16)
                sp.dma_start(bias_sb[0][:], bias[bass.ts(hp, 2), 0:P, 0:P].rearrange("h q k -> q h k")).then_inc(s_bias0, 16)

            load_pair(0)
            sp.dma_start(wo_sb[:], Wo.rearrange("(c p) d -> p c d", p=P)).then_inc(s_wo, 16)
            for n, (dst, src) in enumerate([
                    (wraw[:, 0:HB, :], w_q.rearrange("(h p) d -> p h d", p=P)),
                    (wraw[:, HB:HB + KVH, :], w_k.rearrange("(h p) d -> p h d", p=P)),
                    (wraw[:, HB + KVH:HB + 2 * KVH, :], w_v.rearrange("(h p) d -> p h d", p=P)),
                    (wraw[:, HB + 2 * KVH:GB, :], w_o.rearrange("p (h d) -> p h d", d=D)),
                    (g1_c[:], g1.rearrange("(d o) -> d o", o=1)),
                    (g2_c[:], g2.rearrange("(d o) -> d o", o=1)),
                    (cs_tok[:], rope_tok.rearrange("(i p) a d -> p i a d", p=P)),
                    (cs_feat[:], rope_feat),
                    (wg[:], w_gate)]):
                sp.dma_start(dst, src).then_inc(ev("b_in"), 16)
            sp.wait_ge(ev("wq_scales"), 1)
            half = P // 2
            sp.dma_start(sq_swap[0:half, :], q_stat[half:P, 2, 0:HB]).then_inc(ev("scales_swapped"), 16)
            sp.dma_start(sq_swap[half:P, :], q_stat[0:half, 2, 0:HB]).then_inc(ev("scales_swapped"), 16)
            sp.wait_ge(ev("result"), T)
            sp.dma_start(out.rearrange("b (i p) d -> p (b i) d", p=P), hx).then_inc(s_out, 16)
            sp.wait_ge(s_out, 16)

        @block.gpsimd
        def _(pool):
            pool.memset(identf[:], 0.0).then_inc(s_pool0, 1)
            pool.wait_ge(s_pool0, 1)
            pool.affine_select(out=identf[:], in_=identf[:], compare_op=ALU.not_equal, fill=1.0, base=0,
                               pattern=[[-1, P]], channel_multiplier=1).then_inc(s_ident, 1)
            pool.wait_ge(s_ident, 1)
            pool.tensor_copy(identb[:], identf[:]).then_inc(s_ident, 1)
            pool.memset(below[:], 1.0).then_inc(s_pool0, 1)
            pool.memset(causal[:], 0.0).then_inc(s_pool0, 1)
            pool.wait_ge(s_pool0, 3)
            pool.affine_select(out=below[:], in_=below[:], compare_op=ALU.is_ge, fill=0.0, base=-1,
                               pattern=[[1, E], [-1, E]], channel_multiplier=0).then_inc(ev("b_const"), 1)
            pool.affine_select(out=causal[:], in_=causal[:], compare_op=ALU.is_ge, fill=MASKED, base=0,
                               pattern=[[-1, P]], channel_multiplier=1).then_inc(ev("b_const"), 1)
            pool.wait_ge(s_dve0, 22)
            pool.affine_select(out=mask_i0[:], in_=mask_i0[:], compare_op=ALU.is_ge, fill=MASKED, base=0,
                               pattern=[[0, B], [-1, P]], channel_multiplier=1).then_inc(s_pool0, 1)
            pool.affine_select(out=mask_i1[:, :, P:N], in_=mask_i1[:, :, P:N], compare_op=ALU.is_ge, fill=MASKED,
                               base=0, pattern=[[0, B], [-1, P]], channel_multiplier=1).then_inc(s_pool0, 1)

            def normalise(U, u):
                i, bh, W = unit(u)
                pool.wait_ge(s_rec, U + 1)
                pool.tensor_tensor(px[u][:, :, 0:W], px[u][:, :, 0:W], rec[u][:].unsqueeze(2).to_broadcast([P, 4, W]),
                                   ALU.mult).then_inc(s_norm, 1)

            def pair(hp, first=False):
                if not first:
                    normalise(hp * 4 - 1, 3)
                for u in range(3):
                    normalise(hp * 4 + u, u)

            pair(0, True)
            with pool.Fori(1, PAIRS_A) as hp:
                pair(hp)
            normalise(PAIRS_A * 4 - 1, 3)

            def rope_sum(hp, hd, half):
                f = (hp * 2 + hd) * 2 + half
                pool.wait_ge(ev("q_rotated"), 2 * f + 2)
                if hp >= 2:
                    pool.wait_ge(ev("scored_b"), (hp - 1) * 4)
                pool.tensor_tensor(qrT[hp % 2][:, hd, half * HALF:(half + 1) * HALF], qa[f % 2][:], qb[f % 2][:],
                                   ALU.add).then_inc(ev("q_summed"), 1)

            def normalise_b(hp, u):
                i, bh, W = unit(u)
                pool.wait_ge(ev("inverted_b"), hp * 4 + u + 1)
                pool.tensor_tensor(px[u][:, :, 0:W], px[u][:, :, 0:W], rec[u][:].unsqueeze(2).to_broadcast([P, 4, W]),
                                   ALU.mult).then_inc(ev("normalised_b"), 1)

            for hd in range(2):
                for half in range(2):
                    rope_sum(0, hd, half)
            for hp in range(PAIRS_B):
                for u in range(4):
                    if hp + 1 < PAIRS_B:
                        rope_sum(hp + 1, u // 2, u % 2)
                    normalise_b(hp, u)

            pool.wait_ge(ev("h_ready"), 1)
            pool.tensor_tensor(hx, y_sb[:], x_sb[:], ALU.add).then_inc(ev("hx_ready"), 1)

            def round_c(n):
                pool.wait_ge(ev("scaled_c"), n + 1)
                pool.sem_inc(ev("pool_rounds"), 1)
                for g in range(8):
                    ins = pool.tensor_scalar(w13[:, g, :], w13[:, g, :], st13[0:FP, 5, g:g + 1], MAGIC, ALU.min, ALU.add)
                for g in range(7):
                    ins = pool.tensor_scalar(w2r[:, g, :], w2r[:, g, :], st13[0:DH, 5, 8 + g:9 + g], MAGIC, ALU.min, ALU.add)
                ins.then_inc(ev("rounded_c"), 1)

            round_c(0)
            with pool.Fori(1, E) as e:
                round_c(e)

        @block.scalar
        def _(act):
            act.wait_ge(s_dve0, 16)
            act.activation(std[:], mv[:, :, 1], ACT.Sqrt, bias=EPS).then_inc(s_act0, 1)
            act.wait_ge(s_pe0, 8)
            act.wait_ge(s_small, 16 * 7)
            act.activation(xnT[:], ps[:, 0:2, :].rearrange("p b c -> p (b c)"), ACT.Copy, scale=gin_c[:, 0:1]).then_inc(s_act0, 1)
            act.wait_ge(s_pe0, 10)
            act.wait_ge(s_zero, 2)
            for h in range(2):
                r = slice(DH * h, DH * h + DH)
                act.activation(kz[h][r, :], ps[r, 2:4, :].rearrange("p b c -> p (b c)"), ACT.Copy,
                               scale=float(DH) ** -0.5).then_inc(s_act0, 1)

            def exps(hp, u):
                i, bh, W = unit(u)
                act.wait_ge(s_max, hp * 4 + u + 1)
                for k in range(4):
                    ins = act.activation(px[u][:, k, 0:W + 1], px[u][:, k, 0:W + 1], ACT.Exp, bias=negm[u][:, k:k + 1],
                                         accum_out=sums[u][:, k:k + 1])
                ins.then_inc(s_exp, 1)

            def turned_copy(hp, u):
                act.wait_ge(s_turn, hp * 4 + u + 1)
                if not (isinstance(hp, int) and hp * 4 + u < 2):
                    act.wait_ge(s_pv, hp * 4 + u - 1)
                act.activation(pt[u % 2][:, 0:4, :], ps[:, 4, :].rearrange("p (k c) -> p k c", k=4), ACT.Copy).then_inc(s_pta, 1)

            def mix_copy(hp, u):
                i, bh, W = unit(u)
                act.wait_ge(s_pv, hp * 4 + u + 1)
                dst = oT[:, hp, :].rearrange("p (b i c) -> p b i c", b=B, i=2)[:, 2 * bh:2 * bh + 2, i, :]
                act.activation(dst, ps[:, 6, 0:2 * P].rearrange("p (b c) -> p b c", b=2), ACT.Identity,
                               bias=vn_c[:, 0:1]).then_inc(s_oev, 1)

            def q_copy(hp, half):
                act.wait_ge(s_q, hp * 2 + half + 1)
                if not isinstance(hp, int) or hp:
                    act.wait_ge(s_scored, hp * 4)
                act.activation(qT[:, half * HALF:(half + 1) * HALF], ps[:, 7, :], ACT.Copy).then_inc(s_qev, 1)

            def load_queries(hp):
                act.dma_start(wq_p[:], Wq[:, bass.ts(hp, P)]).then_inc(s_wqp, 16)

            def load_bias(hp, i):
                src = bias[bass.ts(hp, 2), i * P:(i + 1) * P, 0:(i + 1) * P].rearrange("h q k -> q h k")
                act.dma_start(bias_sb[i][:], src).then_inc(s_bias1 if i else s_bias0, 16)

            def pair(hp, first=False, last=False):
                if not first:
                    turned_copy(hp - 1, 2)
                    mix_copy(hp - 1, 2)
                    mix_copy(hp - 1, 3)
                exps(hp, 0)
                if not last:
                    load_queries(hp + 1)
                exps(hp, 1)
                if not last:
                    load_bias(hp + 1, 1)
                turned_copy(hp, 0)
                exps(hp, 2)
                mix_copy(hp, 0)
                if not last:
                    q_copy(hp + 1, 0)
                exps(hp, 3)
                turned_copy(hp, 1)
                if not last:
                    load_bias(hp + 1, 0)
                    q_copy(hp + 1, 1)
                mix_copy(hp, 1)

            q_copy(0, 0)
            q_copy(0, 1)
            pair(0, first=True)
            with act.Fori(1, PAIRS_A - 1) as hp:
                pair(hp)
            pair(PAIRS_A - 1, last=True)
            turned_copy(PAIRS_A - 1, 2)
            mix_copy(PAIRS_A - 1, 2)
            mix_copy(PAIRS_A - 1, 3)
            def root(src, dst, scale, before, after, n=1):
                act.wait_ge(before, n)
                act.activation(dst, src, ACT.Sqrt, bias=EPS, scale=scale).then_inc(after, 1)

            root(mv[:, :, 1], std[:], 1.0, ev("ln2_stats"), ev("ln2_root"), T)

            root(ssq[:], std[:], 1.0 / D, ev("rms1_sum"), ev("rms1_root"))
            act.wait_ge(ev("b_in"), 16 * 9)
            act.wait_ge(ev("rms1_turned"), 1)
            act.activation(xnT[:], ps[:, 0:2, :].rearrange("p b c -> p (b c)"), ACT.Copy, scale=g1_c[:, 0:1]).then_inc(ev("xn1_ready"), 1)
            act.wait_ge(ev("wq_turned"), 1)
            turned = ps[:, 4, :].bitcast(BF16).rearrange("p (h c) -> p h c", h=HB)
            act.activation(wqT[:], turned, ACT.Copy).then_inc(ev("wqT_ready"), 1)
            half = P // 2
            act.activation(wqrT[:, :, 0:half], turned[:, :, half:P], ACT.Copy).then_inc(ev("wqT_ready"), 1)
            act.activation(wqrT[:, :, half:P], turned[:, :, 0:half], ACT.Copy).then_inc(ev("wqT_ready"), 1)
            act.wait_ge(ev("wkv_turned"), 1)
            act.activation(wkvT[:], ps[:, 5, :], ACT.Copy).then_inc(ev("wkvT_ready"), 1)
            act.wait_ge(ev("wo_turned"), 1)
            act.activation(woT[:], ps[:, 6:8, :].rearrange("p b (h c) -> p (b h) c", c=D), ACT.Copy).then_inc(ev("woT_ready"), 1)
            for t in range(T):
                act.wait_ge(ev("kv_product"), t + 1)
                act.activation(kv_sb[:, t, :, :], ps[:, t, :].rearrange("p (g c) -> p g c", c=D), ACT.Copy).then_inc(ev("kv_copied"), 1)
            for kv in range(KVH):
                act.wait_ge(ev("k_turned"), kv + 1)
                act.activation(kT[:, kv, :], ps[:, 2 * kv:2 * kv + 2, :].rearrange("p b c -> p (b c)"), ACT.Copy,
                               scale=float(D) ** -0.5).then_inc(ev("kT_ready"), 1)

            def exps_b(hp, u):
                i, bh, W = unit(u)
                act.wait_ge(ev("max_b"), hp * 4 + u + 1)
                if hp:
                    act.wait_ge(ev("turned_b"), hp * 4 + u - 3)
                for k in range(4):
                    src = ps[:, 2 * (u % 2) + k // 2, (k % 2) * W:(k % 2 + 1) * W]
                    ins = act.activation(px[u][:, k, 0:W], src, ACT.Exp, bias=negm[u][:, k:k + 1],
                                         accum_out=sums[u][:, k:k + 1])
                ins.then_inc(ev("exp_b"), 1)

            def turned_copy_b(hp, u):
                n = hp * 4 + u
                act.wait_ge(ev("turned_b"), n + 1)
                if n >= 2:
                    act.wait_ge(ev("mixed_b"), n - 1)
                act.activation(pt[u % 2][:, 0:4, :], ps[:, 4, :].rearrange("p (k c) -> p k c", k=4), ACT.Copy).then_inc(ev("copied_act_b"), 1)

            def mix_copy_b(hp, u):
                i, bh, W = unit(u)
                act.wait_ge(ev("mixed_b"), hp * 4 + u + 1)
                for hd in range(2):
                    dst = oT[:, 2 * hp + hd, :].rearrange("p (b i c) -> p b i c", b=B, i=2)[:, 2 * bh:2 * bh + 2, i, :]
                    ins = act.activation(dst, ps[:, 6, hd * 2 * P:(hd + 1) * 2 * P].rearrange("p (b c) -> p b c", b=2), ACT.Copy)
                ins.then_inc(ev("mix_copied_b"), 1)

            for hp in range(PAIRS_B):
                if hp:
                    turned_copy_b(hp - 1, 2)
                    mix_copy_b(hp - 1, 2)
                    mix_copy_b(hp - 1, 3)
                exps_b(hp, 0)
                exps_b(hp, 1)
                turned_copy_b(hp, 0)
                exps_b(hp, 2)
                mix_copy_b(hp, 0)
                exps_b(hp, 3)
                turned_copy_b(hp, 1)
                mix_copy_b(hp, 1)
            turned_copy_b(PAIRS_B - 1, 2)
            mix_copy_b(PAIRS_B - 1, 2)
            mix_copy_b(PAIRS_B - 1, 3)

            root(ssq[:], std[:], 1.0 / D, ev("rms2_sum"), ev("rms2_root"))
            act.wait_ge(ev("rms2_turned"), 1)
            act.activation(xnT[:], ps[:, 0:2, :].rearrange("p b c -> p (b c)"), ACT.Copy, scale=g2_c[:, 0:1]).then_inc(ev("hn_ready"), 1)
            act.activation(wgT[:], ps[:, 3, 0:E], ACT.Copy).then_inc(ev("wgT_ready"), 1)
            act.wait_ge(ev("logits_shifted"), 1)
            act.activation(lg[:], lg[:], ACT.Exp).then_inc(ev("gates_exp"), 1)

            def load_expert(e, n):
                if not isinstance(n, int) or n:
                    act.wait_ge(ev("ints_c"), n)
                w1e = w1[bass.ts(e, 1)].rearrange("e (c p) d -> p (e c) d", p=FP)
                w3e = w3[bass.ts(e, 1)].rearrange("e (c p) d -> p (e c) d", p=FP)
                w2e = w2[bass.ts(e, 1)].rearrange("e (r a) f -> r (e a f)", a=2)
                act.dma_start(w13[:, 0:FC, :], w1e).then_inc(ev("w1_in"), 16)
                act.dma_start(w13[:, FC:2 * FC, :], w3e).then_inc(ev("w3_in"), 16)
                act.wait_ge(ev("w2_turned"), n + 0) if (not isinstance(n, int) or n) else None
                act.dma_start(w2r.rearrange("r g c -> r (g c)"), w2e).then_inc(ev("w2_in"), 16)

            def copies_c(e):
                act.wait_ge(ev("w13_turned"), e + 1)
                act.activation(w13T[:], ps[:, 4, :].bitcast(BF16)[:, 0:8 * FP].rearrange("p (g c) -> p g c", c=FP),
                               ACT.Copy).then_inc(ev("w13T_ready"), 1)
                act.wait_ge(ev("hr_turned"), e * 2 + 1)
                act.activation(hr_hi[:, 0:HALF], ps[:, 5, :], ACT.Copy, scale=g2_c[:, 0:1]).then_inc(ev("hr_hi_ready"), 1)
                act.wait_ge(ev("hr_turned"), e * 2 + 2)
                act.activation(hr_hi[:, HALF:NT], ps[:, 5, :], ACT.Copy, scale=g2_c[:, 0:1]).then_inc(ev("hr_hi_ready"), 1)
                act.wait_ge(ev("w2_turned"), e + 1)
                act.activation(w2T[:], ps[0:FP, 4, :].rearrange("p (c d) -> p c d", c=FC), ACT.Copy).then_inc(ev("w2T_ready"), 1)

            def silus(e):
                for half in range(2):
                    for c in range(FC):
                        s = half * FC + c
                        act.wait_ge(ev("hidden"), e * 16 + 2 * s + 1)
                        if not (isinstance(e, int) and e == 0 and s < 2):
                            act.wait_ge(ev("up_ready"), e * 8 + s - 1)
                        act.activation(gate[s % 2], ps[0:FP, 2 * (s % 2), :], ACT.Silu, scale=s13[:, c:c + 1]).then_inc(ev("gate_ready"), 1)

            load_expert(0, 0)
            copies_c(0)
            def expert(e):
                load_expert(e + 1, e + 1)
                silus(e)
                copies_c(e + 1)

            expert(0)
            with act.Fori(1, E - 1) as e:
                expert(e)
            silus(E - 1)
            for half in range(2):
                act.wait_ge(ev("experts_summed"), half + 1)
                act.activation(moeT[:, half * HALF:(half + 1) * HALF], ps[:, 6 + half, :], ACT.Copy).then_inc(ev("moeT_ready"), 1)

        @block.vector
        def _(dve):
            n0 = [0]

            def m0(ins):
                n0[0] += 1
                ins.then_inc(s_dve0, 1)

            for h in range(2):
                dve.memset(kz[h], 0.0).then_inc(s_zero, 1)
            dve.wait_ge(s_x, 16)
            for t in range(T):
                m0(dve.bn_stats(stats[:, t, :], x_sb[:, t, :]))
            for t in range(T):
                dve.wait_ge(s_dve0, t + 1)
                m0(dve.bn_aggr(mv[:, t, :], stats[:, t, :]))
            dve.wait_ge(s_small, 16 * 7)
            dve.wait_ge(s_wqf, 16)
            dve.wait_ge(s_wkv, 16)
            m0(dve.tensor_copy(wkk[:, 0:DH], wkv_sb[:, 0:DH]))
            m0(dve.tensor_copy(wkk[:, DH:P], wkv_sb[:, 0:DH]))
            prod = oT[:, 0, :]
            m0(dve.tensor_tensor(prod.rearrange("p (h c) -> p h c", h=HA), wq_full[:].rearrange("p (h c) -> p h c", h=HA),
                                 nk_b[:].unsqueeze(1).to_broadcast([P, HA, DH]), ALU.mult))
            dve.wait_ge(s_dve0, 19)
            m0(dve.tensor_reduce(u_sb[:], prod.rearrange("p (h c) -> p h c", h=HA), AX.X, ALU.add))
            dve.wait_ge(s_mask, 16)
            m0(dve.tensor_scalar(mask_i1[:], mask_u[:], -1.0, -MASKED, ALU.add, ALU.mult))
            m0(dve.tensor_scalar(mask_i0[:], mask_u[:, :, 0:P], -1.0, -MASKED, ALU.add, ALU.mult))
            dve.wait_ge(s_act0, 1)
            m0(dve.reciprocal(rstd[:], std[:]))
            dve.wait_ge(s_dve0, 23)
            for t in range(T):
                m0(dve.tensor_scalar(xh[:, t, :], x_sb[:, t, :], mv[:, t, 0:1], rstd[:, t:t + 1], ALU.subtract, ALU.mult))
            dve.wait_ge(s_pe0, 12)
            m0(dve.tensor_tensor(v_sb[:], ps[:, 4:6, :].rearrange("p b (t c) -> p (b t) c", c=P)[:, :, DH:P],
                                 vn_b[:].unsqueeze(1).to_broadcast([P, T, DH]), ALU.subtract))
            dve.wait_ge(s_pe0, 13)
            dve.wait_ge(s_small, 16 * 7)
            m0(dve.scalar_tensor_tensor(out=snull[:], in0=ps[:, 6, 0:T * HA].rearrange("p (t h) -> p t h", h=HA),
                                        scalar=float(DH) ** -0.5, in1=nb_b[:].unsqueeze(1).to_broadcast([P, T, HA]),
                                        op0=ALU.mult, op1=ALU.add))
            dve.wait_ge(s_dve0, 33)

            def add(hp, u):
                i, bh, W = unit(u)
                dve.wait_ge(s_scored, hp * 4 + u + 1)
                dve.wait_ge(s_bias1 if i else s_bias0, hp * 16 + 16)
                if not isinstance(hp, int) or hp:
                    dve.wait_ge(s_turn, hp * 4 + u - 3)
                snv = snull[:].rearrange("p (b i) h -> p b i h", i=2)[:, 2 * bh:2 * bh + 2, i, bass.ts(hp, 2)]
                dve.tensor_copy(px[u][:, :, W].rearrange("p (h b) -> p b h", b=2), snv)
                k = u % 2
                for hd in range(2):
                    ins = dve.tensor_tensor(px[u][:, 2 * hd:2 * hd + 2, 0:W],
                                            ps[:, 2 * k + hd, 0:2 * W].rearrange("p (b c) -> p b c", b=2),
                                            bias_sb[i][:, hd, :].unsqueeze(1).to_broadcast([P, 2, W]), ALU.add)
                ins.then_inc(s_added, 1)

            def rowmax(hp, u):
                i, bh, W = unit(u)
                dve.wait_ge(s_added, hp * 4 + u + 1)
                dve.tensor_reduce(negm[u][:], px[u][:, :, 0:W + 1], AX.X, ALU.max, negate=True).then_inc(s_max, 1)

            def invert(hp, u):
                dve.wait_ge(s_exp, hp * 4 + u + 1)
                dve.reciprocal(rec[u][:], sums[u][:]).then_inc(s_rec, 1)

            def turned_copy(hp, u):
                dve.wait_ge(s_turn, hp * 4 + u + 1)
                if not (isinstance(hp, int) and hp * 4 + u < 2):
                    dve.wait_ge(s_pv, hp * 4 + u - 1)
                o = 4 if u < 2 else 0
                dve.tensor_copy(pt[u % 2][:, o:o + 4, :], ps[:, 5, :].rearrange("p (k c) -> p k c", k=4)).then_inc(s_ptd, 1)

            def pair(hp, first=False):
                add(hp, 0)
                if not first:
                    invert(hp - 1, 3)
                    turned_copy(hp - 1, 3)
                rowmax(hp, 0)
                add(hp, 1)
                rowmax(hp, 1)
                invert(hp, 0)
                add(hp, 2)
                rowmax(hp, 2)
                invert(hp, 1)
                turned_copy(hp, 0)
                add(hp, 3)
                rowmax(hp, 3)
                turned_copy(hp, 1)
                invert(hp, 2)

            pair(0, first=True)
            with dve.Fori(1, PAIRS_A) as hp:
                pair(hp)
            invert(PAIRS_A - 1, 3)
            turned_copy(PAIRS_A - 1, 3)
            chain = [0]

            def link(ins):
                chain[0] += 1
                ins.then_inc(ev("dve_chain"), 1)
                dve.wait_ge(ev("dve_chain"), chain[0])

            for t in range(T):
                dve.wait_ge(s_wod, t + 1)
                link(dve.bn_stats(stats[:, t, :], ps[:, t, 0:D]))
                dve.bn_aggr(mv[:, t, :], stats[:, t, :]).then_inc(ev("ln2_stats"), 1)
            dve.wait_ge(ev("ln2_root"), 1)
            link(dve.reciprocal(rstd[:], std[:]))
            for t in range(T):
                ins = dve.tensor_scalar(xh[:, t, :], ps[:, t, 0:D], mv[:, t, 0:1], rstd[:, t:t + 1], ALU.subtract, ALU.mult)
            link(ins)
            link(dve.tensor_tensor(y_sb[:], xh[:], gout_b[:].unsqueeze(1).to_broadcast([P, T, D]), ALU.mult))

            def rms(name):
                link(dve.tensor_tensor(tmp, y_sb[:], y_sb[:], ALU.mult))
                dve.tensor_reduce(ssq[:], tmp, AX.X, ALU.add).then_inc(ev(name + "_sum"), 1)
                dve.wait_ge(ev(name + "_root"), 1)
                link(dve.reciprocal(rstd[:], std[:]))
                for t in range(T):
                    dve.tensor_scalar(xh[:, t, :], y_sb[:, t, :], rstd[:, t:t + 1], None, ALU.mult).then_inc(ev(name + "_scaled"), 1)

            def split(name, src):
                dve.wait_ge(ev(name), 1)
                link(dve.tensor_copy(x_hi[:], src))
                link(dve.tensor_tensor(x_lo[:], src, x_hi[:].bitcast(F32), ALU.subtract))

            def group_stats(w, st, G, rows, last=None):
                r = slice(0, rows)
                dve.tensor_reduce(st[r, 0, 0:G], w, AX.X, ALU.max)
                link(dve.tensor_reduce(st[r, 1, 0:G], w, AX.X, ALU.min))
                group_levels(st, G, rows)

            def group_levels(st, G, rows):
                r = slice(0, rows)
                link(dve.tensor_tensor(st[r, 2, 0:G], st[r, 0, 0:G], st[r, 1, 0:G], ALU.subtract))
                link(dve.tensor_scalar(st[r, 2, 0:G], st[r, 2, 0:G], 1e-5, 1.0 / QMAX, ALU.max, ALU.mult))
                link(dve.reciprocal(st[r, 3, 0:G], st[r, 2, 0:G]))
                link(dve.tensor_tensor(st[r, 4, 0:G], st[r, 1, 0:G], st[r, 3, 0:G], ALU.mult))
                link(dve.tensor_scalar(st[r, 4, 0:G], st[r, 4, 0:G], MAGIC, None, ALU.add))
                link(dve.tensor_scalar(st[r, 4, 0:G], st[r, 4, 0:G], -MAGIC, 0.0, ALU.add, ALU.min))
                link(dve.tensor_scalar(st[r, 4, 0:G], st[r, 4, 0:G], -QMAX, None, ALU.max))
                link(dve.tensor_scalar(st[r, 5, 0:G], st[r, 4, 0:G], QMAX, None, ALU.add))

            def group_round(w, st, G, g0=0):
                for g in range(G):
                    s = g0 + g
                    ins = dve.tensor_scalar(w[:, g, :], w[:, g, :], st[:, 3, s:s + 1], st[:, 4, s:s + 1], ALU.mult, ALU.max)
                link(ins)
                for g in range(G):
                    s = g0 + g
                    ins = dve.tensor_scalar(w[:, g, :], w[:, g, :], st[:, 5, s:s + 1], MAGIC, ALU.min, ALU.add)
                link(ins)

            rms("rms1")
            dve.wait_ge(ev("b_in"), 16 * 9)
            group_stats(wraw[:], q_stat, GB, P)
            dve.engine_nop().then_inc(ev("wq_scales"), 1)
            group_round(wraw[:], q_stat, GB)
            dve.tensor_scalar(wint[:], wraw[:, 0:HB, :], -MAGIC, None, ALU.add).then_inc(ev("wq_ints"), 1)
            for g in range(HB, GB):
                ins = dve.tensor_scalar(wraw[:, g, :], wraw[:, g, :], -MAGIC, q_stat[:, 2, g:g + 1], ALU.add, ALU.mult)
            ins.then_inc(ev("w_dequantised"), 1)
            split("xn1_ready", xnT[:])
            dve.engine_nop().then_inc(ev("x_split"), 1)
            dve.wait_ge(ev("kv_copied"), T)
            kvf = kv_sb[:].rearrange("p t g c -> p (t g) c")
            kst = cmp.rearrange("p t e f -> p (t e f)")[:, 0:256].rearrange("p (s g) -> p s g", s=8)
            GK = T * 2 * KVH
            group_stats(kvf, kst, GK, P)
            group_round(kvf, kst, GK)
            for g in range(GK):
                ins = dve.tensor_scalar(kvf[:, g, :], kvf[:, g, :], -MAGIC, kst[:, 2, g:g + 1], ALU.add, ALU.mult)
            link(ins)
            half = D // 2
            kq = kv_sb[:].rearrange("p (b i) g c -> p b i g c", i=2)
            kr = k_rot[:].rearrange("p (b i) g c -> p b i g c", i=2)
            rot = oT[:, 0:2, :].rearrange("p a (b i c) -> p a b i c", b=B, i=2)
            for i in range(2):
                for g in range(KVH):
                    dst, src, r = kr[:, :, i, g, :], kq[:, :, i, g, :], rot[:, g, :, i, :]
                    dve.tensor_tensor(dst, src, cs_tok[:, i, 0, :].unsqueeze(1).to_broadcast([P, B, D]), ALU.mult)
                    dve.tensor_tensor(r[:, :, 0:half], src[:, :, half:D],
                                      cs_tok[:, i, 1, 0:half].unsqueeze(1).to_broadcast([P, B, half]), ALU.mult)
                    link(dve.tensor_tensor(r[:, :, half:D], src[:, :, 0:half],
                                           cs_tok[:, i, 1, half:D].unsqueeze(1).to_broadcast([P, B, half]), ALU.mult))
                    ins = dve.tensor_tensor(dst, dst, r, ALU.add)
            ins.then_inc(ev("k_ready"), 1)

            def rope_q(hp, hd, hf):
                f = (hp * 2 + hd) * 2 + hf
                h = 2 * hp + hd
                for k, (dst, scale) in enumerate(((qa, q_stat[:, 2, h:h + 1]), (qb, sq_swap[:, h:h + 1]))):
                    dve.wait_ge(ev("q_product_b"), 2 * f + k + 1)
                    if f >= 2:
                        dve.wait_ge(ev("q_summed"), f - 1)
                    if f == 0:
                        dve.wait_ge(ev("scales_swapped"), 32)
                    dve.scalar_tensor_tensor(out=dst[f % 2][:].rearrange("p (b c) -> p b c", b=2),
                                             in0=ps[:, 7, :].rearrange("p (b c) -> p b c", b=2), scalar=scale,
                                             in1=cs_feat[:, k, :].unsqueeze(1).to_broadcast([P, 2, N]),
                                             op0=ALU.mult, op1=ALU.mult).then_inc(ev("q_rotated"), 1)

            def rowmax_b(hp, u):
                i, bh, W = unit(u)
                dve.wait_ge(ev("scored_b"), hp * 4 + u + 1)
                k = u % 2
                dve.tensor_reduce(negm[u][:].rearrange("p (h b) -> p h b", h=2),
                                  ps[:, 2 * k:2 * k + 2, 0:2 * W].rearrange("p h (b c) -> p h b c", b=2),
                                  AX.X, ALU.max, negate=True).then_inc(ev("max_b"), 1)

            def invert_b(hp, u):
                dve.wait_ge(ev("exp_b"), hp * 4 + u + 1)
                dve.reciprocal(rec[u][:], sums[u][:]).then_inc(ev("inverted_b"), 1)

            def turned_copy_b(hp, u):
                n = hp * 4 + u
                dve.wait_ge(ev("turned_b"), n + 1)
                if n >= 2:
                    dve.wait_ge(ev("mixed_b"), n - 1)
                o = 4 if u < 2 else 0
                dve.tensor_copy(pt[u % 2][:, o:o + 4, :], ps[:, 5, :].rearrange("p (k c) -> p k c", k=4)).then_inc(ev("copied_dve_b"), 1)

            for hd in range(2):
                for hf in range(2):
                    rope_q(0, hd, hf)
            for hp in range(PAIRS_B):
                more = hp + 1 < PAIRS_B
                rowmax_b(hp, 0)
                if hp:
                    invert_b(hp - 1, 3)
                    turned_copy_b(hp - 1, 3)
                if more:
                    rope_q(hp + 1, 0, 0)
                rowmax_b(hp, 1)
                invert_b(hp, 0)
                if more:
                    rope_q(hp + 1, 0, 1)
                turned_copy_b(hp, 0)
                rowmax_b(hp, 2)
                invert_b(hp, 1)
                if more:
                    rope_q(hp + 1, 1, 0)
                rowmax_b(hp, 3)
                turned_copy_b(hp, 1)
                if more:
                    rope_q(hp + 1, 1, 1)
                invert_b(hp, 2)
            invert_b(PAIRS_B - 1, 3)
            turned_copy_b(PAIRS_B - 1, 3)
            for t in range(T):
                dve.wait_ge(ev("o_product"), t + 1)
                ins = dve.tensor_tensor(y_sb[:, t, :], ps[:, t, 0:D], y_sb[:, t, :], ALU.add)
            link(ins)
            dve.engine_nop().then_inc(ev("h_ready"), 1)

            rms("rms2")
            dve.wait_ge(ev("logits"), 1)
            link(dve.tensor_copy(lg[:], ps[:, 2, 0:T * E].rearrange("p (t e) -> p t e", e=E)))
            link(dve.tensor_reduce(lgm[:], lg[:], AX.X, ALU.max, negate=True))
            dve.tensor_tensor(lg[:], lg[:], lgm[:].unsqueeze(2).to_broadcast([P, T, E]), ALU.add).then_inc(ev("logits_shifted"), 1)
            dve.wait_ge(ev("gates_exp"), 1)
            dve.wait_ge(ev("b_const"), 2)
            for t in range(T):
                mine = lg[:, t, :].unsqueeze(2).to_broadcast([P, E, E])
                other = lg[:, t, :].unsqueeze(1).to_broadcast([P, E, E])
                dve.tensor_tensor(cmp[:, t, :, :], other, mine, ALU.is_gt)
                ins = dve.tensor_tensor(cmq[:, t, :, :], other, mine, ALU.is_equal)
            link(ins)
            link(dve.tensor_tensor(cmq, cmq, below[:].unsqueeze(1).to_broadcast([P, T, E, E]), ALU.mult))
            link(dve.tensor_tensor(cmp, cmp, cmq, ALU.add))
            link(dve.tensor_reduce(rank[:], cmp, AX.X, ALU.add))
            link(dve.scalar_tensor_tensor(out=rw[:], in0=rank[:], scalar=2.0, in1=lg[:], op0=ALU.is_lt, op1=ALU.mult))
            link(dve.tensor_reduce(rsm[:], rw[:], AX.X, ALU.add))
            link(dve.reciprocal(rsm[:], rsm[:]))
            link(dve.tensor_tensor(rw[:], rw[:], rsm[:].unsqueeze(2).to_broadcast([P, T, E]), ALU.mult))
            split("hn_ready", xnT[:])
            dve.engine_nop().then_inc(ev("hn_split"), 1)
            dve.memset(st13[:], 0.0).then_inc(ev("c_chain"), 1)
            dve.memset(zrow[:], 0.0).then_inc(ev("zeros"), 1)

            C_LINKS = 11

            def prepare(e):
                k = [e * C_LINKS + 1]

                def step(ins):
                    k[0] = k[0] + 1
                    ins.then_inc(ev("c_chain"), 1)
                    dve.wait_ge(ev("c_chain"), k[0])

                if not isinstance(e, int) or e:
                    dve.wait_ge(ev("hr_turned"), e * 2)
                else:
                    dve.wait_ge(ev("c_chain"), 1)
                for t in range(T):
                    ins = dve.tensor_scalar(hr[:, t, :], xh[:, t, :], rw[:, t, bass.ts(e, 1)], None, ALU.mult)
                ins.then_inc(ev("hr_weighed"), 1)
                dve.wait_ge(ev("w1_in"), e * 16 + 16)
                dve.wait_ge(ev("w3_in"), e * 16 + 16)
                dve.wait_ge(ev("w2_in"), e * 16 + 16)
                F, R = slice(0, FP), slice(0, DH)
                dve.tensor_reduce(st13[F, 0, 0:8], w13, AX.X, ALU.max)
                dve.tensor_reduce(st13[F, 1, 0:8], w13, AX.X, ALU.min)
                dve.tensor_reduce(st13[R, 0, 8:15], w2r, AX.X, ALU.max)
                step(dve.tensor_reduce(st13[R, 1, 8:15], w2r, AX.X, ALU.min))
                st = st13
                step(dve.tensor_tensor(st[:, 2, :], st[:, 0, :], st[:, 1, :], ALU.subtract))
                step(dve.tensor_scalar(st[:, 2, :], st[:, 2, :], 1e-5, 1.0 / QMAX, ALU.max, ALU.mult))
                step(dve.reciprocal(st[:, 3, :], st[:, 2, :]))
                step(dve.tensor_tensor(st[:, 4, :], st[:, 1, :], st[:, 3, :], ALU.mult))
                step(dve.tensor_scalar(st[:, 4, :], st[:, 4, :], MAGIC, None, ALU.add))
                step(dve.tensor_scalar(st[:, 4, :], st[:, 4, :], -MAGIC, 0.0, ALU.add, ALU.min))
                step(dve.tensor_scalar(st[:, 4, :], st[:, 4, :], -QMAX, None, ALU.max))
                step(dve.tensor_scalar(st[:, 5, :], st[:, 4, :], QMAX, None, ALU.add))
                for g in range(8):
                    dve.tensor_scalar(w13[:, g, :], w13[:, g, :], st[F, 3, g:g + 1], st[F, 4, g:g + 1], ALU.mult, ALU.max)
                for g in range(7):
                    ins = dve.tensor_scalar(w2r[:, g, :], w2r[:, g, :], st[R, 3, 8 + g:9 + g], st[R, 4, 8 + g:9 + g], ALU.mult, ALU.max)
                ins.then_inc(ev("scaled_c"), 1)
                return step

            def integers(e, step):
                dve.wait_ge(ev("rounded_c"), e + 1)
                if not isinstance(e, int) or e:
                    dve.wait_ge(ev("w13_turned"), e)
                step(dve.tensor_scalar(i13[:], w13, -MAGIC, None, ALU.add))
                for g in range(7):
                    ins = dve.tensor_scalar(w2r[:, g, :], w2r[:, g, :], -MAGIC, st13[0:DH, 2, 8 + g:9 + g], ALU.add, ALU.mult)
                step(ins)
                if not isinstance(e, int) or e:
                    dve.wait_ge(ev("gate_ready"), e * 8)
                dve.tensor_copy(s13[:], st13[0:FP, 2, 0:8]).then_inc(ev("ints_c"), 1)

            def low_parts(e):
                for half in range(2):
                    dve.wait_ge(ev("hr_hi_ready"), e * 2 + half + 1)
                    dve.scalar_tensor_tensor(out=hr_lo[:, half * HALF:(half + 1) * HALF], in0=ps[:, 5, :], scalar=g2_c[:, 0:1],
                                             in1=hr_hi[:, half * HALF:(half + 1) * HALF].bitcast(F32), op0=ALU.mult,
                                             op1=ALU.subtract).then_inc(ev("hr_lo_ready"), 1)

            def ups(e, steps):
                for s in steps:
                    c = s % FC
                    dve.wait_ge(ev("hidden"), e * 16 + 2 * s + 2)
                    dve.wait_ge(ev("gate_ready"), e * 8 + s + 1)
                    if not (isinstance(e, int) and e == 0 and s < 2):
                        dve.wait_ge(ev("down"), e * 8 + s - 1)
                    dve.scalar_tensor_tensor(out=up[s % 2], in0=ps[0:FP, 2 * (s % 2) + 1, :],
                                             scalar=s13[:, FC + c:FC + c + 1], in1=gate[s % 2], op0=ALU.mult,
                                             op1=ALU.mult).then_inc(ev("up_ready"), 1)

            integers(0, prepare(0))
            low_parts(0)
            def expert(e):
                ups(e, range(0, 3))
                step = prepare(e + 1)
                ups(e, range(3, 8))
                integers(e + 1, step)
                low_parts(e + 1)

            expert(0)
            with dve.Fori(1, E - 1) as e:
                expert(e)
            ups(E - 1, range(8))
            dve.wait_ge(ev("hx_ready"), 1)
            for t in range(T):
                dve.wait_ge(ev("moe_turned"), t + 1)
                moe = ps[:, t % 4, 0:D].rearrange("p (a r) -> p r a", a=2)
                dve.tensor_tensor(hx[:, t, :].rearrange("p (r a) -> p r a", a=2), moe,
                                  hx[:, t, :].rearrange("p (r a) -> p r a", a=2), ALU.add).then_inc(ev("result"), 1)

        @block.tensor
        def _(pe):
            pe.wait_ge(s_ident, 2)
            for t in range(T):
                pe.wait_ge(s_dve0, 24 + t)
                pe.transpose(ps[:, t // 4, (t % 4) * P:(t % 4) * P + P], xh[:, t, :], identf[:]).then_inc(s_pe0, 1)
            pe.wait_ge(s_act0, 2)
            for half in range(2):
                pe.matmul(ps[:, 2 + half, :], wkk[:], xnT[:, half * HALF:(half + 1) * HALF], start=True, stop=True).then_inc(s_pe0, 1)
            pe.wait_ge(s_wkv, 16)
            for t in range(T):
                ins = pe.matmul(ps[:, 4 + t // 4, (t % 4) * P:(t % 4) * P + P], xnT[:, t * P:(t + 1) * P], wkv_sb[:],
                                start=True, stop=True)
                if t % 4 == 3:
                    ins.then_inc(s_pe0, 1)
            for t in range(T):
                ins = pe.matmul(ps[:, 6, t * HA:(t + 1) * HA], xnT[:, t * P:(t + 1) * P], u_sb[:], start=True, stop=True)
            ins.then_inc(s_pe0, 1)

            def queries(hp, half):
                pe.wait_ge(s_wqp, hp * 16 + 16)
                if not (isinstance(hp, int) and hp == 0 and half == 0):
                    pe.wait_ge(s_qev, hp * 2 + half)
                pe.matmul(ps[:, 7, :], wq_p[:], xnT[:, half * HALF:(half + 1) * HALF], start=True, stop=True).then_inc(s_q, 1)

            def scores(hp, u):
                i, bh, W = unit(u)
                k = u % 2
                pe.wait_ge(s_qev, hp * 2 + bh + 1)
                if not (isinstance(hp, int) and hp * 4 + u < 2):
                    pe.wait_ge(s_added, hp * 4 + u - 1)
                for hd in range(2):
                    for b2 in range(2):
                        b = 2 * bh + b2
                        t = 2 * b + i
                        dst = ps[:, 2 * k + hd, b2 * W:(b2 + 1) * W]
                        pe.matmul(dst, qT[:, t * P:(t + 1) * P], kz[hd][:, b * N:b * N + W], start=True, stop=False)
                        m = mask_i1[:, b, :] if i else mask_i0[:, b, :]
                        ins = pe.matmul(dst, identb[:], m, start=False, stop=True)
                ins.then_inc(s_scored, 1)

            def turn(hp, u):
                i, bh, W = unit(u)
                pe.wait_ge(s_norm, hp * 4 + u + 1)
                n = hp * 3 + min(u, 2)
                if not (isinstance(hp, int) and hp * 3 + min(u, 2) == 0):
                    if 4 in pt_banks(u):
                        pe.wait_ge(s_pta, n)
                    if 5 in pt_banks(u):
                        pe.wait_ge(s_ptd, n)
                for hd in range(2):
                    for b2 in range(2):
                        for jt in range(i + 1):
                            n = blk(i, hd, b2, jt)
                            bank = pt_banks(u)[n // 4]
                            ins = pe.transpose(ps[:, bank, (n % 4) * P:(n % 4 + 1) * P],
                                               px[u][:, hd * 2 + b2, jt * P:(jt + 1) * P], identf[:])
                ins.then_inc(s_turn, 1)

            def mix(hp, u):
                i, bh, W = unit(u)
                n = hp * 3 + min(u, 2) + 1
                if 4 in pt_banks(u):
                    pe.wait_ge(s_pta, n)
                if 5 in pt_banks(u):
                    pe.wait_ge(s_ptd, n)
                if not (isinstance(hp, int) and hp * 4 + u == 0):
                    pe.wait_ge(s_oev, hp * 4 + u)
                for b2 in range(2):
                    for jt in range(i + 1):
                        for hd in range(2):
                            t = 2 * (2 * bh + b2) + jt
                            ins = pe.matmul(ps[hd * DH:(hd + 1) * DH, 6, b2 * P:(b2 + 1) * P], v_sb[:, t, :],
                                            pt[u % 2][:, blk(i, hd, b2, jt), :], start=(jt == 0), stop=(jt == i))
                ins.then_inc(s_pv, 1)

            def pair(hp, first=False, last=False):
                if not first:
                    turn(hp - 1, 2)
                    mix(hp - 1, 2)
                scores(hp, 0)
                if not first:
                    turn(hp - 1, 3)
                    mix(hp - 1, 3)
                scores(hp, 1)
                scores(hp, 2)
                if not last:
                    queries(hp + 1, 0)
                turn(hp, 0)
                mix(hp, 0)
                scores(hp, 3)
                turn(hp, 1)
                mix(hp, 1)
                if not last:
                    queries(hp + 1, 1)

            queries(0, 0)
            queries(0, 1)
            pe.wait_ge(s_pool0, 5)
            pe.wait_ge(s_act0, 4)
            pe.wait_ge(s_dve0, 33)
            pair(0, first=True)
            with pe.Fori(1, PAIRS_A - 1) as hp:
                pair(hp)
            pair(PAIRS_A - 1, last=True)
            turn(PAIRS_A - 1, 2)
            mix(PAIRS_A - 1, 2)
            turn(PAIRS_A - 1, 3)
            mix(PAIRS_A - 1, 3)
            pe.wait_ge(s_oev, PAIRS_A * 4)
            pe.wait_ge(s_wo, 16)
            for t in range(T):
                for hp in range(PAIRS_A):
                    ins = pe.matmul(ps[:, t, 0:D], oT[:, hp, t * P:(t + 1) * P], wo_sb[:, hp, :],
                                    start=(hp == 0), stop=(hp == PAIRS_A - 1))
                ins.then_inc(s_wod, 1)


            def turn_x(name):
                for t in range(T):
                    pe.wait_ge(ev(name + "_scaled"), t + 1)
                    ins = pe.transpose(ps[:, t // 4, (t % 4) * P:(t % 4) * P + P], xh[:, t, :], identf[:])
                ins.then_inc(ev(name + "_turned"), 1)

            turn_x("rms1")
            pe.wait_ge(ev("wq_ints"), 1)
            for h in range(HB):
                ins = pe.transpose(ps[:, 4, :].bitcast(BF16)[:, h * P:(h + 1) * P], wint[:, h, :], identb[:])
            ins.then_inc(ev("wq_turned"), 1)
            pe.wait_ge(ev("w_dequantised"), 1)
            for g in range(2 * KVH):
                ins = pe.transpose(ps[:, 5, g * P:(g + 1) * P], wraw[:, HB + g, :], identf[:])
            ins.then_inc(ev("wkv_turned"), 1)
            for h in range(HB):
                ins = pe.transpose(ps[:, 6 + h // 4, (h % 4) * P:(h % 4 + 1) * P], wraw[:, HB + 2 * KVH + h, :], identf[:])
            ins.then_inc(ev("wo_turned"), 1)
            pe.wait_ge(ev("xn1_ready"), 1)
            pe.wait_ge(ev("wkvT_ready"), 1)
            pe.wait_ge(ev("woT_ready"), 1)
            for t in range(T):
                pe.matmul(ps[:, t, :], xnT[:, t * P:(t + 1) * P], wkvT[:], start=True, stop=True).then_inc(ev("kv_product"), 1)
            pe.wait_ge(ev("k_ready"), 1)
            for kv in range(KVH):
                for t in range(T):
                    ins = pe.transpose(ps[:, 2 * kv + t // 4, (t % 4) * P:(t % 4 + 1) * P], k_rot[:, t, kv, :], identf[:])
                ins.then_inc(ev("k_turned"), 1)

            def queries_b(hp, hd, hf):
                h = 2 * hp + hd
                f = h * 2 + hf
                for k, w in enumerate((wqT, wqrT)):
                    if f + k:
                        pe.wait_ge(ev("q_rotated"), 2 * f + k)
                    cols = slice(hf * HALF, (hf + 1) * HALF)
                    pe.matmul(ps[:, 7, :], w[:, h, :], x_hi[:, cols], start=True, stop=False)
                    pe.matmul(ps[:, 7, :], w[:, h, :], x_lo[:, cols], start=False, stop=True).then_inc(ev("q_product_b"), 1)

            def scores_b(hp, u):
                i, bh, W = unit(u)
                n, k, kv = hp * 4 + u, u % 2, hp * KVH // PAIRS_B
                pe.wait_ge(ev("q_summed"), 4 * hp + 4)
                if n >= 2:
                    pe.wait_ge(ev("exp_b"), n - 1)
                for hd in range(2):
                    for b2 in range(2):
                        b = 2 * bh + b2
                        t = 2 * b + i
                        pe.matmul(ps[:, 2 * k + hd, b2 * W:(b2 + 1) * W], qrT[hp % 2][:, hd, t * P:(t + 1) * P],
                                  kT[:, kv, b * N:b * N + W], start=True, stop=False)
                        ins = pe.matmul(ps[:, 2 * k + hd, (b2 + 1) * W - P:(b2 + 1) * W], identb[:], causal[:],
                                        start=False, stop=True)
                ins.then_inc(ev("scored_b"), 1)

            def turn_b(hp, u):
                i, bh, W = unit(u)
                pe.wait_ge(ev("normalised_b"), hp * 4 + u + 1)
                n = hp * 3 + min(u, 2)
                if n:
                    if 4 in pt_banks(u):
                        pe.wait_ge(ev("copied_act_b"), n)
                    if 5 in pt_banks(u):
                        pe.wait_ge(ev("copied_dve_b"), n)
                for hd in range(2):
                    for b2 in range(2):
                        for jt in range(i + 1):
                            n = blk(i, hd, b2, jt)
                            ins = pe.transpose(ps[:, pt_banks(u)[n // 4], (n % 4) * P:(n % 4 + 1) * P],
                                               px[u][:, hd * 2 + b2, jt * P:(jt + 1) * P], identf[:])
                ins.then_inc(ev("turned_b"), 1)

            def mix_b(hp, u):
                i, bh, W = unit(u)
                kv = hp * KVH // PAIRS_B
                n = hp * 3 + min(u, 2) + 1
                if 4 in pt_banks(u):
                    pe.wait_ge(ev("copied_act_b"), n)
                if 5 in pt_banks(u):
                    pe.wait_ge(ev("copied_dve_b"), n)
                if hp * 4 + u:
                    pe.wait_ge(ev("mix_copied_b"), hp * 4 + u)
                probs = pt[u % 2][:, 0:4 * (i + 1), :].rearrange("p (h b j) c -> p h b j c", h=2, b=2)
                mixed = ps[:, 6, :].rearrange("p (h b c) -> p h b c", h=2, b=2)
                for b2 in range(2):
                    for jt in range(i + 1):
                        t = 2 * (2 * bh + b2) + jt
                        ins = pe.matmul(mixed[:, :, b2, :], kv_sb[:, t, KVH + kv, :], probs[:, :, b2, jt, :],
                                        start=(jt == 0), stop=(jt == i))
                ins.then_inc(ev("mixed_b"), 1)

            pe.wait_ge(ev("x_split"), 1)
            pe.wait_ge(ev("wqT_ready"), 3)
            for hd in range(2):
                for hf in range(2):
                    queries_b(0, hd, hf)
            pe.wait_ge(ev("kT_ready"), 2)
            pe.wait_ge(ev("b_const"), 2)
            for hp in range(PAIRS_B):
                more = hp + 1 < PAIRS_B
                if hp:
                    turn_b(hp - 1, 2)
                    mix_b(hp - 1, 2)
                scores_b(hp, 0)
                if hp:
                    turn_b(hp - 1, 3)
                    mix_b(hp - 1, 3)
                if more:
                    queries_b(hp + 1, 0, 0)
                scores_b(hp, 1)
                if more:
                    queries_b(hp + 1, 0, 1)
                turn_b(hp, 0)
                scores_b(hp, 2)
                mix_b(hp, 0)
                if more:
                    queries_b(hp + 1, 1, 0)
                scores_b(hp, 3)
                turn_b(hp, 1)
                if more:
                    queries_b(hp + 1, 1, 1)
                mix_b(hp, 1)
            for u in (2, 3):
                turn_b(PAIRS_B - 1, u)
                mix_b(PAIRS_B - 1, u)
            pe.wait_ge(ev("mix_copied_b"), 4 * PAIRS_B)
            for t in range(T):
                for h in range(HB):
                    ins = pe.matmul(ps[:, t, 0:D], oT[:, h, t * P:(t + 1) * P], woT[:, h, :], start=(h == 0), stop=(h == HB - 1))
                ins.then_inc(ev("o_product"), 1)

            pe.wait_ge(ev("h_ready"), 1)
            pe.transpose(ps[:, 3, 0:E], wg[:], identf[0:E, 0:E])
            turn_x("rms2")
            pe.wait_ge(ev("hn_ready"), 1)
            pe.wait_ge(ev("wgT_ready"), 1)
            for t in range(T):
                ins = pe.matmul(ps[:, 2, t * E:(t + 1) * E], xnT[:, t * P:(t + 1) * P], wgT[:], start=True, stop=True)
            ins.then_inc(ev("logits"), 1)
            pe.wait_ge(ev("zeros"), 1)
            pe.wait_ge(ev("hn_split"), 1)
            for half in range(2):
                pe.matmul(ps[:, 6 + half, :], zrow[:], xnT[:, 0:HALF], start=True, stop=False, skip_group_check=True)

            def turn_weights(e):
                pe.wait_ge(ev("ints_c"), e + 1)
                if not isinstance(e, int) or e:
                    pe.wait_ge(ev("w2T_ready"), e)
                for g in range(8):
                    ins = pe.transpose(ps[:, 4, :].bitcast(BF16)[:, g * FP:(g + 1) * FP], i13[:, g, :], identb[0:FP, 0:FP])
                ins.then_inc(ev("w13_turned"), 1)

            def turn_down(e):
                w = w2r.rearrange("r g c -> r (g c)").rearrange("r (a c f) -> r a c f", a=2, c=FC)
                for c in range(FC):
                    for a in range(2):
                        ins = pe.transpose(ps[0:FP, 4, c * P + a * DH:c * P + (a + 1) * DH], w[:, a, c, :], identf[0:DH, 0:DH])
                ins.then_inc(ev("w2_turned"), 1)

            def turn_tokens(e, half):
                if half == 0:
                    pe.wait_ge(ev("hr_weighed"), e + 1)
                else:
                    pe.wait_ge(ev("w13T_ready"), e + 1)
                if not (isinstance(e, int) and e == 0 and half == 0):
                    pe.wait_ge(ev("hr_lo_ready"), e * 2 + half)
                for t in range(4):
                    ins = pe.transpose(ps[:, 5, t * P:(t + 1) * P], hr[:, half * 4 + t, :], identf[:])
                ins.then_inc(ev("hr_turned"), 1)

            def hidden(e, s):
                half, c = s // FC, s % FC
                cols = slice(half * HALF, (half + 1) * HALF)
                k = s % 2
                if not (isinstance(e, int) and e == 0 and s < 2):
                    pe.wait_ge(ev("up_ready"), e * 8 + s - 1)
                if s == 0:
                    pe.wait_ge(ev("w13T_ready"), e + 1)
                pe.matmul(ps[0:FP, 2 * k, :], w13T[:, c, :], x_hi[:, cols], start=True, stop=False)
                pe.matmul(ps[0:FP, 2 * k, :], w13T[:, c, :], x_lo[:, cols], start=False, stop=True).then_inc(ev("hidden"), 1)
                if c == 0:
                    pe.wait_ge(ev("hr_hi_ready"), e * 2 + half + 1)
                    pe.wait_ge(ev("hr_lo_ready"), e * 2 + half + 1)
                pe.matmul(ps[0:FP, 2 * k + 1, :], w13T[:, FC + c, :], hr_hi[:, cols], start=True, stop=False)
                pe.matmul(ps[0:FP, 2 * k + 1, :], w13T[:, FC + c, :], hr_lo[:, cols], start=False, stop=True).then_inc(ev("hidden"), 1)

            def down(e, s):
                half, c = s // FC, s % FC
                if s == 0:
                    pe.wait_ge(ev("w2T_ready"), e + 1)
                pe.wait_ge(ev("up_ready"), e * 8 + s + 1)
                return pe.matmul(ps[:, 6 + half, :], w2T[:, c, :], up[s % 2], start=False, stop=False,
                                 skip_group_check=True).then_inc(ev("down"), 1)

            def expert(e, last=False):
                for s in range(8):
                    hidden(e, s)
                    if s:
                        down(e, s - 1)
                if not last:
                    turn_weights(e + 1)
                    turn_tokens(e + 1, 0)
                down(e, 7)
                if not last:
                    turn_tokens(e + 1, 1)
                    turn_down(e + 1)

            turn_weights(0)
            turn_tokens(0, 0)
            turn_tokens(0, 1)
            turn_down(0)
            expert(0)
            with pe.Fori(1, E - 1) as e:
                expert(e)
            expert(E - 1, last=True)
            for half in range(2):
                pe.matmul(ps[:, 6 + half, :], zrow[:], xnT[:, 0:HALF], start=False, stop=True,
                          skip_group_check=True).then_inc(ev("experts_summed"), 1)
            for t in range(T):
                pe.wait_ge(ev("moeT_ready"), t // 4 + 1)
                if t >= 4:
                    pe.wait_ge(ev("result"), t - 3)
                pe.transpose(ps[:, t % 4, 0:D], moeT[:, t * P:(t + 1) * P], identf[:]).then_inc(ev("moe_turned"), 1)


_NAMES = ["x", "fside_16xSxS_0", "cond_64", "mask_BxS_bk0", "L0_cond_g_in", "L0_cond_null_attn_bias", "L0_cond_Wq",
          "L0_cond_Wkv", "L0_cond_Wo", "L0_cond_g_out", "L0_ffn_w_q", "L0_ffn_w_k", "L0_ffn_w_v", "L0_ffn_w_o",
          "L0_ffn_g1", "L0_ffn_g2", "L0_ffn_w_gate", "L0_ffn_w1", "L0_ffn_w3", "L0_ffn_w2"]


def rope_tables(S, HD):
    inv = 1.0 / np.float32(1000000.0) ** (np.arange(0, HD, 2, dtype=np.float32) / np.float32(HD))
    freqs = np.arange(S, dtype=np.float32)[:, None] * inv[None, :].astype(np.float32)
    emb = np.concatenate([freqs, freqs], -1).astype(np.float32)
    sign = np.where(np.arange(HD) < HD // 2, -1.0, 1.0).astype(np.float32)
    tok = np.stack([np.cos(emb), np.sin(emb) * sign], 1).astype(np.float32)
    return np.ascontiguousarray(tok), np.ascontiguousarray(tok.transpose(2, 1, 0))


def kernel(**inputs):
    import concourse.bacc as bacc
    from concourse.bass_utils import run_bass_kernel_spmd

    nc = bacc.Bacc("TRN2", target_bir_lowering=False, num_devices=1)
    arrays, args = {}, []

    def give(name, a):
        arrays[name] = a
        args.append(nc.dram_tensor(name, a.shape, mybir.dt.from_np(a.dtype), kind="ExternalInput").ap())

    for name in _NAMES:
        give(f"in_{name}", np.ascontiguousarray(inputs[name]))
    tok, feat = rope_tables(256, 128)
    give("in_rope_tok", tok)
    give("in_rope_feat", feat)
    args.append(nc.dram_tensor("out_0", inputs["x"].shape, F32, kind="ExternalOutput").ap())
    build(nc, *args)
    r = run_bass_kernel_spmd(nc, [arrays], core_ids=[0])
    return r.results[0]["out_0"]
```

```python
from contextlib import ExitStack

import numpy as np

import concourse.bass as bass
from concourse import mybir

F32 = mybir.dt.float32
F32R = mybir.dt.float32r
BF16 = mybir.dt.bfloat16
U8 = mybir.dt.uint8
ALU = mybir.AluOpType
ACT = mybir.ActivationFunctionType
AX = mybir.AxisListType

P = 128
EPS = 1e-5
MASKED = -1e30
MAGIC = 1.5 * 2.0**23
QMAX = 15.0


def build(nc, x, bias, cond, mask, g_in, null_bias, Wq, Wkv, Wo, g_out, w_q, w_k, w_v, w_o,
          g1, g2, w_gate, w1, w3, w2, rope_tok, rope_feat, out, dbg=None):
    B, N, D = x.shape
    T = B * N // P
    NT = B * N
    DH = cond.shape[1]
    HA = bias.shape[0]
    PAIRS_A = HA // 2
    HB = w_q.shape[0] // D
    KVH = w_k.shape[0] // D
    PAIRS_B = HB // 2
    E, FFN, _ = w1.shape
    HALF = NT // 2
    FC = 4
    FP = FFN // FC
    WG0 = T * E
    assert (B, N, D, DH) == (4, 256, P, 64) and FP == 112

    ctx = ExitStack()
    with ctx:
        def sb(name, shape, dt=F32):
            return ctx.enter_context(nc.sbuf_tensor(name, shape, dt))

        def sem(name):
            return ctx.enter_context(nc.semaphore(name))

        ps = ctx.enter_context(nc.psum_tensor("ps", [P, 8, 512], F32))

        identf = sb("identf", [P, P])
        identb = sb("identb", [P, P], BF16)
        gin_c = sb("gin_c", [P, 1])
        gout_b = sb("gout_b", [P, D])
        nk_b = sb("nk_b", [P, DH])
        vn_b = sb("vn_b", [P, DH])
        vn_c = sb("vn_c", [P, 1])
        nb_b = sb("nb_b", [P, HA])
        mask_u = sb("mask_u", [P, B, N], U8)
        mask_i1 = sb("mask_i1", [P, B, N], BF16)
        mask_i0 = sb("mask_i0", [P, B, P], BF16)
        x_sb = sb("x_sb", [P, T, D])
        xh = sb("xh", [P, T, D])
        xnT = sb("xnT", [P, NT])
        stats = sb("stats", [P, T, 6])
        mv = sb("mv", [P, T, 2])
        std = sb("std", [P, T])
        rstd = sb("rstd", [P, T])
        wkv_sb = sb("wkv_sb", [P, 2 * DH])
        wkk = sb("wkk", [P, P])
        kT = sb("kT", [P, 2, NT])
        kz = [kT[:, h, :] for h in range(2)]
        v_sb = sb("v_sb", [P, T, DH])
        wq_full = sb("wq_full", [P, HA * DH])
        u_sb = sb("u_sb", [P, HA])
        snull = sb("snull", [P, T, HA])
        wq_p = sb("wq_p", [P, P])
        bias_sb = [sb(f"bias{i}", [P, 2, (i + 1) * P]) for i in range(2)]
        qT = sb("qT", [P, NT])
        px = [sb(f"px{u}", [P, 4, N + 1]) for u in range(4)]
        negm = [sb(f"negm{u}", [P, 4]) for u in range(4)]
        lowest = [sb(f"lowest{u}", [P, 4]) for u in range(4)]
        sums = [sb(f"sums{u}", [P, 4]) for u in range(4)]
        rec = [sb(f"rec{u}", [P, 4]) for u in range(4)]
        pt = [sb(f"pt{k}", [P, 8, P]) for k in range(2)]
        oT = sb("oT", [P, PAIRS_A, NT])
        wo_sb = sb("wo_sb", [P, PAIRS_A, D])

        y_sb = sb("y_sb", [P, T, D])
        squares = px[3][:].rearrange("p k c -> p (k c)")[:, 0:NT]
        ssq = sb("ssq", [P, T])
        g1_c = sb("g1_c", [P, 1])
        g2_c = sb("g2_c", [P, 1])
        x_hi = sb("x_hi", [P, NT], F32R)
        x_lo = sb("x_lo", [P, NT], F32R)
        GB = HB + 2 * KVH + HB
        wraw = sb("wraw", [P, GB, D])
        wint = sb("wint", [P, HB, D], BF16)
        q_stat = sb("q_stat", [P, 6, GB])
        wqT = sb("wqT", [P, HB, D], F32R)
        wqrT = sb("wqrT", [P, HB, D], F32R)
        sq_swap = sb("sq_swap", [P, HB])
        wkvT = sb("wkvT", [P, 2 * KVH * D])
        woT = sb("woT", [P, HB, D])
        kv_stat = sb("kv_stat", [P, 6, 2, 2, 8])
        kv_sb = sb("kv_sb", [P, T, 2 * KVH, D])
        k_rot = sb("k_rot", [P, T, KVH, D])
        rot_k = wq_full[:, 0:4 * D].rearrange("p (t d) -> p t d", t=4)
        cs_tok = sb("cs_tok", [P, 2, 2, D])
        cs_feat = sb("cs_feat", [P, 2, N])
        causal = sb("causal", [P, P], BF16)
        qa = [sb(f"qa{k}", [P, HALF]) for k in range(2)]
        qb = [sb(f"qb{k}", [P, HALF]) for k in range(2)]
        qrT = [sb(f"qrT{k}", [P, 2, NT]) for k in range(2)]
        wg = sb("wg", [E, D])
        wgT = sb("wgT", [P, E])
        lg = sb("lg", [P, T, E])
        lgm = sb("lgm", [P, T])
        gates = px[0][:].rearrange("p k c -> p (k c)")
        cmp = gates[:, 0:512].rearrange("p (t e f) -> p t e f", t=T, e=E)
        cmq = gates[:, 512:1024].rearrange("p (t e f) -> p t e f", t=T, e=E)
        below = sb("below", [P, E, E])
        rank = sb("rank", [P, T, E])
        rw = sb("rw", [P, T, E])
        rsm = sb("rsm", [P, T])
        hx = wq_full[:].rearrange("p (t d) -> p t d", t=T)
        spare = wraw[:].rearrange("p g d -> p (g d)")
        w13 = [spare[0:FP, k * 1024:k * 1024 + 2 * FC * D].rearrange("p (g d) -> p g d", g=2 * FC) for k in range(2)]
        i13 = sb("i13", [FP, 2 * FC, D], BF16)
        st13 = [sb(f"st13_{k}", [FP, 6, 2 * FC]) for k in range(2)]
        G2 = FFN * 2 // D
        R2 = D // 2
        st2 = sb("st2", [P, 6, G2])
        rotated = k_rot[:].rearrange("p t g d -> p (t g d)")
        w2r = rotated[:, 0:G2 * D].rearrange("p (g d) -> p g d", g=G2)
        w2T = rotated[0:FP, 1024:1024 + FC * 2 * D].rearrange("p (c e d) -> p c e d", c=FC, e=2)
        w13T = [sb("w13T", [P, 2 * FC, FP], F32R)[:], wqT[:, :, 0:FP]]
        free = oT[:].rearrange("p h t -> p (h t)")
        NBUF = 4
        gate = [free[0:FP, k * HALF:(k + 1) * HALF] for k in range(NBUF)]
        ups = [free[0:FP, (NBUF + k) * HALF:(NBUF + k + 1) * HALF] for k in range(NBUF)]
        up = [free[0:FP, (2 * NBUF + k) * HALF:(2 * NBUF + k + 1) * HALF] for k in range(NBUF)]
        rwb = [free[0:FP, 3 * NBUF * HALF + k * NT:3 * NBUF * HALF + (k + 1) * NT] for k in range(2)]
        rw3 = sb("rw3", [P, T, E // 2, 2, 3], BF16)
        rw_r = [sb(f"rw_r{k}", [P, T, E]) for k in range(2)]
        rwT = kT[:].rearrange("p a t -> p (a t)").bitcast(BF16).rearrange("p (q t) -> p q t", q=E // 2)
        GATE_BANKS = (5, 4, 6, 7)
        pick = sb("pick", [P, 2, FP], BF16)
        zrow = sb("zrow", [P, P], BF16)
        finite = mask_i1[:, 0:2, :].rearrange("p b c -> p (b c)")
        moeT = qrT[0][:, 0, :]

        sems = {}

        def ev(name):
            if name not in sems:
                sems[name] = sem(name)
            return sems[name]

        s_x, s_small, s_wkv, s_wqf, s_wo, s_mask = (sem(n) for n in
                                                    ("x_in", "small_in", "wkv_in", "wqf_in", "wo_in", "mask_in"))
        s_wqp, s_bias1, s_bias0 = sem("wqp_in"), sem("bias1_in"), sem("bias0_in")
        s_ident, s_pool0 = sem("ident_ready"), sem("pool_setup")
        s_dve0, s_act0, s_pe0 = sem("dve_setup"), sem("act_setup"), sem("pe_setup")
        s_q, s_qev = sem("q_product"), sem("q_copied")
        s_scored, s_added, s_max, s_exp = sem("scored"), sem("bias_added"), sem("max_taken"), sem("exp_done")
        s_rec, s_norm, s_turn = sem("sum_inverted"), sem("probs_normalised"), sem("probs_turned")
        s_pta, s_ptd, s_pv, s_oev = sem("turned_copied_act"), sem("turned_copied_dve"), sem("values_mixed"), sem("mix_copied")
        s_wod, s_ln2 = sem("wo_done"), sem("ln2_chain")
        s_out = sem("out_written")
        s_zero = sem("key_rows_zeroed")

        block = ctx.enter_context(nc.Block())

        def unit(u):
            i = 1 if u < 2 else 0
            return i, u % 2, (i + 1) * P

        def blk(i, hd, b2, jt):
            return (hd * 2 + b2) * (i + 1) + jt

        def pt_banks(u):
            return (4, 5) if u < 2 else ((4,) if u == 2 else (5,))

        def back(hp, u, lag):
            if u >= lag:
                return hp, u - lag
            if isinstance(hp, int) and hp == 0:
                return None
            return hp - 1, u - lag + 4

        def after(do, hp, u, lag):
            at = back(hp, u, lag)
            if at is not None:
                do(*at)

        def kv_psum(kv, half):
            b = 4 * kv + 2 * half
            return ps[:, b:b + 2, :].rearrange("p b (t g c) -> p (b t) g c", t=2, g=2)

        W_STEPS = 12
        KEY_BANKS = ((4, 5), (7, 7))

        def positive(n):
            return not isinstance(n, int) or n > 0

        w13_in = [sem(f"w13_in_{k}") for k in range(2)]

        def load13(eng, e, k, q):
            eng.dma_start(w13[k][:, 0:FC, :], w1[bass.ts(e, 1)].rearrange("e (c p) d -> p (e c) d", p=FP)).then_inc(w13_in[k], 16)
            eng.dma_start(w13[k][:, FC:2 * FC, :], w3[bass.ts(e, 1)].rearrange("e (c p) d -> p (e c) d", p=FP)).then_inc(w13_in[k], 16)

        def load2(eng, q):
            src = w2[bass.ts(q, 2)].rearrange("e (r a) f -> (e r) (a f)", a=2)
            eng.dma_start(w2r.rearrange("r g c -> r (g c)"), src).then_inc(ev("w2_in"), 16)

        @block.sync
        def _(sp):
            sp.dma_start(x_sb[:], x.rearrange("b (i p) d -> p (b i) d", p=P)).then_inc(s_x, 16)
            sp.dma_start(wkv_sb[:], Wkv).then_inc(s_wkv, 16)
            sp.dma_start(wq_full[:], Wq).then_inc(s_wqf, 16)
            small = [
                (gin_c[:], g_in.rearrange("(d o) -> d o", o=1)),
                (gout_b[:], g_out.partition_broadcast(P)),
                (nk_b[:], cond[0].partition_broadcast(P)),
                (vn_b[:], cond[1].partition_broadcast(P)),
                (vn_c[0:DH, :], cond[1].rearrange("(d o) -> d o", o=1)),
                (vn_c[DH:P, :], cond[1].rearrange("(d o) -> d o", o=1)),
                (nb_b[:], null_bias.partition_broadcast(P)),
            ]
            for dst, src in small:
                sp.dma_start(dst, src).then_inc(s_small, 16)
            sp.dma_start(mask_u[:], mask.partition_broadcast(P)).then_inc(s_mask, 16)

            def load_pair(hp, s_in=None):
                sp.dma_start(wq_p[:], Wq[:, bass.ts(hp, P)]).then_inc(s_wqp, 16)
                sp.dma_start(bias_sb[1][:], bias[bass.ts(hp, 2), P:N, :].rearrange("h q k -> q h k")).then_inc(s_bias1, 16)
                sp.dma_start(bias_sb[0][:], bias[bass.ts(hp, 2), 0:P, 0:P].rearrange("h q k -> q h k")).then_inc(s_bias0, 16)

            load_pair(0)
            sp.dma_start(wo_sb[:], Wo.rearrange("(c p) d -> p c d", p=P)).then_inc(s_wo, 16)
            for n, (dst, src) in enumerate([
                    (wraw[:, 0:HB, :], w_q.rearrange("(h p) d -> p h d", p=P)),
                    (wraw[:, HB:HB + KVH, :], w_k.rearrange("(h p) d -> p h d", p=P)),
                    (wraw[:, HB + KVH:HB + 2 * KVH, :], w_v.rearrange("(h p) d -> p h d", p=P)),
                    (wraw[:, HB + 2 * KVH:GB, :], w_o.rearrange("p (h d) -> p h d", d=D)),
                    (g1_c[:], g1.rearrange("(d o) -> d o", o=1)),
                    (g2_c[:], g2.rearrange("(d o) -> d o", o=1)),
                    (cs_tok[:], rope_tok.rearrange("(i p) a d -> p i a d", p=P)),
                    (cs_feat[:], rope_feat),
                    (wg[:], w_gate)]):
                sp.dma_start(dst, src).then_inc(ev("b_in"), 16)
            sp.wait_ge(ev("w_chain"), 5)
            half = P // 2
            sp.dma_start(sq_swap[0:half, :], q_stat[half:P, 2, 0:HB]).then_inc(ev("scales_swapped"), 16)
            sp.dma_start(sq_swap[half:P, :], q_stat[0:half, 2, 0:HB]).then_inc(ev("scales_swapped"), 16)
            sp.wait_ge(ev("wo_turned"), 1)
            load13(sp, 0, 0, 0)
            load13(sp, 1, 1, 0)
            sp.wait_ge(ev("k_turned"), KVH * 2)
            load2(sp, 0)
            sp.wait_ge(ev("result"), T)
            sp.dma_start(out.rearrange("b (i p) d -> p (b i) d", p=P), hx).then_inc(s_out, 16)
            sp.wait_ge(s_out, 16)

        @block.gpsimd
        def _(pool):
            pool.memset(identf[:], 0.0).then_inc(s_pool0, 1)
            pool.wait_ge(s_pool0, 1)
            pool.affine_select(out=identf[:], in_=identf[:], compare_op=ALU.not_equal, fill=1.0, base=0,
                               pattern=[[-1, P]], channel_multiplier=1).then_inc(s_ident, 1)
            pool.wait_ge(s_ident, 1)
            pool.tensor_copy(identb[:], identf[:]).then_inc(s_ident, 1)
            pool.memset(below[:], 1.0).then_inc(s_pool0, 1)
            pool.memset(causal[:], 0.0).then_inc(s_pool0, 1)
            pool.wait_ge(s_pool0, 3)
            pool.affine_select(out=below[:], in_=below[:], compare_op=ALU.is_ge, fill=0.0, base=-1,
                               pattern=[[1, E], [-1, E]], channel_multiplier=0).then_inc(ev("b_const"), 1)
            pool.affine_select(out=causal[:], in_=causal[:], compare_op=ALU.is_ge, fill=MASKED, base=0,
                               pattern=[[-1, P]], channel_multiplier=1).then_inc(ev("b_const"), 1)
            pool.memset(pick[:], 1.0).then_inc(s_pool0, 1)
            pool.wait_ge(s_pool0, 4)
            pool.affine_select(out=pick[:], in_=pick[:], compare_op=ALU.is_ge, fill=0.0, base=0,
                               pattern=[[-3, 2], [0, FP]], channel_multiplier=1).then_inc(s_pool0, 1)
            pool.wait_ge(s_pool0, 5)
            pool.affine_select(out=pick[:], in_=pick[:], compare_op=ALU.is_ge, fill=0.0, base=2,
                               pattern=[[3, 2], [0, FP]], channel_multiplier=-1).then_inc(ev("pick_ready"), 1)
            pool.wait_ge(s_dve0, 22)
            pool.affine_select(out=mask_i0[:], in_=mask_i0[:], compare_op=ALU.is_ge, fill=MASKED, base=0,
                               pattern=[[0, B], [-1, P]], channel_multiplier=1).then_inc(s_pool0, 1)
            pool.affine_select(out=mask_i1[:, :, P:N], in_=mask_i1[:, :, P:N], compare_op=ALU.is_ge, fill=MASKED,
                               base=0, pattern=[[0, B], [-1, P]], channel_multiplier=1).then_inc(s_pool0, 1)

            def normalise(U, u):
                i, bh, W = unit(u)
                pool.wait_ge(s_rec, U + 1)
                pool.tensor_tensor(px[u][:, :, 0:W], px[u][:, :, 0:W], rec[u][:].unsqueeze(2).to_broadcast([P, 4, W]),
                                   ALU.mult).then_inc(s_norm, 1)

            def pair(hp):
                for u in range(4):
                    after(lambda h, v: normalise(h * 4 + v, v), hp, u, 1)

            pair(0)
            with pool.Fori(1, PAIRS_A) as hp:
                pair(hp)
            normalise(PAIRS_A * 4 - 1, 3)

            def rope_sum(hp, hd, half):
                f = hp * 4 + half * 2 + hd
                pool.wait_ge(ev("q_rotated"), 2 * f + 2)
                if hp >= 2:
                    pool.wait_ge(ev("scored_b"), (hp - 1) * 4)
                pool.tensor_tensor(qrT[hp % 2][:, hd, half * HALF:(half + 1) * HALF], qa[f % 2][:], qb[f % 2][:],
                                   ALU.add).then_inc(ev("q_summed"), 1)

            def normalise_b(hp, u):
                i, bh, W = unit(u)
                pool.wait_ge(ev("inverted_b"), hp * 4 + u + 1)
                pool.tensor_tensor(px[u][:, :, 0:W], px[u][:, :, 0:W], rec[u][:].unsqueeze(2).to_broadcast([P, 4, W]),
                                   ALU.mult).then_inc(ev("normalised_b"), 1)

            def scale13(e, k):
                pool.wait_ge(ev("inverse13"), e + 1)
                pool.tensor_tensor(w13[k], w13[k], st13[k][:, 3, :].unsqueeze(2).to_broadcast([FP, 2 * FC, D]),
                                   ALU.mult).then_inc(ev("scaled13"), 1)

            def scale2(q):
                pool.wait_ge(ev("inverse2"), q + 1)
                pool.tensor_tensor(w2r, w2r, st2[:, 3, :].unsqueeze(2).to_broadcast([P, G2, D]),
                                   ALU.mult).then_inc(ev("scaled2"), 1)

            def rope_keys(kv, half):
                pool.wait_ge(ev("kv_dequantised"), kv * 2 + half + 1)
                h = D // 2
                ts = slice(half * 4, half * 4 + 4)
                kq = kv_sb[:, ts, kv, :].rearrange("p (b i) c -> p b i c", i=2)
                kr = k_rot[:, ts, kv, :].rearrange("p (b i) c -> p b i c", i=2)
                r = rot_k.rearrange("p (b i) c -> p b i c", i=2)
                if kv or half:
                    pool.wait_ge(ev("k_ready"), kv * 2 + half)
                cos = cs_tok[:, :, 0, :].unsqueeze(1).to_broadcast([P, 2, 2, D])
                pool.tensor_tensor(kr, kq, cos, ALU.mult)
                for a, b in ((0, h), (h, 0)):
                    sin = cs_tok[:, :, 1, a:a + h].unsqueeze(1).to_broadcast([P, 2, 2, h])
                    ins = pool.tensor_tensor(r[:, :, :, a:a + h], kq[:, :, :, b:b + h], sin, ALU.mult)
                ins.then_inc(ev("keys_rotated"), 1)
                pool.wait_ge(ev("keys_rotated"), kv * 2 + half + 1)
                pool.tensor_tensor(kr, kr, r, ALU.add).then_inc(ev("k_ready"), 1)

            def split(name, half, done):
                pool.wait_ge(ev(name), half * 2 + 2)
                cols = slice(half * HALF, (half + 1) * HALF)
                pool.tensor_tensor(x_lo[:, cols], xnT[:, cols], x_hi[:, cols].bitcast(F32), ALU.subtract).then_inc(ev(done), 1)

            split("xn1_ready", 0, "x_split")
            split("xn1_ready", 1, "x_split")
            rope_keys(0, 0)
            rope_sum(0, 0, 0)
            rope_sum(0, 1, 0)
            rope_keys(0, 1)
            rope_sum(0, 0, 1)
            rope_sum(0, 1, 1)
            for hp in range(PAIRS_B):
                for u in range(4):
                    after(normalise_b, hp, u, 1)
                    if hp + 1 < PAIRS_B:
                        rope_sum(hp + 1, u % 2, u // 2)
                    if hp == 1 and u in (0, 2):
                        rope_keys(1, u // 2)
                    if hp == PAIRS_B - 2 and u == 3:
                        scale13(0, 0)
                        scale2(0)
            normalise_b(PAIRS_B - 1, 3)

            pool.wait_ge(ev("rms2_y"), 2)
            pool.memset(rwT, 0.0).then_inc(ev("rwT_zeroed"), 1)
            split("hn_ready", 0, "hn_split")
            split("hn_ready", 1, "hn_split")
            pool.tensor_tensor(hx, y_sb[:], x_sb[:], ALU.add).then_inc(ev("hx_ready"), 1)

            def product(q, j, s):
                n = q * 16 + j * 8 + s
                k = s % NBUF
                pool.wait_ge(ev("up_scaled"), n + 1)
                pool.wait_ge(ev("gate_ready"), n + 1)
                if positive(n - NBUF + 1):
                    pool.wait_ge(ev("down"), n - NBUF + 1)
                pool.tensor_tensor(up[k], ups[k], gate[k], ALU.mult).then_inc(ev("up_ready"), 1)

            def pair_c(q, last=False):
                for j in range(2):
                    for s in range(8):
                        product(q, j, s)
                        if s == 0 and j == 1 and not last:
                            scale2(q + 1)
                        if s == 1 and not (last and j == 1):
                            scale13(q * 2 + j + 1, 1 - j)

            pair_c(0)
            with pool.Fori(1, E // 2 - 1) as q:
                pair_c(q)
            pair_c(E // 2 - 1, last=True)

        @block.scalar
        def _(act):
            act.wait_ge(s_dve0, 16)
            act.activation(std[:], mv[:, :, 1], ACT.Sqrt, bias=EPS).then_inc(s_act0, 1)
            act.wait_ge(s_pe0, 8)
            act.wait_ge(s_small, 16 * 7)
            act.activation(xnT[:], ps[:, 0:2, :].rearrange("p b c -> p (b c)"), ACT.Copy, scale=gin_c[:, 0:1]).then_inc(s_act0, 1)
            act.wait_ge(s_pe0, 10)
            act.wait_ge(s_zero, 2)
            for h in range(2):
                r = slice(DH * h, DH * h + DH)
                act.activation(kz[h][r, :], ps[r, 2:4, :].rearrange("p b c -> p (b c)"), ACT.Copy,
                               scale=float(DH) ** -0.5).then_inc(s_act0, 1)

            def exps(hp, u):
                i, bh, W = unit(u)
                act.wait_ge(s_max, hp * 4 + u + 1)
                for k in range(4):
                    ins = act.activation(px[u][:, k, 0:W + 1], px[u][:, k, 0:W + 1], ACT.Exp, bias=negm[u][:, k:k + 1], scale=-1.0,
                                         accum_out=sums[u][:, k:k + 1])
                ins.then_inc(s_exp, 1)

            def turned_copy(hp, u):
                act.wait_ge(s_turn, hp * 4 + u + 1)
                if not (isinstance(hp, int) and hp * 4 + u < 2):
                    act.wait_ge(s_pv, hp * 4 + u - 1)
                act.activation(pt[u % 2][:, 0:4, :], ps[:, 4, :].rearrange("p (k c) -> p k c", k=4), ACT.Copy).then_inc(s_pta, 1)

            def mix_copy(hp, u):
                i, bh, W = unit(u)
                act.wait_ge(s_pv, hp * 4 + u + 1)
                dst = oT[:, hp, :].rearrange("p (b i c) -> p b i c", b=B, i=2)[:, 2 * bh:2 * bh + 2, i, :]
                act.activation(dst, ps[:, 6, 0:2 * P].rearrange("p (b c) -> p b c", b=2), ACT.Identity,
                               bias=vn_c[:, 0:1]).then_inc(s_oev, 1)

            def q_copy(hp, half):
                act.wait_ge(s_q, hp * 2 + half + 1)
                if not isinstance(hp, int) or hp:
                    act.wait_ge(s_scored, hp * 4)
                act.activation(qT[:, half * HALF:(half + 1) * HALF], ps[:, 7, :], ACT.Copy).then_inc(s_qev, 1)

            def load_queries(hp):
                act.dma_start(wq_p[:], Wq[:, bass.ts(hp, P)]).then_inc(s_wqp, 16)

            def load_bias(hp, i):
                src = bias[bass.ts(hp, 2), i * P:(i + 1) * P, 0:(i + 1) * P].rearrange("h q k -> q h k")
                act.dma_start(bias_sb[i][:], src).then_inc(s_bias1 if i else s_bias0, 16)

            def dequantise_b(u):
                act.wait_ge(ev("w_chain"), (PAIRS_A - 1) * W_STEPS)
                n = (GB - HB) // 4
                for g in range(HB + n * u, HB + n * u + n):
                    act.activation(wraw[:, g, :], wraw[:, g, :], ACT.Copy, scale=q_stat[:, 2, g:g + 1]).then_inc(ev("w_dequantised"), 1)

            def pair(hp, last=False):
                for u in range(4):
                    after(turned_copy_a, hp, u, 3)
                    after(mix_copy, hp, u, 4)
                    after(exps, hp, u, 1)
                    if last:
                        dequantise_b(u)
                    if u == 0 and not (isinstance(hp, int) and hp == 0):
                        load_bias(hp, 0)
                    if last:
                        continue
                    if u == 1:
                        load_queries(hp + 1)
                    if u == 2:
                        load_bias(hp + 1, 1)
                    if u == 3:
                        q_copy(hp + 1, 0)
                        q_copy(hp + 1, 1)

            def turned_copy_a(hp, u):
                if u != 3:
                    turned_copy(hp, u)

            q_copy(0, 0)
            q_copy(0, 1)
            pair(0)
            with act.Fori(1, PAIRS_A - 1) as hp:
                pair(hp)
            pair(PAIRS_A - 1, last=True)
            exps(PAIRS_A - 1, 3)
            mix_copy(PAIRS_A - 1, 0)
            for u in range(1, 4):
                turned_copy_a(PAIRS_A - 1, u)
                mix_copy(PAIRS_A - 1, u)

            def root(src, dst, scale, before, after, n=1):
                act.wait_ge(before, n)
                act.activation(dst, src, ACT.Sqrt, bias=EPS, scale=scale).then_inc(after, 1)

            halves = [slice(4 * h, 4 * h + 4) for h in range(2)]

            def square_sums(name, half):
                act.wait_ge(ev(name + "_y"), half + 1)
                for t in range(4 * half, 4 * half + 4):
                    ins = act.activation(squares[:, t * D:(t + 1) * D], y_sb[:, t, :], ACT.Square, accum_out=ssq[:, t:t + 1])
                ins.then_inc(ev(name + "_sum"), 1)
                root(ssq[:, halves[half]], std[:, halves[half]], 1.0 / D, ev(name + "_sum"), ev(name + "_root"), half + 1)

            def transposed_copy(half, bank, gain, done):
                cols = slice(half * HALF, (half + 1) * HALF)
                for dst in (xnT, x_hi):
                    act.activation(dst[:, cols], ps[:, bank + half, :], ACT.Copy, scale=gain[:, 0:1]).then_inc(ev(done), 1)

            act.wait_ge(ev("wq_turned"), 1)
            turned = ps[:, 4, :].bitcast(BF16).rearrange("p (h c) -> p h c", h=HB)
            act.activation(wqT[:], turned, ACT.Copy).then_inc(ev("wqT_ready"), 1)
            half = P // 2
            act.activation(wqrT[:, :, 0:half], turned[:, :, half:P], ACT.Copy).then_inc(ev("wqT_ready"), 1)
            act.activation(wqrT[:, :, half:P], turned[:, :, 0:half], ACT.Copy).then_inc(ev("wqT_ready"), 1)
            act.wait_ge(ev("wkv_turned"), 1)
            act.activation(wkvT[:], ps[:, 5, :], ACT.Copy).then_inc(ev("wkvT_ready"), 1)
            act.wait_ge(ev("wo_turned"), 1)
            act.activation(woT[:], ps[:, 6:8, :].rearrange("p b (h c) -> p (b h) c", c=D), ACT.Copy).then_inc(ev("woT_ready"), 1)
            for half in range(2):
                root(mv[:, halves[half], 1], std[:, halves[half]], 1.0, ev("ln2_stats"), ev("ln2_root"), half + 1)
                square_sums("rms1", half)
                act.wait_ge(ev("rms1_turned"), half + 1)
                transposed_copy(half, 4, g1_c, "xn1_ready")

            def scale_kv(kv, half):
                act.wait_ge(ev("kv_inverse"), kv * 2 + half + 1)
                for t in range(4):
                    for g in range(2):
                        dst = kv_sb[:, half * 4 + t, g * KVH + kv, :]
                        src = kv_psum(kv, half)[:, t, g, :] if kv == 0 else dst
                        ins = act.activation(dst, src, ACT.Copy, scale=kv_stat[:, 3, kv, half, t * 2 + g:t * 2 + g + 1])
                ins.then_inc(ev("kv_scaled"), 1)

            def dequantise_kv(kv, half):
                act.wait_ge(ev("kv_ints"), kv * 2 + half + 1)
                for t in range(4):
                    for g in range(2):
                        dst = kv_sb[:, half * 4 + t, g * KVH + kv, :]
                        ins = act.activation(dst, dst, ACT.Copy, scale=kv_stat[:, 2, kv, half, t * 2 + g:t * 2 + g + 1])
                ins.then_inc(ev("kv_dequantised"), 1)

            def copy_keys(kv, half):
                act.wait_ge(ev("k_turned"), kv * 2 + half + 1)
                act.activation(kT[:, kv, half * HALF:(half + 1) * HALF], ps[:, KEY_BANKS[kv][half], :], ACT.Copy,
                               scale=float(D) ** -0.5).then_inc(ev("kT_ready"), 1)

            scale_kv(0, 0)
            for half in range(2):
                act.wait_ge(ev("kv_product"), 3 + half)
                act.activation(kv_sb[:, halves[half], :, :].rearrange("p t (g k) c -> p t g k c", k=KVH)[:, :, :, 1, :],
                               kv_psum(1, half), ACT.Copy).then_inc(ev("kv_copied"), 1)
            scale_kv(0, 1)
            dequantise_kv(0, 0)
            dequantise_kv(0, 1)
            copy_keys(0, 0)
            copy_keys(0, 1)

            def exps_b(hp, u):
                i, bh, W = unit(u)
                act.wait_ge(ev("max_b"), hp * 4 + u + 1)
                if hp:
                    act.wait_ge(ev("turned_b"), hp * 4 + u - 3)
                for k in range(4):
                    src = ps[:, 2 * (u % 2) + k // 2, (k % 2) * W:(k % 2 + 1) * W]
                    ins = act.activation(px[u][:, k, 0:W], src, ACT.Exp, bias=negm[u][:, k:k + 1],
                                         accum_out=sums[u][:, k:k + 1])
                ins.then_inc(ev("exp_b"), 1)

            def turned_copy_b(hp, u):
                n = hp * 4 + u
                act.wait_ge(ev("turned_b"), n + 1)
                if n >= 2:
                    act.wait_ge(ev("mixed_b"), n - 1)
                act.activation(pt[u % 2][:, 0:4, :], ps[:, 4, :].rearrange("p (k c) -> p k c", k=4), ACT.Copy).then_inc(ev("copied_act_b"), 1)

            def mix_copy_b(hp, u):
                i, bh, W = unit(u)
                act.wait_ge(ev("mixed_b"), hp * 4 + u + 1)
                for hd in range(2):
                    dst = oT[:, 2 * hp + hd, :].rearrange("p (b i c) -> p b i c", b=B, i=2)[:, 2 * bh:2 * bh + 2, i, :]
                    ins = act.activation(dst, ps[:, 6, hd * 2 * P:(hd + 1) * 2 * P].rearrange("p (b c) -> p b c", b=2), ACT.Copy)
                ins.then_inc(ev("mix_copied_b"), 1)

            def turned_copy_ab(hp, u):
                if u != 3:
                    turned_copy_b(hp, u)

            for hp in range(PAIRS_B):
                for u in range(4):
                    after(turned_copy_ab, hp, u, 3)
                    after(mix_copy_b, hp, u, 4)
                    after(exps_b, hp, u, 1)
                    if hp == 0 and u in (1, 2):
                        scale_kv(1, u - 1)
                    if (hp, u) in ((1, 0), (1, 1)):
                        dequantise_kv(1, u)
                    if hp == 1 and u >= 2:
                        copy_keys(1, u - 2)
            exps_b(PAIRS_B - 1, 3)
            mix_copy_b(PAIRS_B - 1, 0)
            for u in range(1, 4):
                turned_copy_ab(PAIRS_B - 1, u)
                mix_copy_b(PAIRS_B - 1, u)

            def copy13(e, k):
                act.wait_ge(ev("w13_turned"), e + 1)
                act.activation(w13T[k], ps[:, 4, :].bitcast(BF16)[:, 0:8 * FP].rearrange("p (g c) -> p g c", c=FP),
                               ACT.Copy).then_inc(ev("w13T_ready"), 1)

            def dequantise2(q):
                act.wait_ge(ev("ints2"), q + 1)
                for g in range(G2):
                    ins = act.activation(w2r[:, g, :], w2r[:, g, :], ACT.Copy, scale=st2[:, 2, g:g + 1])
                ins.then_inc(ev("w2_dequantised"), 1)

            def copy2(q, part):
                act.wait_ge(ev("w2_turned"), q * 2 + part + 1)
                n = q * 16 - 2 + 2 * part
                if positive(q * 16):
                    act.wait_ge(ev("down"), n)
                src = ps[0:FP, 5, :].rearrange("p (c a e r) -> p e c a r", c=2, a=2, e=2)
                for e in range(2):
                    dst = w2T[:, 2 * part:2 * part + 2, e, :].rearrange("p c (a r) -> p c a r", a=2)
                    ins = act.activation(dst, src[:, e], ACT.Copy)
                ins.then_inc(ev("w2T_ready"), 1)

            dequantise2(0)
            copy13(0, 0)

            for half in range(2):
                square_sums("rms2", half)
                if half == 0:
                    copy2(0, 0)
                act.wait_ge(ev("rms2_turned"), half + 1)
                if half == 0:
                    act.activation(wgT[:], ps[:, 7, WG0:WG0 + E], ACT.Copy).then_inc(ev("wgT_ready"), 1)
                transposed_copy(half, 2, g2_c, "hn_ready")
            act.wait_ge(ev("logits_shifted"), 1)
            act.activation(lg[:], lg[:], ACT.Exp).then_inc(ev("gates_exp"), 1)

            def copy_gates(e, k, half):
                act.wait_ge(ev("rw_spread"), e * 2 + half + 1)
                if positive(e * 8 - 8):
                    act.wait_ge(ev("up_scaled"), e * 8 - 8)
                act.activation(rwb[k][:, half * HALF:(half + 1) * HALF], ps[0:FP, 5, :], ACT.Copy).then_inc(ev("rwb_ready"), 1)

            def turned_gates(k):
                act.wait_ge(ev("rwT_zeroed"), 1)
                act.wait_ge(ev("rw_turned"), k + 1)
                act.activation(rwT[0:6, k, :], ps[0:6, GATE_BANKS[k], :].bitcast(BF16), ACT.Copy).then_inc(ev("rwT_ready_act"), 1)

            def silu(q, j, s):
                n = q * 16 + j * 8 + s
                act.wait_ge(ev("gate_product"), n + 1)
                if positive(n - NBUF + 1):
                    act.wait_ge(ev("up_ready"), n - NBUF + 1)
                c = s % FC
                act.activation(gate[s % NBUF], ps[0:FP, 2 * (s % 2), :], ACT.Silu, scale=st13[j][:, 2, c:c + 1]).then_inc(ev("gate_ready"), 1)


            def pair_c(q, last=False):
                for j in range(2):
                    e = q * 2 + j
                    more = not (last and j == 1)
                    for s in range(8):
                        silu(q, j, s)
                        if s == 0 and not last:
                            act.wait_ge(ev("ints13"), e + 1)
                            load13(act, e + 2, j, q + 1)
                        if s == 1 and j == 0:
                            if isinstance(q, int) and q == 0:
                                turned_gates(0)
                                copy_gates(0, 0, 0)
                                copy_gates(0, 0, 1)
                                turned_gates(2)
                            copy2(q, 1)
                            if not last:
                                load2(act, q + 1)
                        if s in (4, 5) and more:
                            copy_gates(e + 1, 1 - j, s - 4)
                        if s == 5 and j == 1 and more:
                            dequantise2(q + 1)
                        if s == 6 and more:
                            copy13(e + 1, 1 - j)
                        if s == 7 and j == 1 and more:
                            copy2(q + 1, 0)

            pair_c(0)
            with act.Fori(1, E // 2 - 1) as q:
                pair_c(q)
            pair_c(E // 2 - 1, last=True)
            for half in range(2):
                act.wait_ge(ev("experts_summed"), half + 1)
                act.activation(moeT[:, half * HALF:(half + 1) * HALF], ps[:, 6 + half, :], ACT.Copy).then_inc(ev("moeT_ready"), 1)

        @block.vector
        def _(dve):
            n0 = [0]

            def m0(ins):
                n0[0] += 1
                ins.then_inc(s_dve0, 1)

            for h in range(2):
                dve.memset(kz[h], 0.0).then_inc(s_zero, 1)
            dve.wait_ge(s_x, 16)
            for t in range(T):
                m0(dve.bn_stats(stats[:, t, :], x_sb[:, t, :]))
            for t in range(T):
                dve.wait_ge(s_dve0, t + 1)
                m0(dve.bn_aggr(mv[:, t, :], stats[:, t, :]))
            dve.wait_ge(s_small, 16 * 7)
            dve.wait_ge(s_wqf, 16)
            dve.wait_ge(s_wkv, 16)
            m0(dve.tensor_copy(wkk[:, 0:DH], wkv_sb[:, 0:DH]))
            m0(dve.tensor_copy(wkk[:, DH:P], wkv_sb[:, 0:DH]))
            prod = oT[:, 0, :]
            m0(dve.tensor_tensor(prod.rearrange("p (h c) -> p h c", h=HA), wq_full[:].rearrange("p (h c) -> p h c", h=HA),
                                 nk_b[:].unsqueeze(1).to_broadcast([P, HA, DH]), ALU.mult))
            dve.wait_ge(s_dve0, 19)
            m0(dve.tensor_reduce(u_sb[:], prod.rearrange("p (h c) -> p h c", h=HA), AX.X, ALU.add))
            dve.wait_ge(s_mask, 16)
            m0(dve.tensor_scalar(mask_i1[:], mask_u[:], -1.0, -MASKED, ALU.add, ALU.mult))
            m0(dve.tensor_scalar(mask_i0[:], mask_u[:, :, 0:P], -1.0, -MASKED, ALU.add, ALU.mult))
            dve.wait_ge(s_act0, 1)
            m0(dve.reciprocal(rstd[:], std[:]))
            dve.wait_ge(s_dve0, 23)
            for t in range(T):
                m0(dve.tensor_scalar(xh[:, t, :], x_sb[:, t, :], mv[:, t, 0:1], rstd[:, t:t + 1], ALU.subtract, ALU.mult))
            dve.wait_ge(s_pe0, 12)
            m0(dve.tensor_tensor(v_sb[:], ps[:, 4:6, :].rearrange("p b (t c) -> p (b t) c", c=P)[:, :, DH:P],
                                 vn_b[:].unsqueeze(1).to_broadcast([P, T, DH]), ALU.subtract))
            dve.wait_ge(s_pe0, 13)
            dve.wait_ge(s_small, 16 * 7)
            m0(dve.scalar_tensor_tensor(out=snull[:], in0=ps[:, 6, 0:T * HA].rearrange("p (t h) -> p t h", h=HA),
                                        scalar=-float(DH) ** -0.5, in1=nb_b[:].unsqueeze(1).to_broadcast([P, T, HA]),
                                        op0=ALU.mult, op1=ALU.subtract))
            dve.wait_ge(s_dve0, 33)

            def null_scores(hp, i, bh):
                return snull[:].rearrange("p (b i) h -> p b i h", i=2)[:, 2 * bh:2 * bh + 2, i, bass.ts(hp, 2)]

            def add(hp, u):
                i, bh, W = unit(u)
                dve.wait_ge(s_scored, hp * 4 + u + 1)
                dve.wait_ge(s_bias1 if i else s_bias0, hp * 16 + 16)
                if not isinstance(hp, int) or hp:
                    dve.wait_ge(s_turn, hp * 4 + u - 3)
                dve.tensor_copy(px[u][:, :, W].rearrange("p (h b) -> p b h", b=2), null_scores(hp, i, bh))
                k = u % 2
                for hd in range(2):
                    for b2 in range(2):
                        n = 2 * hd + b2
                        ins = dve.tensor_tensor_reduce(px[u][:, n, 0:W], ps[:, 2 * k + hd, b2 * W:(b2 + 1) * W], bias_sb[i][:, hd, :],
                                                       -1.0, -MASKED, ALU.add, ALU.min, lowest[u][:, n:n + 1])
                ins.then_inc(s_added, 1)

            def rowmax(hp, u):
                i, bh, W = unit(u)
                dve.wait_ge(s_added, hp * 4 + u + 1)
                dve.tensor_tensor(negm[u][:].rearrange("p (h b) -> p b h", b=2), lowest[u][:].rearrange("p (h b) -> p b h", b=2),
                                  null_scores(hp, i, bh), ALU.min).then_inc(s_max, 1)

            def invert(hp, u):
                dve.wait_ge(s_exp, hp * 4 + u + 1)
                dve.reciprocal(rec[u][:], sums[u][:]).then_inc(s_rec, 1)

            def turned_copy(hp, u):
                dve.wait_ge(s_turn, hp * 4 + u + 1)
                if not (isinstance(hp, int) and hp * 4 + u < 2):
                    dve.wait_ge(s_pv, hp * 4 + u - 1)
                o = 4 if u < 2 else 0
                dve.tensor_copy(pt[u % 2][:, o:o + 4, :], ps[:, 5, :].rearrange("p (k c) -> p k c", k=4)).then_inc(s_ptd, 1)

            def turned_copy_d(hp, u):
                if u != 2:
                    turned_copy(hp, u)

            def pair(hp, last=False):
                for u in range(4):
                    after(turned_copy_d, hp, u, 3)
                    if not last:
                        weight_step(hp, 3 * u)
                    add(hp, u)
                    if not last:
                        weight_step(hp, 3 * u + 1)
                    after(invert, hp, u, 1)
                    rowmax(hp, u)
                    if not last:
                        weight_step(hp, 3 * u + 2)

            def levels(st, done, count, step):
                step(dve.tensor_tensor(st(2), st(0), st(1), ALU.subtract))
                step(dve.tensor_scalar(st(2), st(2), 1e-5, 1.0 / QMAX, ALU.max, ALU.mult))
                dve.reciprocal(st(3), st(2)).then_inc(done, 1)
                dve.wait_ge(done, count)
                step(dve.tensor_tensor(st(4), st(1), st(3), ALU.mult))
                step(dve.tensor_scalar(st(4), st(4), MAGIC, MAGIC, ALU.add, ALU.min))
                step(dve.tensor_scalar(st(4), st(4), MAGIC - QMAX, None, ALU.max))
                return dve.tensor_scalar(st(5), st(4), -MAGIC, QMAX, ALU.add, ALU.add)


            def weight_step(hp, i):
                if isinstance(hp, int):
                    at, n, dst = slice(0, HB), HB, wint[:]
                else:
                    at, n = bass.ts(hp + (HB // 2 - 1), 2), 2
                    dst = wraw[:, at, :]
                w = wraw[:, at, :]
                rows = [q_stat[:, r, at] for r in range(6)]
                top, low, scale, inverse, first, last = rows

                def wide(row):
                    return row.unsqueeze(2).to_broadcast([P, n, D])

                if i:
                    dve.wait_ge(ev("w_chain"), hp * W_STEPS + i)
                elif isinstance(hp, int):
                    dve.wait_ge(ev("b_in"), 16 * 9)
                if i == 0:
                    ins = dve.tensor_reduce(top, w, AX.X, ALU.max)
                elif i == 1:
                    ins = dve.tensor_reduce(low, w, AX.X, ALU.min)
                elif i == 2:
                    ins = dve.tensor_tensor(scale, top, low, ALU.subtract)
                elif i == 3:
                    ins = dve.tensor_scalar(scale, scale, 1e-5, 1.0 / QMAX, ALU.max, ALU.mult)
                elif i == 4:
                    ins = dve.reciprocal(inverse, scale)
                elif i == 5:
                    ins = dve.tensor_tensor(first, low, inverse, ALU.mult)
                elif i == 6:
                    ins = dve.tensor_scalar(first, first, MAGIC, MAGIC, ALU.add, ALU.min)
                elif i == 7:
                    ins = dve.tensor_scalar(first, first, MAGIC - QMAX, None, ALU.max)
                elif i == 8:
                    ins = dve.tensor_scalar(last, first, -MAGIC, QMAX, ALU.add, ALU.add)
                elif i == 9:
                    ins = dve.tensor_tensor(w, w, wide(inverse), ALU.mult)
                elif i == 10:
                    ins = dve.scalar_tensor_tensor(out=w, in0=w, scalar=MAGIC, in1=wide(first), op0=ALU.add, op1=ALU.max)
                elif i == 11:
                    ins = dve.scalar_tensor_tensor(out=dst, in0=w, scalar=-MAGIC, in1=wide(last), op0=ALU.add, op1=ALU.min)
                ins.then_inc(ev("w_chain"), 1)

            pair(0)
            with dve.Fori(1, PAIRS_A - 1) as hp:
                pair(hp)
            pair(PAIRS_A - 1, last=True)
            invert(PAIRS_A - 1, 3)
            for u in range(1, 4):
                turned_copy_d(PAIRS_A - 1, u)
            chain = [0]

            def link(ins):
                chain[0] += 1
                ins.then_inc(ev("dve_chain"), 1)
                dve.wait_ge(ev("dve_chain"), chain[0])

            def normalise_rms(name, half):
                dve.wait_ge(ev(name + "_root"), half + 1)
                hs = slice(half * 4, half * 4 + 4)
                link(dve.reciprocal(rstd[:, hs], std[:, hs]))
                for t in range(half * 4, half * 4 + 4):
                    dve.tensor_scalar(xh[:, t, :], y_sb[:, t, :], rstd[:, t:t + 1], None, ALU.mult).then_inc(ev(name + "_scaled"), 1)

            for half in range(2):
                hs = slice(half * 4, half * 4 + 4)
                for t in range(half * 4, half * 4 + 4):
                    dve.wait_ge(s_wod, t // 2 * 2 + 2)
                    src = ps[:, t // 2, (t % 2) * P:(t % 2 + 1) * P]
                    link(dve.bn_stats(stats[:, t, :], src))
                    ins = dve.bn_aggr(mv[:, t, :], stats[:, t, :])
                ins.then_inc(ev("ln2_stats"), 1)
                dve.wait_ge(ev("ln2_root"), half + 1)
                link(dve.reciprocal(rstd[:, hs], std[:, hs]))
                for t in range(half * 4, half * 4 + 4):
                    src = ps[:, t // 2, (t % 2) * P:(t % 2 + 1) * P]
                    ins = dve.tensor_scalar(xh[:, t, :], src, mv[:, t, 0:1], rstd[:, t:t + 1], ALU.subtract, ALU.mult)
                link(ins)
                dve.tensor_tensor(y_sb[:, hs, :], xh[:, hs, :], gout_b[:].unsqueeze(1).to_broadcast([P, 4, D]),
                                  ALU.mult).then_inc(ev("rms1_y"), 1)
                normalise_rms("rms1", half)

            def kvf(kv, half):
                return kv_sb[:, half * 4:half * 4 + 4, :, :].rearrange("p t (g k) c -> p t g k c", k=KVH)[:, :, :, kv, :]

            def kv_st(kv, half, wide=False):
                def st(row):
                    a = kv_stat[:, row, kv, half, :]
                    return a.rearrange("p (t g) -> p t g", g=2).unsqueeze(3).to_broadcast([P, 4, 2, D]) if wide else a
                return st

            def kv_max(kv, half, step):
                if kv:
                    dve.wait_ge(ev("kv_copied"), half + 1)
                else:
                    dve.wait_ge(ev("kv_product"), half + 1)
                src = kvf(kv, half) if kv else kv_psum(kv, half)
                dve.tensor_reduce(kv_st(kv, half)(0).rearrange("p (t g) -> p t g", g=2), src, AX.X, ALU.max)

            def kv_min(kv, half, step):
                src = kvf(kv, half) if kv else kv_psum(kv, half)
                step(dve.tensor_reduce(kv_st(kv, half)(1).rearrange("p (t g) -> p t g", g=2), src, AX.X, ALU.min))
                levels(kv_st(kv, half), ev("kv_inverse"), kv * 2 + half + 1, step)

            def kv_low(kv, half, step):
                dve.wait_ge(ev("kv_scaled"), kv * 2 + half + 1)
                w = kvf(kv, half)
                step(dve.scalar_tensor_tensor(out=w, in0=w, scalar=MAGIC, in1=kv_st(kv, half, True)(4), op0=ALU.add, op1=ALU.max))

            def kv_ints(kv, half, step):
                w = kvf(kv, half)
                dve.scalar_tensor_tensor(out=w, in0=w, scalar=-MAGIC, in1=kv_st(kv, half, True)(5),
                                         op0=ALU.add, op1=ALU.min).then_inc(ev("kv_ints"), 1)

            def rope_q(hp, hd, hf, k):
                f = hp * 4 + hf * 2 + hd
                h = 2 * hp + hd
                dst, scale = ((qa, q_stat[:, 2, h:h + 1]), (qb, sq_swap[:, h:h + 1]))[k]
                dve.wait_ge(ev("q_product_b"), 2 * f + k + 1)
                if f >= 2:
                    dve.wait_ge(ev("q_summed"), f - 1)
                if f == 0 and k:
                    dve.wait_ge(ev("scales_swapped"), 32)
                bank = 6 + k if hp == 0 else 7
                dve.scalar_tensor_tensor(out=dst[f % 2][:].rearrange("p (b c) -> p b c", b=2),
                                         in0=ps[:, bank, :].rearrange("p (b c) -> p b c", b=2), scalar=scale,
                                         in1=cs_feat[:, k, :].unsqueeze(1).to_broadcast([P, 2, N]),
                                         op0=ALU.mult, op1=ALU.mult).then_inc(ev("q_rotated"), 1)

            def rowmax_b(hp, u):
                i, bh, W = unit(u)
                dve.wait_ge(ev("scored_b"), hp * 4 + u + 1)
                k = u % 2
                dve.tensor_reduce(negm[u][:].rearrange("p (h b) -> p h b", h=2),
                                  ps[:, 2 * k:2 * k + 2, 0:2 * W].rearrange("p h (b c) -> p h b c", b=2),
                                  AX.X, ALU.max, negate=True).then_inc(ev("max_b"), 1)

            def invert_b(hp, u):
                dve.wait_ge(ev("exp_b"), hp * 4 + u + 1)
                dve.reciprocal(rec[u][:], sums[u][:]).then_inc(ev("inverted_b"), 1)

            def turned_copy_b(hp, u):
                n = hp * 4 + u
                dve.wait_ge(ev("turned_b"), n + 1)
                if n >= 2:
                    dve.wait_ge(ev("mixed_b"), n - 1)
                o = 4 if u < 2 else 0
                dve.tensor_copy(pt[u % 2][:, o:o + 4, :], ps[:, 5, :].rearrange("p (k c) -> p k c", k=4)).then_inc(ev("copied_dve_b"), 1)

            def max13(n, k, step):
                dve.wait_ge(w13_in[k], (n * 16 + (2 - k) * 16))
                if positive(n * 8 - 8):
                    dve.wait_ge(ev("gate_ready"), n * 8 - 8)
                dve.tensor_reduce(st13[k][:, 0, :], w13[k], AX.X, ALU.max)

            def min13(n, k, step):
                step(dve.tensor_reduce(st13[k][:, 1, :], w13[k], AX.X, ALU.min))
                levels(lambda row: st13[k][:, row, :], ev("inverse13"), n + 1, step)

            def max2(n, k, step):
                dve.wait_ge(ev("w2_in"), n * 16 + 16)
                if positive(n):
                    dve.wait_ge(ev("w2_dequantised"), n)
                dve.tensor_reduce(st2[:, 0, :], w2r, AX.X, ALU.max)

            def min2(n, k, step):
                step(dve.tensor_reduce(st2[:, 1, :], w2r, AX.X, ALU.min))
                levels(lambda row: st2[:, row, :], ev("inverse2"), n + 1, step)

            def low13(n, k, step):
                dve.wait_ge(ev("scaled13"), n + 1)
                step(dve.scalar_tensor_tensor(out=w13[k], in0=w13[k], scalar=MAGIC, in1=st13[k][:, 4, :].unsqueeze(2).to_broadcast([FP, 2 * FC, D]),
                                              op0=ALU.add, op1=ALU.max))

            def ints13(n, k, step):
                if positive(n):
                    dve.wait_ge(ev("w13_turned"), n)
                dve.scalar_tensor_tensor(out=i13[:], in0=w13[k], scalar=-MAGIC, in1=st13[k][:, 5, :].unsqueeze(2).to_broadcast([FP, 2 * FC, D]),
                                         op0=ALU.add, op1=ALU.min).then_inc(ev("ints13"), 1)

            def low2(n, k, step):
                dve.wait_ge(ev("scaled2"), n + 1)
                step(dve.scalar_tensor_tensor(out=w2r, in0=w2r, scalar=MAGIC, in1=st2[:, 4, :].unsqueeze(2).to_broadcast([P, G2, D]),
                                              op0=ALU.add, op1=ALU.max))

            def ints2(n, k, step):
                dve.scalar_tensor_tensor(out=w2r, in0=w2r, scalar=-MAGIC, in1=st2[:, 5, :].unsqueeze(2).to_broadcast([P, G2, D]),
                                         op0=ALU.add, op1=ALU.min).then_inc(ev("ints2"), 1)

            kv_max(0, 0, link)
            kv_min(0, 0, link)
            kv_max(0, 1, link)
            kv_min(0, 1, link)
            kv_low(0, 0, link)
            kv_ints(0, 0, link)
            rope_q(0, 0, 0, 0)
            rope_q(0, 0, 0, 1)
            rope_q(0, 1, 0, 0)
            rope_q(0, 1, 0, 1)
            kv_low(0, 1, link)
            kv_ints(0, 1, link)
            rope_q(0, 0, 1, 0)
            rope_q(0, 0, 1, 1)
            rope_q(0, 1, 1, 0)
            rope_q(0, 1, 1, 1)
            def turned_copy_db(hp, u):
                if u != 2:
                    turned_copy_b(hp, u)

            for hp in range(PAIRS_B):
                for u in range(4):
                    after(turned_copy_db, hp, u, 3)
                    if hp + 1 < PAIRS_B:
                        rope_q(hp + 1, u % 2, u // 2, 0)
                    rowmax_b(hp, u)
                    if hp + 1 < PAIRS_B:
                        rope_q(hp + 1, u % 2, u // 2, 1)
                    after(invert_b, hp, u, 1)
                    if hp == 0:
                        (kv_max, kv_min, kv_low, kv_ints)[u](1, 0, link)
                        if u < 2:
                            (kv_max, kv_min)[u](1, 1, link)
                    if hp == 1 and u < 2:
                        (kv_low, kv_ints)[u](1, 1, link)
                    if hp >= PAIRS_B - 2:
                        (max13, min13, max2, min2, low13, ints13, low2, ints2)[(hp - PAIRS_B + 2) * 4 + u](0, 0, link)
            invert_b(PAIRS_B - 1, 3)
            for u in range(1, 4):
                turned_copy_db(PAIRS_B - 1, u)
            for half in range(2):
                dve.wait_ge(ev("o_product"), half * 4 + 4)
                y = y_sb[:, half * 4:half * 4 + 4, :]
                dve.tensor_tensor(y, ps[:, half, :].rearrange("p (t d) -> p t d", d=D), y, ALU.add).then_inc(ev("rms2_y"), 1)
                normalise_rms("rms2", half)
            dve.memset(zrow[:], 0.0).then_inc(ev("zeros"), 1)
            dve.wait_ge(ev("logits"), 1)
            link(dve.tensor_copy(lg[:], ps[:, 7, 0:T * E].rearrange("p (t e) -> p t e", e=E)))
            link(dve.tensor_reduce(lgm[:], lg[:], AX.X, ALU.max, negate=True))
            dve.tensor_tensor(lg[:], lg[:], lgm[:].unsqueeze(2).to_broadcast([P, T, E]), ALU.add).then_inc(ev("logits_shifted"), 1)
            dve.wait_ge(ev("gates_exp"), 1)
            dve.wait_ge(ev("b_const"), 2)
            mine = lg[:].unsqueeze(3).to_broadcast([P, T, E, E])
            other = lg[:].unsqueeze(2).to_broadcast([P, T, E, E])
            dve.tensor_tensor(cmp, other, mine, ALU.is_gt)
            link(dve.tensor_tensor(cmq, other, mine, ALU.is_equal))
            link(dve.tensor_tensor(cmq, cmq, below[:].unsqueeze(1).to_broadcast([P, T, E, E]), ALU.mult))
            link(dve.tensor_tensor(cmp, cmp, cmq, ALU.add))
            link(dve.tensor_reduce(rank[:], cmp, AX.X, ALU.add))
            link(dve.scalar_tensor_tensor(out=rw[:], in0=rank[:], scalar=2.0, in1=lg[:], op0=ALU.is_lt, op1=ALU.mult))
            link(dve.tensor_reduce(rsm[:], rw[:], AX.X, ALU.add))
            link(dve.reciprocal(rsm[:], rsm[:]))
            link(dve.tensor_tensor(rw[:], rw[:], rsm[:].unsqueeze(2).to_broadcast([P, T, E]), ALU.mult))
            gates3 = rw3[:].rearrange("p t q j s -> p t (q j) s")
            link(dve.tensor_copy(gates3[:, :, :, 0], rw[:]))
            link(dve.tensor_tensor(rw_r[0][:], rw[:], gates3[:, :, :, 0], ALU.subtract))
            link(dve.tensor_copy(gates3[:, :, :, 1], rw_r[0][:]))
            link(dve.tensor_tensor(rw_r[1][:], rw_r[0][:], gates3[:, :, :, 1], ALU.subtract))
            dve.tensor_copy(gates3[:, :, :, 2], rw_r[1][:]).then_inc(ev("rw_split"), 1)

            dve.wait_ge(ev("rwT_zeroed"), 1)
            for k in (1, 3):
                dve.wait_ge(ev("rw_turned"), k + 1)
                dve.tensor_copy(rwT[0:6, k, :], ps[0:6, GATE_BANKS[k], :].bitcast(BF16)).then_inc(ev("rwT_ready_dve"), 1)

            def scale_up(q, j, s):
                n = q * 16 + j * 8 + s
                half, c = s // FC, s % FC
                dve.wait_ge(ev("up_product"), n + 1)
                if c == 0:
                    dve.wait_ge(ev("rwb_ready"), q * 4 + j * 2 + half + 1)
                if positive(n - NBUF + 1):
                    dve.wait_ge(ev("up_ready"), n - NBUF + 1)
                dve.scalar_tensor_tensor(out=ups[s % NBUF], in0=ps[0:FP, 2 * (s % 2) + 1, :],
                                         scalar=st13[j][:, 2, FC + c:FC + c + 1], in1=rwb[j][:, half * HALF:(half + 1) * HALF],
                                         op0=ALU.mult, op1=ALU.mult).then_inc(ev("up_scaled"), 1)

            LINKS_C = 21

            def pair_c(q, last=False):
                k = [0]

                def step(ins):
                    k[0] += 1
                    ins.then_inc(ev("c_chain"), 1)
                    dve.wait_ge(ev("c_chain"), q * LINKS_C + k[0])

                for j in range(2):
                    n = q * 2 + j + 1
                    for s in range(8):
                        scale_up(q, j, s)
                        if not (last and j == 1):
                            work = {0: max13, 1: min13, 4: low13, 5: ints13}.get(s)
                            if work:
                                work(n, 1 - j, step)
                        if not last:
                            work = {(0, 6): max2, (0, 7): min2, (1, 2): low2, (1, 3): ints2}.get((j, s))
                            if work:
                                work(q + 1, 0, step)
                assert last or k[0] == LINKS_C, k[0]

            pair_c(0)
            with dve.Fori(1, E // 2 - 1) as q:
                pair_c(q)
            pair_c(E // 2 - 1, last=True)
            dve.wait_ge(ev("hx_ready"), 1)
            for t in range(T):
                dve.wait_ge(ev("moe_turned"), t + 1)
                moe = ps[:, t % 4, 0:D].rearrange("p (a r) -> p r a", a=2)
                dve.tensor_tensor(hx[:, t, :].rearrange("p (r a) -> p r a", a=2), moe,
                                  hx[:, t, :].rearrange("p (r a) -> p r a", a=2), ALU.add).then_inc(ev("result"), 1)

        @block.tensor
        def _(pe):
            pe.wait_ge(s_ident, 2)
            for t in range(T):
                pe.wait_ge(s_dve0, 24 + t)
                pe.transpose(ps[:, t // 4, (t % 4) * P:(t % 4) * P + P], xh[:, t, :], identf[:]).then_inc(s_pe0, 1)
            pe.wait_ge(s_act0, 2)
            for half in range(2):
                pe.matmul(ps[:, 2 + half, :], wkk[:], xnT[:, half * HALF:(half + 1) * HALF], start=True, stop=True).then_inc(s_pe0, 1)
            pe.wait_ge(s_wkv, 16)
            for t in range(T):
                ins = pe.matmul(ps[:, 4 + t // 4, (t % 4) * P:(t % 4) * P + P], xnT[:, t * P:(t + 1) * P], wkv_sb[:],
                                start=True, stop=True)
                if t % 4 == 3:
                    ins.then_inc(s_pe0, 1)
            for t in range(T):
                ins = pe.matmul(ps[:, 6, t * HA:(t + 1) * HA], xnT[:, t * P:(t + 1) * P], u_sb[:], start=True, stop=True)
            ins.then_inc(s_pe0, 1)

            def queries(hp, half):
                pe.wait_ge(s_wqp, hp * 16 + 16)
                if not (isinstance(hp, int) and hp == 0 and half == 0):
                    pe.wait_ge(s_qev, hp * 2 + half)
                pe.matmul(ps[:, 7, :], wq_p[:], xnT[:, half * HALF:(half + 1) * HALF], start=True, stop=True).then_inc(s_q, 1)

            def scores(hp, u):
                i, bh, W = unit(u)
                k = u % 2
                pe.wait_ge(s_qev, hp * 2 + bh + 1)
                if not (isinstance(hp, int) and hp * 4 + u < 2):
                    pe.wait_ge(s_added, hp * 4 + u - 1)
                for hd in range(2):
                    for b2 in range(2):
                        b = 2 * bh + b2
                        t = 2 * b + i
                        dst = ps[:, 2 * k + hd, b2 * W:(b2 + 1) * W]
                        pe.matmul(dst, qT[:, t * P:(t + 1) * P], kz[hd][:, b * N:b * N + W], start=True, stop=False)
                        m = mask_i1[:, b, :] if i else mask_i0[:, b, :]
                        ins = pe.matmul(dst, identb[:], m, start=False, stop=True)
                ins.then_inc(s_scored, 1)

            def turn(hp, u):
                i, bh, W = unit(u)
                pe.wait_ge(s_norm, hp * 4 + u + 1)
                n = hp * 3 + min(u, 2)
                if not (isinstance(hp, int) and hp * 3 + min(u, 2) == 0):
                    if 4 in pt_banks(u):
                        pe.wait_ge(s_pta, n)
                    if 5 in pt_banks(u):
                        pe.wait_ge(s_ptd, n)
                for hd in range(2):
                    for b2 in range(2):
                        for jt in range(i + 1):
                            n = blk(i, hd, b2, jt)
                            bank = pt_banks(u)[n // 4]
                            ins = pe.transpose(ps[:, bank, (n % 4) * P:(n % 4 + 1) * P],
                                               px[u][:, hd * 2 + b2, jt * P:(jt + 1) * P], identf[:])
                ins.then_inc(s_turn, 1)

            def mix(hp, u):
                i, bh, W = unit(u)
                n = hp * 3 + min(u, 2) + 1
                if 4 in pt_banks(u):
                    pe.wait_ge(s_pta, n)
                if 5 in pt_banks(u):
                    pe.wait_ge(s_ptd, n)
                if not (isinstance(hp, int) and hp * 4 + u == 0):
                    pe.wait_ge(s_oev, hp * 4 + u)
                for b2 in range(2):
                    for jt in range(i + 1):
                        for hd in range(2):
                            t = 2 * (2 * bh + b2) + jt
                            ins = pe.matmul(ps[hd * DH:(hd + 1) * DH, 6, b2 * P:(b2 + 1) * P], v_sb[:, t, :],
                                            pt[u % 2][:, blk(i, hd, b2, jt), :], start=(jt == 0), stop=(jt == i))
                ins.then_inc(s_pv, 1)

            def pair(hp, last=False):
                for u in range(4):
                    after(turn, hp, u, 3)
                    scores(hp, u)
                    after(mix, hp, u, 3)
                    if not last and u >= 2:
                        queries(hp + 1, u - 2)

            queries(0, 0)
            queries(0, 1)
            pe.wait_ge(s_pool0, 7)
            pe.wait_ge(s_act0, 4)
            pe.wait_ge(s_dve0, 33)
            pair(0)
            with pe.Fori(1, PAIRS_A - 1) as hp:
                pair(hp)
            pair(PAIRS_A - 1, last=True)
            for u in range(1, 4):
                turn(PAIRS_A - 1, u)
                mix(PAIRS_A - 1, u)
            pe.wait_ge(ev("w_chain"), W_STEPS)
            for h in range(HB):
                ins = pe.transpose(ps[:, 4, :].bitcast(BF16)[:, h * P:(h + 1) * P], wint[:, h, :], identb[:])
            ins.then_inc(ev("wq_turned"), 1)
            pe.wait_ge(ev("w_dequantised"), GB - HB)
            for g in range(2 * KVH):
                ins = pe.transpose(ps[:, 5, g * P:(g + 1) * P], wraw[:, HB + g, :], identf[:])
            ins.then_inc(ev("wkv_turned"), 1)
            pe.wait_ge(s_oev, PAIRS_A * 4)
            for h in range(HB):
                ins = pe.transpose(ps[:, 6 + h // 4, (h % 4) * P:(h % 4 + 1) * P], wraw[:, HB + 2 * KVH + h, :], identf[:])
            ins.then_inc(ev("wo_turned"), 1)
            pe.wait_ge(s_wo, 16)
            for t in range(T):
                for hp in range(PAIRS_A):
                    ins = pe.matmul(ps[:, t // 2, (t % 2) * P:(t % 2 + 1) * P], oT[:, hp, t * P:(t + 1) * P], wo_sb[:, hp, :],
                                    start=(hp == 0), stop=(hp == PAIRS_A - 1))
                ins.then_inc(s_wod, 1)


            def turn_x(name, bank, half):
                for t in range(4):
                    pe.wait_ge(ev(name + "_scaled"), half * 4 + t + 1)
                    ins = pe.transpose(ps[:, bank + half, t * P:(t + 1) * P], xh[:, half * 4 + t, :], identf[:])
                ins.then_inc(ev(name + "_turned"), 1)

            wkv_heads = wkvT[:].rearrange("p (g k c) -> p k g c", g=2, k=KVH)
            for kv in range(KVH):
                for half in range(2):
                    if kv == 0:
                        pe.wait_ge(ev("woT_ready"), 1)
                        turn_x("rms1", 4, half)
                    pe.wait_ge(ev("xn1_ready"), 4 if kv else 2 * half + 1)
                    for t in range(4):
                        ins = pe.matmul(kv_psum(kv, half)[:, t], xnT[:, (half * 4 + t) * P:(half * 4 + t + 1) * P],
                                        wkv_heads[:, kv], start=True, stop=True)
                    ins.then_inc(ev("kv_product"), 1)

            def turn_keys(kv, half):
                pe.wait_ge(ev("k_ready"), kv * 2 + half + 1)
                for t in range(4):
                    ins = pe.transpose(ps[:, KEY_BANKS[kv][half], t * P:(t + 1) * P], k_rot[:, half * 4 + t, kv, :], identf[:])
                ins.then_inc(ev("k_turned"), 1)

            def query_bank(hp, k):
                return 6 + k if hp == 0 else 7

            def queries_b(hp, hd, hf, k):
                f, h, bank = hp * 4 + hf * 2 + hd, 2 * hp + hd, query_bank(hp, k)
                n = 2 * f + k
                if hp == 0:
                    n = n - 1
                if n > 0:
                    pe.wait_ge(ev("q_rotated"), n)
                cols, w = slice(hf * HALF, (hf + 1) * HALF), (wqT, wqrT)[k]
                pe.matmul(ps[:, bank, :], w[:, h, :], x_hi[:, cols], start=True, stop=False)
                pe.matmul(ps[:, bank, :], w[:, h, :], x_lo[:, cols], start=False, stop=True).then_inc(ev("q_product_b"), 1)

            def scores_b(hp, u):
                i, bh, W = unit(u)
                n, k, kv = hp * 4 + u, u % 2, hp * KVH // PAIRS_B
                pe.wait_ge(ev("q_summed"), 4 * hp + 4)
                if n >= 2:
                    pe.wait_ge(ev("exp_b"), n - 1)
                if hp * KVH == PAIRS_B * kv and u < 2:
                    pe.wait_ge(ev("kT_ready"), kv * 2 + u + 1)
                for hd in range(2):
                    for b2 in range(2):
                        b = 2 * bh + b2
                        t = 2 * b + i
                        pe.matmul(ps[:, 2 * k + hd, b2 * W:(b2 + 1) * W], qrT[hp % 2][:, hd, t * P:(t + 1) * P],
                                  kT[:, kv, b * N:b * N + W], start=True, stop=False)
                        ins = pe.matmul(ps[:, 2 * k + hd, (b2 + 1) * W - P:(b2 + 1) * W], identb[:], causal[:],
                                        start=False, stop=True)
                ins.then_inc(ev("scored_b"), 1)

            def turn_b(hp, u):
                i, bh, W = unit(u)
                pe.wait_ge(ev("normalised_b"), hp * 4 + u + 1)
                n = hp * 3 + min(u, 2)
                if n:
                    if 4 in pt_banks(u):
                        pe.wait_ge(ev("copied_act_b"), n)
                    if 5 in pt_banks(u):
                        pe.wait_ge(ev("copied_dve_b"), n)
                for hd in range(2):
                    for b2 in range(2):
                        for jt in range(i + 1):
                            n = blk(i, hd, b2, jt)
                            ins = pe.transpose(ps[:, pt_banks(u)[n // 4], (n % 4) * P:(n % 4 + 1) * P],
                                               px[u][:, hd * 2 + b2, jt * P:(jt + 1) * P], identf[:])
                ins.then_inc(ev("turned_b"), 1)

            def mix_b(hp, u):
                i, bh, W = unit(u)
                kv = hp * KVH // PAIRS_B
                n = hp * 3 + min(u, 2) + 1
                if 4 in pt_banks(u):
                    pe.wait_ge(ev("copied_act_b"), n)
                if 5 in pt_banks(u):
                    pe.wait_ge(ev("copied_dve_b"), n)
                if hp * 4 + u:
                    pe.wait_ge(ev("mix_copied_b"), hp * 4 + u)
                probs = pt[u % 2][:, 0:4 * (i + 1), :].rearrange("p (h b j) c -> p h b j c", h=2, b=2)
                mixed = ps[:, 6, :].rearrange("p (h b c) -> p h b c", h=2, b=2)
                for b2 in range(2):
                    for jt in range(i + 1):
                        t = 2 * (2 * bh + b2) + jt
                        ins = pe.matmul(mixed[:, :, b2, :], kv_sb[:, t, KVH + kv, :], probs[:, :, b2, jt, :],
                                        start=(jt == 0), stop=(jt == i))
                ins.then_inc(ev("mixed_b"), 1)

            pe.wait_ge(ev("x_split"), 2)
            pe.wait_ge(ev("wqT_ready"), 3)
            pe.wait_ge(ev("kv_copied"), 2)
            for f in range(4):
                for k in range(2):
                    queries_b(0, f % 2, f // 2, k)
            turn_keys(0, 0)
            turn_keys(0, 1)
            pe.wait_ge(ev("kT_ready"), 2)
            pe.wait_ge(ev("b_const"), 2)
            for hp in range(PAIRS_B):
                for u in range(4):
                    after(turn_b, hp, u, 3)
                    if hp + 1 < PAIRS_B:
                        if (hp, u) in ((1, 3), (2, 0)):
                            pe.wait_ge(ev("kT_ready"), 3 + (hp == 2))
                        queries_b(hp + 1, u % 2, u // 2, 0)
                    scores_b(hp, u)
                    if hp + 1 < PAIRS_B:
                        queries_b(hp + 1, u % 2, u // 2, 1)
                    if hp == 1 and u >= 2:
                        pe.wait_ge(ev("q_rotated"), 8 * 2 + 2 * (u + 1))
                        turn_keys(1, u - 2)
                    after(mix_b, hp, u, 3)
            for u in range(1, 4):
                turn_b(PAIRS_B - 1, u)
                mix_b(PAIRS_B - 1, u)
            pe.wait_ge(ev("mix_copied_b"), 4 * PAIRS_B)

            def turn13(e):
                pe.wait_ge(ev("ints13"), e + 1)
                if positive(e):
                    pe.wait_ge(ev("w13T_ready"), e)
                for g in range(2 * FC):
                    ins = pe.transpose(ps[:, 4, :].bitcast(BF16)[:, g * FP:(g + 1) * FP], i13[:, g, :], identb[0:FP, 0:FP])
                ins.then_inc(ev("w13_turned"), 1)

            def turn2(q, part):
                pe.wait_ge(ev("w2_dequantised"), q + 1)
                if part:
                    pe.wait_ge(ev("w2T_ready"), q * 2 + 1)
                if part or positive(q):
                    pe.wait_ge(ev("rwb_ready"), q * 4 + 2)
                w = w2r.rearrange("r g c -> r (g c)").rearrange("r (a c f) -> r a c f", a=2, c=FC)
                for c in range(2):
                    for a in range(2):
                        n = c * 2 + a
                        ins = pe.transpose(ps[0:FP, 5, n * P:(n + 1) * P], w[:, a, 2 * part + c, :], identf[:])
                ins.then_inc(ev("w2_turned"), 1)

            def spread(q, j, half):
                if positive(q * 4 + j * 2 + half):
                    pe.wait_ge(ev("rwb_ready"), q * 4 + j * 2 + half)
                if j == 1:
                    pe.wait_ge(ev("w2T_ready"), q * 2 + 2)
                pe.matmul(ps[0:FP, 5, :], pick[:, j, :], rwT[:, bass.ts(q, 1), half * HALF:(half + 1) * HALF].rearrange("p q t -> p (q t)"),
                          start=True, stop=True).then_inc(ev("rw_spread"), 1)

            turn13(0)
            for t in range(T):
                if t == T // 2:
                    turn2(0, 0)
                for h in range(HB):
                    ins = pe.matmul(ps[:, t // 4, (t % 4) * P:(t % 4 + 1) * P], oT[:, h, t * P:(t + 1) * P], woT[:, h, :],
                                    start=(h == 0), stop=(h == HB - 1))
                ins.then_inc(ev("o_product"), 1)

            pe.transpose(ps[:, 7, WG0:WG0 + E], wg[:], identf[0:E, 0:E])
            for half in range(2):
                turn_x("rms2", 2, half)
                pe.wait_ge(ev("hn_ready"), 2 * half + 1)
                pe.wait_ge(ev("wgT_ready"), 1)
                for t in range(4 * half, 4 * half + 4):
                    ins = pe.matmul(ps[:, 7, t * E:(t + 1) * E], xnT[:, t * P:(t + 1) * P], wgT[:], start=True, stop=True)
            ins.then_inc(ev("logits"), 1)
            pe.wait_ge(ev("hn_split"), 2)
            pe.wait_ge(ev("zeros"), 1)

            def turn_gates():
                pe.wait_ge(ev("rw_split"), 1)
                pe.wait_ge(ev("w2T_ready"), 1)
                for q in range(E // 2):
                    for t in range(T):
                        ins = pe.transpose(ps[0:6, GATE_BANKS[q], :].bitcast(BF16)[:, t * P:(t + 1) * P],
                                           rw3[:, t, q, :, :].rearrange("p j s -> p (j s)"), identb[:])
                    ins.then_inc(ev("rw_turned"), 1)
                pe.wait_ge(ev("pick_ready"), 1)
                pe.wait_ge(ev("rwT_ready_act"), 1)
                spread(0, 0, 0)
                spread(0, 0, 1)
                pe.wait_ge(ev("rwT_ready_act"), 2)
                pe.wait_ge(ev("rwT_ready_dve"), 2)
                for half in range(2):
                    pe.matmul(ps[:, 6 + half, :], zrow[:], finite, start=True, stop=False, skip_group_check=True)

            def hidden(q, j, s):
                n = q * 16 + j * 8 + s
                half, c = s // FC, s % FC
                cols = slice(half * HALF, (half + 1) * HALF)
                k = s % 2
                if s == 0:
                    pe.wait_ge(ev("w13T_ready"), q * 2 + j + 1)
                if positive(n - 1):
                    pe.wait_ge(ev("gate_ready"), n - 1)
                pe.matmul(ps[0:FP, 2 * k, :], w13T[j][:, c, :], x_hi[:, cols], start=True, stop=False)
                pe.matmul(ps[0:FP, 2 * k, :], w13T[j][:, c, :], x_lo[:, cols], start=False, stop=True).then_inc(ev("gate_product"), 1)
                if positive(n - 1):
                    pe.wait_ge(ev("up_scaled"), n - 1)
                pe.matmul(ps[0:FP, 2 * k + 1, :], w13T[j][:, FC + c, :], x_hi[:, cols], start=True, stop=False)
                pe.matmul(ps[0:FP, 2 * k + 1, :], w13T[j][:, FC + c, :], x_lo[:, cols], start=False, stop=True).then_inc(ev("up_product"), 1)

            def down(q, j, s):
                half, c = s // FC, s % FC
                if j == 0 and s in (0, 2):
                    pe.wait_ge(ev("w2T_ready"), q * 2 + 1 + s // 2)
                pe.wait_ge(ev("up_ready"), q * 16 + j * 8 + s + 1)
                pe.matmul(ps[:, 6 + half, :], w2T[:, c, j, :], up[s % NBUF], start=False, stop=False,
                          skip_group_check=True).then_inc(ev("down"), 1)

            def pair_c(q, last=False):
                for j in range(2):
                    more = not (last and j == 1)
                    for s in range(8):
                        hidden(q, j, s)
                        if s >= 2:
                            down(q, j, s - 2)
                        elif j:
                            down(q, 0, s + 6)
                        elif not isinstance(q, int) or q:
                            down(q - 1, 1, s + 6)
                        if s == 1 and j == 0:
                            if isinstance(q, int) and q == 0:
                                turn_gates()
                            turn2(q, 1)
                        if s in (4, 5) and more:
                            spread(*((q, 1) if j == 0 else (q + 1, 0)), s - 4)
                        if s == 6 and more:
                            turn13(q * 2 + j + 1)
                        if s == 7 and j == 1 and more:
                            turn2(q + 1, 0)

            pair_c(0)
            with pe.Fori(1, E // 2 - 1) as q:
                pair_c(q)
            pair_c(E // 2 - 1, last=True)
            down(E // 2 - 1, 1, 6)
            down(E // 2 - 1, 1, 7)
            for half in range(2):
                pe.matmul(ps[:, 6 + half, :], zrow[:], finite, start=False, stop=True,
                          skip_group_check=True).then_inc(ev("experts_summed"), 1)
            for t in range(T):
                pe.wait_ge(ev("moeT_ready"), t // 4 + 1)
                if t >= 4:
                    pe.wait_ge(ev("result"), t - 3)
                pe.transpose(ps[:, t % 4, 0:D], moeT[:, t * P:(t + 1) * P], identf[:]).then_inc(ev("moe_turned"), 1)


_NAMES = ["x", "fside_16xSxS_0", "cond_64", "mask_BxS_bk0", "L0_cond_g_in", "L0_cond_null_attn_bias", "L0_cond_Wq",
          "L0_cond_Wkv", "L0_cond_Wo", "L0_cond_g_out", "L0_ffn_w_q", "L0_ffn_w_k", "L0_ffn_w_v", "L0_ffn_w_o",
          "L0_ffn_g1", "L0_ffn_g2", "L0_ffn_w_gate", "L0_ffn_w1", "L0_ffn_w3", "L0_ffn_w2"]


def rope_tables(S, HD):
    inv = 1.0 / np.float32(1000000.0) ** (np.arange(0, HD, 2, dtype=np.float32) / np.float32(HD))
    freqs = np.arange(S, dtype=np.float32)[:, None] * inv[None, :].astype(np.float32)
    emb = np.concatenate([freqs, freqs], -1).astype(np.float32)
    sign = np.where(np.arange(HD) < HD // 2, -1.0, 1.0).astype(np.float32)
    tok = np.stack([np.cos(emb), np.sin(emb) * sign], 1).astype(np.float32)
    return np.ascontiguousarray(tok), np.ascontiguousarray(tok.transpose(2, 1, 0))


def kernel(**inputs):
    import concourse.bacc as bacc
    from concourse.bass_utils import run_bass_kernel_spmd

    nc = bacc.Bacc("TRN2", target_bir_lowering=False, num_devices=1)
    arrays, args = {}, []

    def give(name, a):
        arrays[name] = a
        args.append(nc.dram_tensor(name, a.shape, mybir.dt.from_np(a.dtype), kind="ExternalInput").ap())

    for name in _NAMES:
        give(f"in_{name}", np.ascontiguousarray(inputs[name]))
    tok, feat = rope_tables(256, 128)
    give("in_rope_tok", tok)
    give("in_rope_feat", feat)
    args.append(nc.dram_tensor("out_0", inputs["x"].shape, F32, kind="ExternalOutput").ap())
    build(nc, *args)
    r = run_bass_kernel_spmd(nc, [arrays], core_ids=[0])
    return r.results[0]["out_0"]
```

```python
from contextlib import ExitStack

import numpy as np

import concourse.bass as bass
from concourse import mybir

F32 = mybir.dt.float32
F32R = mybir.dt.float32r
BF16 = mybir.dt.bfloat16
U8 = mybir.dt.uint8
ALU = mybir.AluOpType
ACT = mybir.ActivationFunctionType
AX = mybir.AxisListType

P = 128
EPS = 1e-5
MASKED = -1e30
MAGIC = 1.5 * 2.0**23
QMAX = 15.0


def build(nc, x, bias, cond, mask, g_in, null_bias, Wq, Wkv, Wo, g_out, w_q, w_k, w_v, w_o,
          g1, g2, w_gate, w1, w3, w2, rope_tok, rope_feat, out, dbg=None):
    B, N, D = x.shape
    T = B * N // P
    NT = B * N
    DH = cond.shape[1]
    HA = bias.shape[0]
    PAIRS_A = HA // 2
    HB = w_q.shape[0] // D
    KVH = w_k.shape[0] // D
    PAIRS_B = HB // 2
    E, FFN, _ = w1.shape
    HALF = NT // 2
    FC = 4
    FP = FFN // FC
    WG0 = T * E
    assert (B, N, D, DH) == (4, 256, P, 64) and FP == 112

    ctx = ExitStack()
    with ctx:
        def sb(name, shape, dt=F32):
            return ctx.enter_context(nc.sbuf_tensor(name, shape, dt))

        def sem(name):
            return ctx.enter_context(nc.semaphore(name))

        ps = ctx.enter_context(nc.psum_tensor("ps", [P, 8, 512], F32))

        identf = sb("identf", [P, P])
        identb = sb("identb", [P, P], BF16)
        gin_c = sb("gin_c", [P, 1])
        gout_b = sb("gout_b", [P, D])
        nk_b = sb("nk_b", [P, DH])
        vn_b = sb("vn_b", [P, DH])
        vn_c = sb("vn_c", [P, 1])
        nb_b = sb("nb_b", [P, HA])
        mask_u = sb("mask_u", [P, B, N], U8)
        mask_i1 = sb("mask_i1", [P, B, N], BF16)
        mask_i0 = sb("mask_i0", [P, B, P], BF16)
        x_sb = sb("x_sb", [P, T, D])
        xh = sb("xh", [P, T, D])
        xnT = sb("xnT", [P, NT])
        stats = sb("stats", [P, T, 6])
        mv = sb("mv", [P, T, 2])
        std = sb("std", [P, T])
        rstd = sb("rstd", [P, T])
        wkv_sb = sb("wkv_sb", [P, 2 * DH])
        wkk = sb("wkk", [P, P])
        kT = sb("kT", [P, 2, NT])
        kz = [kT[:, h, :] for h in range(2)]
        v_sb = sb("v_sb", [P, T, DH])
        wq_full = sb("wq_full", [P, HA * DH])
        u_sb = sb("u_sb", [P, HA])
        snull = sb("snull", [P, T, HA])
        wq_p = sb("wq_p", [P, P])
        bias_sb = [sb(f"bias{i}", [P, 2, (i + 1) * P]) for i in range(2)]
        qT = sb("qT", [P, NT])
        px = [sb(f"px{u}", [P, 4, N + 1]) for u in range(4)]
        negm = [sb(f"negm{u}", [P, 4]) for u in range(4)]
        lowest = [sb(f"lowest{u}", [P, 4]) for u in range(4)]
        sums = [sb(f"sums{u}", [P, 4]) for u in range(4)]
        rec = [sb(f"rec{u}", [P, 4]) for u in range(4)]
        pt = [sb(f"pt{k}", [P, 8, P]) for k in range(2)]
        oT = sb("oT", [P, PAIRS_A, NT])
        wo_sb = sb("wo_sb", [P, PAIRS_A, D])

        y_sb = sb("y_sb", [P, T, D])
        ssq = sb("ssq", [P, T])
        warm = sb("warm", [P, 1])
        g1_c = sb("g1_c", [P, 1])
        g2_c = sb("g2_c", [P, 1])
        x_hi = sb("x_hi", [P, NT], F32R)
        x_lo = sb("x_lo", [P, NT], F32R)
        GB = HB + 2 * KVH + HB
        wraw = sb("wraw", [P, GB, D])
        wint = sb("wint", [P, HB, D], BF16)
        q_stat = sb("q_stat", [P, 6, GB])
        wqT = sb("wqT", [P, HB, D], F32R)
        wqrT = sb("wqrT", [P, HB, D], F32R)
        sq_swap = sb("sq_swap", [P, HB])
        wkvT = sb("wkvT", [P, 2 * KVH * D])
        woT = sb("woT", [P, HB, D])
        kv_stat = sb("kv_stat", [P, 6, 2, 2, 8])
        kv_sb = sb("kv_sb", [P, T, 2 * KVH, D])
        k_rot = sb("k_rot", [P, T, KVH, D])
        rot_k = wq_full[:, 0:4 * D].rearrange("p (t d) -> p t d", t=4)
        cs_tok = sb("cs_tok", [P, 2, 2, D])
        cs_feat = sb("cs_feat", [P, 2, N])
        causal = sb("causal", [P, P], BF16)
        qa = [sb(f"qa{k}", [P, HALF]) for k in range(2)]
        qb = [sb(f"qb{k}", [P, HALF]) for k in range(2)]
        qrT = [sb(f"qrT{k}", [P, 2, HALF]) for k in range(3)]
        squares = qrT[0][:].rearrange("p h t -> p (h t)")
        wg = sb("wg", [E, D])
        wgT = sb("wgT", [P, E])
        lg = sb("lg", [P, T, E])
        lgm = sb("lgm", [P, T])
        gates = px[0][:].rearrange("p k c -> p (k c)")
        cmp = gates[:, 0:512].rearrange("p (t e f) -> p t e f", t=T, e=E)
        cmq = gates[:, 512:1024].rearrange("p (t e f) -> p t e f", t=T, e=E)
        below = sb("below", [P, E, E])
        rank = sb("rank", [P, T, E])
        rw = sb("rw", [P, T, E])
        rsm = sb("rsm", [P, T])
        hx = wq_full[:].rearrange("p (t d) -> p t d", t=T)
        spare = wraw[:].rearrange("p g d -> p (g d)")
        w13 = [spare[0:FP, k * 1024:k * 1024 + 2 * FC * D].rearrange("p (g d) -> p g d", g=2 * FC) for k in range(2)]
        i13 = sb("i13", [FP, 2 * FC, D], BF16)
        st13 = [sb(f"st13_{k}", [FP, 6, 2 * FC]) for k in range(2)]
        G2 = FFN * 2 // D
        R2 = D // 2
        st2 = sb("st2", [P, 6, G2])
        rotated = k_rot[:].rearrange("p t g d -> p (t g d)")
        w2r = rotated[:, 0:G2 * D].rearrange("p (g d) -> p g d", g=G2)
        w2T = rotated[0:FP, 1024:1024 + FC * 2 * D].rearrange("p (c e d) -> p c e d", c=FC, e=2)
        w13T = [sb("w13T", [P, 2 * FC, FP], F32R)[:], wqT[:, :, 0:FP]]
        free = oT[:].rearrange("p h t -> p (h t)")
        NBUF = 4
        gate = [free[0:FP, k * HALF:(k + 1) * HALF] for k in range(NBUF)]
        ups = [free[0:FP, (NBUF + k) * HALF:(NBUF + k + 1) * HALF] for k in range(NBUF)]
        up = [free[0:FP, (2 * NBUF + k) * HALF:(2 * NBUF + k + 1) * HALF] for k in range(NBUF)]
        rwb = [free[0:FP, 3 * NBUF * HALF + k * NT:3 * NBUF * HALF + (k + 1) * NT] for k in range(2)]
        rw3 = sb("rw3", [P, T, E, 3], BF16)
        rw_r = [sb(f"rw_r{k}", [P, T, E]) for k in range(2)]
        rwT = kT[:].rearrange("p a t -> p (a t)").bitcast(BF16)[:, 0:NT]
        pick = sb("pick", [P, E, FP], BF16)
        zrow = sb("zrow", [P, P], BF16)
        finite = mask_i1[:, 0:2, :].rearrange("p b c -> p (b c)")
        moeT = qrT[0][:].rearrange("p h t -> p (h t)")

        sems = {}

        def ev(name):
            if name not in sems:
                sems[name] = sem(name)
            return sems[name]

        s_x, s_small, s_wkv, s_wqf, s_wo, s_mask = (sem(n) for n in
                                                    ("x_in", "small_in", "wkv_in", "wqf_in", "wo_in", "mask_in"))
        s_wqp, s_bias1, s_bias0 = sem("wqp_in"), sem("bias1_in"), sem("bias0_in")
        s_ident, s_pool0 = sem("ident_ready"), sem("pool_setup")
        s_dve0, s_act0, s_pe0 = sem("dve_setup"), sem("act_setup"), sem("pe_setup")
        s_q, s_qev = sem("q_product"), sem("q_copied")
        s_scored, s_added, s_max, s_exp = sem("scored"), sem("bias_added"), sem("max_taken"), sem("exp_done")
        s_rec, s_norm, s_turn = sem("sum_inverted"), sem("probs_normalised"), sem("probs_turned")
        s_pta, s_ptd, s_pv, s_oev = sem("turned_copied_act"), sem("turned_copied_dve"), sem("values_mixed"), sem("mix_copied")
        s_wod, s_ln2 = sem("wo_done"), sem("ln2_chain")
        s_out = sem("out_written")
        s_zero = sem("key_rows_zeroed")

        block = ctx.enter_context(nc.Block())

        def unit(u):
            i = 1 if u < 2 else 0
            return i, u % 2, (i + 1) * P

        def blk(i, hd, b2, jt):
            return (hd * 2 + b2) * (i + 1) + jt

        def pt_banks(u):
            return (4, 5) if u < 2 else ((4,) if u == 2 else (5,))

        def back(hp, u, lag):
            if u >= lag:
                return hp, u - lag
            if isinstance(hp, int) and hp == 0:
                return None
            return hp - 1, u - lag + 4

        def after(do, hp, u, lag):
            at = back(hp, u, lag)
            if at is not None:
                do(*at)

        UNITS_B = 4 * PAIRS_B

        def unit_b(n):
            i = 1 - n % 2
            return i, n // (2 * PAIRS_B), n // 2 % PAIRS_B, (i + 1) * P, n % 4

        def banks_b(n):
            return ((4, 5), (4,), (4, 5), (5,))[n % 4]

        def copies_before(n, bank):
            return n // 4 * 3 + ((0, 1, 2, 3) if bank == 4 else (0, 1, 1, 2))[n % 4]

        def order(kv, half):
            return half * KVH + kv

        def kv_psum(kv, half):
            b = (0, 4, 2, 6)[order(kv, half)]
            return ps[:, b:b + 2, :].rearrange("p b (t g c) -> p (b t) g c", t=2, g=2)

        def key_bank(o):
            return 3 if o else 0

        W_STEPS = 12

        def positive(n):
            return not isinstance(n, int) or n > 0

        w13_in = [sem(f"w13_in_{k}") for k in range(2)]

        def load13(eng, e, k, q):
            eng.dma_start(w13[k][:, 0:FC, :], w1[bass.ts(e, 1)].rearrange("e (c p) d -> p (e c) d", p=FP)).then_inc(w13_in[k], 16)
            eng.dma_start(w13[k][:, FC:2 * FC, :], w3[bass.ts(e, 1)].rearrange("e (c p) d -> p (e c) d", p=FP)).then_inc(w13_in[k], 16)

        def load2(eng, q):
            src = w2[bass.ts(q, 2)].rearrange("e (r a) f -> (e r) (a f)", a=2)
            eng.dma_start(w2r.rearrange("r g c -> r (g c)"), src).then_inc(ev("w2_in"), 16)

        @block.sync
        def _(sp):
            sp.dma_start(x_sb[:], x.rearrange("b (i p) d -> p (b i) d", p=P)).then_inc(s_x, 16)
            sp.dma_start(wkv_sb[:], Wkv).then_inc(s_wkv, 16)
            sp.dma_start(wq_full[:], Wq).then_inc(s_wqf, 16)
            small = [
                (gin_c[:], g_in.rearrange("(d o) -> d o", o=1)),
                (gout_b[:], g_out.partition_broadcast(P)),
                (nk_b[:], cond[0].partition_broadcast(P)),
                (vn_b[:], cond[1].partition_broadcast(P)),
                (vn_c[0:DH, :], cond[1].rearrange("(d o) -> d o", o=1)),
                (vn_c[DH:P, :], cond[1].rearrange("(d o) -> d o", o=1)),
                (nb_b[:], null_bias.partition_broadcast(P)),
            ]
            for dst, src in small:
                sp.dma_start(dst, src).then_inc(s_small, 16)
            sp.dma_start(mask_u[:], mask.partition_broadcast(P)).then_inc(s_mask, 16)

            def load_pair(hp, s_in=None):
                sp.dma_start(wq_p[:], Wq[:, bass.ts(hp, P)]).then_inc(s_wqp, 16)
                sp.dma_start(bias_sb[1][:], bias[bass.ts(hp, 2), P:N, :].rearrange("h q k -> q h k")).then_inc(s_bias1, 16)
                sp.dma_start(bias_sb[0][:], bias[bass.ts(hp, 2), 0:P, 0:P].rearrange("h q k -> q h k")).then_inc(s_bias0, 16)

            load_pair(0)
            sp.dma_start(wo_sb[:], Wo.rearrange("(c p) d -> p c d", p=P)).then_inc(s_wo, 16)
            for n, (dst, src) in enumerate([
                    (wraw[:, 0:HB, :], w_q.rearrange("(h p) d -> p h d", p=P)),
                    (wraw[:, HB:HB + KVH, :], w_k.rearrange("(h p) d -> p h d", p=P)),
                    (wraw[:, HB + KVH:HB + 2 * KVH, :], w_v.rearrange("(h p) d -> p h d", p=P)),
                    (wraw[:, HB + 2 * KVH:GB, :], w_o.rearrange("p (h d) -> p h d", d=D)),
                    (g1_c[:], g1.rearrange("(d o) -> d o", o=1)),
                    (g2_c[:], g2.rearrange("(d o) -> d o", o=1)),
                    (cs_tok[:], rope_tok.rearrange("(i p) a d -> p i a d", p=P)),
                    (cs_feat[:], rope_feat),
                    (wg[:], w_gate)]):
                sp.dma_start(dst, src).then_inc(ev("b_in"), 16)
            sp.wait_ge(ev("w_chain"), 5)
            half = P // 2
            sp.dma_start(sq_swap[0:half, :], q_stat[half:P, 2, 0:HB]).then_inc(ev("scales_swapped"), 16)
            sp.dma_start(sq_swap[half:P, :], q_stat[0:half, 2, 0:HB]).then_inc(ev("scales_swapped"), 16)
            sp.wait_ge(ev("wo_turned"), 1)
            load13(sp, 0, 0, 0)
            load13(sp, 1, 1, 0)
            sp.wait_ge(ev("k_turned"), KVH * 2)
            load2(sp, 0)
            sp.wait_ge(ev("result"), T)
            sp.dma_start(out.rearrange("b (i p) d -> p (b i) d", p=P), hx).then_inc(s_out, 16)
            sp.wait_ge(s_out, 16)

        @block.gpsimd
        def _(pool):
            pool.memset(identf[:], 0.0).then_inc(s_pool0, 1)
            pool.wait_ge(s_pool0, 1)
            pool.affine_select(out=identf[:], in_=identf[:], compare_op=ALU.not_equal, fill=1.0, base=0,
                               pattern=[[-1, P]], channel_multiplier=1).then_inc(s_ident, 1)
            pool.wait_ge(s_ident, 1)
            pool.tensor_copy(identb[:], identf[:]).then_inc(s_ident, 1)
            pool.memset(below[:], 1.0).then_inc(s_pool0, 1)
            pool.memset(causal[:], 0.0).then_inc(s_pool0, 1)
            pool.wait_ge(s_pool0, 3)
            pool.affine_select(out=below[:], in_=below[:], compare_op=ALU.is_ge, fill=0.0, base=-1,
                               pattern=[[1, E], [-1, E]], channel_multiplier=0).then_inc(ev("b_const"), 1)
            pool.affine_select(out=causal[:], in_=causal[:], compare_op=ALU.is_ge, fill=MASKED, base=0,
                               pattern=[[-1, P]], channel_multiplier=1).then_inc(ev("b_const"), 1)
            pool.memset(pick[:], 1.0).then_inc(s_pool0, 1)
            pool.wait_ge(s_pool0, 4)
            pool.affine_select(out=pick[:], in_=pick[:], compare_op=ALU.is_ge, fill=0.0, base=0,
                               pattern=[[-3, E], [0, FP]], channel_multiplier=1).then_inc(s_pool0, 1)
            pool.wait_ge(s_pool0, 5)
            pool.affine_select(out=pick[:], in_=pick[:], compare_op=ALU.is_ge, fill=0.0, base=2,
                               pattern=[[3, E], [0, FP]], channel_multiplier=-1).then_inc(ev("pick_ready"), 1)
            pool.wait_ge(s_dve0, 22)
            pool.affine_select(out=mask_i0[:], in_=mask_i0[:], compare_op=ALU.is_ge, fill=MASKED, base=0,
                               pattern=[[0, B], [-1, P]], channel_multiplier=1).then_inc(s_pool0, 1)
            pool.affine_select(out=mask_i1[:, :, P:N], in_=mask_i1[:, :, P:N], compare_op=ALU.is_ge, fill=MASKED,
                               base=0, pattern=[[0, B], [-1, P]], channel_multiplier=1).then_inc(s_pool0, 1)

            def normalise(U, u):
                i, bh, W = unit(u)
                pool.wait_ge(s_rec, U + 1)
                pool.tensor_tensor(px[u][:, :, 0:W], px[u][:, :, 0:W], rec[u][:].unsqueeze(2).to_broadcast([P, 4, W]),
                                   ALU.mult).then_inc(s_norm, 1)

            def pair(hp):
                for u in range(4):
                    after(lambda h, v: normalise(h * 4 + v, v), hp, u, 1)

            pair(0)
            with pool.Fori(1, PAIRS_A) as hp:
                pair(hp)
            normalise(PAIRS_A * 4 - 1, 3)

            def rope_sum(p, hd):
                f = p * 2 + hd
                pool.wait_ge(ev("q_rotated"), 2 * f + 2)
                if p >= 3:
                    pool.wait_ge(ev("scored_b"), (p - 2) * 2)
                pool.tensor_tensor(qrT[p % 3][:, hd, :], qa[f % 2][:], qb[f % 2][:], ALU.add).then_inc(ev("q_summed"), 1)

            def normalise_b(n):
                i, half, hp, W, u = unit_b(n)
                pool.wait_ge(ev("inverted_b"), n + 1)
                pool.tensor_tensor(px[u][:, :, 0:W], px[u][:, :, 0:W], rec[u][:].unsqueeze(2).to_broadcast([P, 4, W]),
                                   ALU.mult).then_inc(ev("normalised_b"), 1)

            def scale13(e, k):
                pool.wait_ge(ev("inverse13"), e + 1)
                pool.tensor_tensor(w13[k], w13[k], st13[k][:, 3, :].unsqueeze(2).to_broadcast([FP, 2 * FC, D]),
                                   ALU.mult).then_inc(ev("scaled13"), 1)

            def scale2(q):
                pool.wait_ge(ev("inverse2"), q + 1)
                pool.tensor_tensor(w2r, w2r, st2[:, 3, :].unsqueeze(2).to_broadcast([P, G2, D]),
                                   ALU.mult).then_inc(ev("scaled2"), 1)

            def rope_keys(kv, half):
                pool.wait_ge(ev("kv_dequantised"), order(kv, half) + 1)
                h = D // 2
                ts = slice(half * 4, half * 4 + 4)
                kq = kv_sb[:, ts, kv, :].rearrange("p (b i) c -> p b i c", i=2)
                kr = k_rot[:, ts, kv, :].rearrange("p (b i) c -> p b i c", i=2)
                r = rot_k.rearrange("p (b i) c -> p b i c", i=2)
                if kv or half:
                    pool.wait_ge(ev("k_ready"), order(kv, half))
                cos = cs_tok[:, :, 0, :].unsqueeze(1).to_broadcast([P, 2, 2, D])
                pool.tensor_tensor(kr, kq, cos, ALU.mult)
                for a, b in ((0, h), (h, 0)):
                    sin = cs_tok[:, :, 1, a:a + h].unsqueeze(1).to_broadcast([P, 2, 2, h])
                    ins = pool.tensor_tensor(r[:, :, :, a:a + h], kq[:, :, :, b:b + h], sin, ALU.mult)
                ins.then_inc(ev("keys_rotated"), 1)
                pool.wait_ge(ev("keys_rotated"), order(kv, half) + 1)
                pool.tensor_tensor(kr, kr, r, ALU.add).then_inc(ev("k_ready"), 1)

            def split(name, half, done):
                pool.wait_ge(ev(name), half * 2 + 2)
                cols = slice(half * HALF, (half + 1) * HALF)
                pool.tensor_tensor(x_lo[:, cols], xnT[:, cols], x_hi[:, cols].bitcast(F32), ALU.subtract).then_inc(ev(done), 1)

            split("xn1_ready", 0, "x_split")
            split("xn1_ready", 1, "x_split")
            rope_sum(0, 0)
            rope_sum(0, 1)
            rope_keys(0, 0)
            rope_sum(1, 0)
            rope_sum(1, 1)
            for n in range(UNITS_B):
                if n:
                    normalise_b(n - 1)
                if n // 2 + 2 < 2 * PAIRS_B:
                    rope_sum(n // 2 + 2, n % 2)
                if n in (1, 5, 9):
                    rope_keys(*{1: (1, 0), 5: (0, 1), 9: (1, 1)}[n])
                if n == 10:
                    scale13(0, 0)
            normalise_b(UNITS_B - 1)
            scale2(0)

            pool.wait_ge(ev("scored_b"), UNITS_B)
            pool.memset(rwT, 0.0).then_inc(ev("rwT_zeroed"), 1)
            scale13(1, 1)
            split("hn_ready", 0, "hn_split")
            pool.wait_ge(ev("rms2_y"), 2)
            pool.tensor_tensor(hx, y_sb[:], x_sb[:], ALU.add).then_inc(ev("hx_ready"), 1)

            def product(q, j, s):
                n = q * 16 + j * 8 + s
                k = s % NBUF
                pool.wait_ge(ev("up_scaled"), n + 1)
                pool.wait_ge(ev("gate_ready"), n + 1)
                if positive(n - NBUF + 1):
                    pool.wait_ge(ev("down"), n - NBUF + 1)
                pool.tensor_tensor(up[k], ups[k], gate[k], ALU.mult).then_inc(ev("up_ready"), 1)

            def pair_c(q, last=False):
                for j in range(2):
                    for s in range(8):
                        product(q, j, s)
                        if isinstance(q, int) and (q, j) == (0, 0):
                            if s == 0:
                                split("hn_ready", 1, "hn_split")
                        if s == 0 and j == 1 and not last:
                            scale2(q + 1)
                        first = isinstance(q, int) and (q, j) == (0, 0)
                        if s == 1 and not (last and j == 1 or first):
                            scale13(q * 2 + j + 1, 1 - j)

            pair_c(0)
            with pool.Fori(1, E // 2 - 1) as q:
                pair_c(q)
            pair_c(E // 2 - 1, last=True)

        @block.scalar
        def _(act):
            act.wait_ge(s_dve0, 16)
            act.activation(std[:], mv[:, :, 1], ACT.Sqrt, bias=EPS).then_inc(s_act0, 1)
            act.wait_ge(s_pe0, 8)
            act.wait_ge(s_small, 16 * 7)
            act.activation(xnT[:], ps[:, 0:2, :].rearrange("p b c -> p (b c)"), ACT.Copy, scale=gin_c[:, 0:1]).then_inc(s_act0, 1)
            act.wait_ge(s_pe0, 10)
            act.wait_ge(s_zero, 2)
            for h in range(2):
                r = slice(DH * h, DH * h + DH)
                act.activation(kz[h][r, :], ps[r, 2:4, :].rearrange("p b c -> p (b c)"), ACT.Copy,
                               scale=float(DH) ** -0.5).then_inc(s_act0, 1)

            def exps(hp, u):
                i, bh, W = unit(u)
                act.wait_ge(s_max, hp * 4 + u + 1)
                for k in range(4):
                    ins = act.activation(px[u][:, k, 0:W + 1], px[u][:, k, 0:W + 1], ACT.Exp, bias=negm[u][:, k:k + 1], scale=-1.0,
                                         accum_out=sums[u][:, k:k + 1])
                ins.then_inc(s_exp, 1)

            def turned_copy(hp, u):
                act.wait_ge(s_turn, hp * 4 + u + 1)
                if not (isinstance(hp, int) and hp * 4 + u < 2):
                    act.wait_ge(s_pv, hp * 4 + u - 1)
                act.activation(pt[u % 2][:, 0:4, :], ps[:, 4, :].rearrange("p (k c) -> p k c", k=4), ACT.Copy).then_inc(s_pta, 1)

            def mix_copy(hp, u):
                i, bh, W = unit(u)
                act.wait_ge(s_pv, hp * 4 + u + 1)
                dst = oT[:, hp, :].rearrange("p (b i c) -> p b i c", b=B, i=2)[:, 2 * bh:2 * bh + 2, i, :]
                act.activation(dst, ps[:, 6, 0:2 * P].rearrange("p (b c) -> p b c", b=2), ACT.Identity,
                               bias=vn_c[:, 0:1]).then_inc(s_oev, 1)

            def q_copy(hp, half):
                act.wait_ge(s_q, hp * 2 + half + 1)
                if not isinstance(hp, int) or hp:
                    act.wait_ge(s_scored, hp * 4)
                act.activation(qT[:, half * HALF:(half + 1) * HALF], ps[:, 7, :], ACT.Copy).then_inc(s_qev, 1)

            def load_queries(hp):
                act.dma_start(wq_p[:], Wq[:, bass.ts(hp, P)]).then_inc(s_wqp, 16)

            def load_bias(hp, i):
                src = bias[bass.ts(hp, 2), i * P:(i + 1) * P, 0:(i + 1) * P].rearrange("h q k -> q h k")
                act.dma_start(bias_sb[i][:], src).then_inc(s_bias1 if i else s_bias0, 16)

            def dequantise_b(u):
                act.wait_ge(ev("w_chain"), (PAIRS_A - 1) * W_STEPS)
                n = (GB - HB) // 4
                for g in range(HB + n * u, HB + n * u + n):
                    act.activation(wraw[:, g, :], wraw[:, g, :], ACT.Copy, scale=q_stat[:, 2, g:g + 1]).then_inc(ev("w_dequantised"), 1)

            def pair(hp, last=False):
                for u in range(4):
                    after(turned_copy_a, hp, u, 3)
                    after(mix_copy, hp, u, 4)
                    after(exps, hp, u, 1)
                    if last:
                        dequantise_b(u)
                    if u == 0 and not (isinstance(hp, int) and hp == 0):
                        load_bias(hp, 0)
                    if last:
                        continue
                    if u == 1:
                        load_queries(hp + 1)
                    if u == 2:
                        load_bias(hp + 1, 1)
                    if u == 3:
                        q_copy(hp + 1, 0)
                        q_copy(hp + 1, 1)

            def turned_copy_a(hp, u):
                if u != 3:
                    turned_copy(hp, u)

            q_copy(0, 0)
            q_copy(0, 1)
            pair(0)
            with act.Fori(1, PAIRS_A - 1) as hp:
                pair(hp)
            pair(PAIRS_A - 1, last=True)
            exps(PAIRS_A - 1, 3)
            mix_copy(PAIRS_A - 1, 0)
            for u in range(1, 4):
                turned_copy_a(PAIRS_A - 1, u)
                mix_copy(PAIRS_A - 1, u)

            def root(src, dst, scale, before, after, n=1):
                act.wait_ge(before, n)
                act.activation(dst, src, ACT.Sqrt, bias=EPS, scale=scale).then_inc(after, 1)

            halves = [slice(4 * h, 4 * h + 4) for h in range(2)]

            def square_sums(name, half):
                act.wait_ge(ev(name + "_y"), half + 1)
                for t in range(4 * half, 4 * half + 4):
                    ins = act.activation(squares[:, t * D:(t + 1) * D], y_sb[:, t, :], ACT.Square, accum_out=ssq[:, t:t + 1])
                ins.then_inc(ev(name + "_sum"), 1)
                root(ssq[:, halves[half]], std[:, halves[half]], 1.0 / D, ev(name + "_sum"), ev(name + "_root"), half + 1)

            def transposed_copy(half, bank, gain, done):
                cols = slice(half * HALF, (half + 1) * HALF)
                for dst in (xnT, x_hi):
                    act.activation(dst[:, cols], ps[:, bank, :], ACT.Copy, scale=gain[:, 0:1]).then_inc(ev(done), 1)

            act.wait_ge(ev("wq_turned"), 1)
            turned = ps[:, 4, :].bitcast(BF16).rearrange("p (h c) -> p h c", h=HB)
            act.activation(wqT[:], turned, ACT.Copy).then_inc(ev("wqT_ready"), 1)
            half = P // 2
            act.activation(wqrT[:, :, 0:half], turned[:, :, half:P], ACT.Copy).then_inc(ev("wqT_ready"), 1)
            act.activation(wqrT[:, :, half:P], turned[:, :, 0:half], ACT.Copy).then_inc(ev("wqT_ready"), 1)
            act.wait_ge(ev("wkv_turned"), 1)
            act.activation(wkvT[:], ps[:, 5, :], ACT.Copy).then_inc(ev("wkvT_ready"), 1)
            act.wait_ge(ev("wo_turned"), 1)
            act.activation(woT[:], ps[:, 6:8, :].rearrange("p b (h c) -> p (b h) c", c=D), ACT.Copy).then_inc(ev("woT_ready"), 1)
            for half in range(2):
                root(mv[:, halves[half], 1], std[:, halves[half]], 1.0, ev("ln2_stats"), ev("ln2_root"), half + 1)
                square_sums("rms1", half)
                act.wait_ge(ev("rms1_turned"), half + 1)
                transposed_copy(half, 6 + half, g1_c, "xn1_ready")

            def scale_kv(kv, half):
                act.wait_ge(ev("kv_inverse"), order(kv, half) + 1)
                for t in range(4):
                    for g in range(2):
                        dst = kv_sb[:, half * 4 + t, g * KVH + kv, :]
                        src = kv_psum(kv, half)[:, t, g, :] if order(kv, half) == 0 else dst
                        ins = act.activation(dst, src, ACT.Copy, scale=kv_stat[:, 3, kv, half, t * 2 + g:t * 2 + g + 1])
                ins.then_inc(ev("kv_scaled"), 1)

            def dequantise_kv(kv, half):
                act.wait_ge(ev("kv_ints"), order(kv, half) + 1)
                for t in range(4):
                    for g in range(2):
                        dst = kv_sb[:, half * 4 + t, g * KVH + kv, :]
                        ins = act.activation(dst, dst, ACT.Copy, scale=kv_stat[:, 2, kv, half, t * 2 + g:t * 2 + g + 1])
                ins.then_inc(ev("kv_dequantised"), 1)

            def copy_keys(kv, half):
                act.wait_ge(ev("k_turned"), order(kv, half) + 1)
                act.activation(kT[:, kv, half * HALF:(half + 1) * HALF], ps[:, key_bank(order(kv, half)), :], ACT.Copy,
                               scale=float(D) ** -0.5).then_inc(ev("kT_ready"), 1)

            scale_kv(0, 0)
            for kv, half in ((1, 0), (0, 1), (1, 1)):
                act.wait_ge(ev("kv_product"), order(kv, half) + 1)
                act.activation(kv_sb[:, halves[half], :, :].rearrange("p t (g k) c -> p t g k c", k=KVH)[:, :, :, kv, :],
                               kv_psum(kv, half), ACT.Copy).then_inc(ev("kv_copied"), 1)
            dequantise_kv(0, 0)
            scale_kv(1, 0)
            copy_keys(0, 0)

            def exps_b(n):
                i, half, hp, W, u = unit_b(n)
                act.wait_ge(ev("max_b"), n + 1)
                if n >= 4:
                    act.wait_ge(ev("turned_b"), n - 3)
                for k in range(4):
                    src = ps[:, k // 2, (k % 2) * W:(k % 2 + 1) * W] if i else ps[:, 2, k * W:(k + 1) * W]
                    ins = act.activation(px[u][:, k, 0:W], src, ACT.Exp, bias=negm[u][:, k:k + 1],
                                         accum_out=sums[u][:, k:k + 1])
                ins.then_inc(ev("exp_b"), 1)

            def turned_copy_b(n):
                if 4 in banks_b(n):
                    act.wait_ge(ev("turned_b"), n + 1)
                    if n >= 2:
                        act.wait_ge(ev("mixed_b"), n - 1)
                    act.activation(pt[n % 2][:, 0:4, :], ps[:, 4, :].rearrange("p (k c) -> p k c", k=4), ACT.Copy).then_inc(ev("copied_act_b"), 1)

            def mix_copy_b(n):
                i, half, hp, W, u = unit_b(n)
                act.wait_ge(ev("mixed_b"), n + 1)
                for hd in range(2):
                    dst = oT[:, 2 * hp + hd, :].rearrange("p (b i c) -> p b i c", b=B, i=2)[:, 2 * half:2 * half + 2, i, :]
                    ins = act.activation(dst, ps[:, 6, hd * 2 * P:(hd + 1) * 2 * P].rearrange("p (b c) -> p b c", b=2), ACT.Copy)
                ins.then_inc(ev("mix_copied_b"), 1)

            for n in range(UNITS_B):
                if n >= 3:
                    turned_copy_b(n - 3)
                if n >= 4:
                    mix_copy_b(n - 4)
                if n in (2, 6):
                    scale_kv(n // 6, 1)
                if n:
                    exps_b(n - 1)
                if n in (0, 4, 8):
                    dequantise_kv(*{0: (1, 0), 4: (0, 1), 8: (1, 1)}[n])
                if n in (3, 7, 11):
                    copy_keys(*{3: (1, 0), 7: (0, 1), 11: (1, 1)}[n])
            last = UNITS_B - 1
            exps_b(last)
            mix_copy_b(last - 3)
            turned_copy_b(last - 2)
            square_sums("rms2", 0)
            mix_copy_b(last - 2)
            turned_copy_b(last - 1)
            mix_copy_b(last - 1)
            act.wait_ge(ev("wg_turned"), 1)
            act.activation(wgT[:], ps[:, 7, WG0:WG0 + E], ACT.Copy).then_inc(ev("wgT_ready"), 1)
            act.wait_ge(ev("rms2_turned"), 1)
            transposed_copy(0, 0, g2_c, "hn_ready")
            mix_copy_b(last)

            def copy13(e, k):
                act.wait_ge(ev("w13_turned"), e + 1)
                act.activation(w13T[k], ps[:, 4, :].bitcast(BF16)[:, 0:8 * FP].rearrange("p (g c) -> p g c", c=FP),
                               ACT.Copy).then_inc(ev("w13T_ready"), 1)

            def dequantise2(q):
                act.wait_ge(ev("ints2"), q + 1)
                for g in range(G2):
                    ins = act.activation(w2r[:, g, :], w2r[:, g, :], ACT.Copy, scale=st2[:, 2, g:g + 1])
                ins.then_inc(ev("w2_dequantised"), 1)

            def copy2(q, part):
                act.wait_ge(ev("w2_turned"), q * 2 + part + 1)
                n = q * 16 - 2 + 2 * part
                if positive(q * 16):
                    act.wait_ge(ev("down"), n)
                src = ps[0:FP, 5, :].rearrange("p (c a e r) -> p e c a r", c=2, a=2, e=2)
                for e in range(2):
                    dst = w2T[:, 2 * part:2 * part + 2, e, :].rearrange("p c (a r) -> p c a r", a=2)
                    ins = act.activation(dst, src[:, e], ACT.Copy)
                ins.then_inc(ev("w2T_ready"), 1)

            dequantise2(0)
            copy13(0, 0)

            def exp_gates(half):
                act.wait_ge(ev("logits_shifted"), half + 1)
                act.activation(lg[:, halves[half], :], lg[:, halves[half], :], ACT.Exp).then_inc(ev("gates_exp"), 1)

            exp_gates(0)
            copy2(0, 0)
            act.activation(warm[:], ssq[:, 0:1], ACT.Sqrt, bias=EPS)

            def copy_gates(e, k, half):
                act.wait_ge(ev("rw_spread"), e * 2 + half + 1)
                if positive(e * 8 - 8):
                    act.wait_ge(ev("up_scaled"), e * 8 - 8)
                act.activation(rwb[k][:, half * HALF:(half + 1) * HALF], ps[0:FP, 5, :], ACT.Copy).then_inc(ev("rwb_ready"), 1)

            def turned_gates(half):
                act.wait_ge(ev("rwT_zeroed"), 1)
                act.wait_ge(ev("rw_turned"), half + 1)
                act.activation(rwT[0:3 * E, half * HALF:(half + 1) * HALF], ps[0:3 * E, 5, :].bitcast(BF16)[:, 0:HALF],
                               ACT.Copy).then_inc(ev("rwT_ready"), 1)

            def silu(q, j, s):
                n = q * 16 + j * 8 + s
                act.wait_ge(ev("gate_product"), n + 1)
                if positive(n - NBUF + 1):
                    act.wait_ge(ev("up_ready"), n - NBUF + 1)
                c = s % FC
                act.activation(gate[s % NBUF], ps[0:FP, 2 * (s % 2), :], ACT.Silu, scale=st13[j][:, 2, c:c + 1]).then_inc(ev("gate_ready"), 1)


            turned_gates(0)
            square_sums("rms2", 1)
            copy_gates(0, 0, 0)

            def pair_c(q, last=False):
                for j in range(2):
                    e = q * 2 + j
                    more = not (last and j == 1)
                    first = isinstance(q, int) and (q, j) == (0, 0)
                    for s in range(8):
                        silu(q, j, s)
                        if s == 0 and not last:
                            act.wait_ge(ev("ints13"), e + 1)
                            load13(act, e + 2, j, q + 1)
                        if s == 0 and first:
                            act.wait_ge(ev("rms2_turned"), 2)
                            transposed_copy(1, 7, g2_c, "hn_ready")
                        if s == 1 and j == 0:
                            copy2(q, 1)
                            if not last:
                                load2(act, q + 1)
                        if s == 1 and first:
                            exp_gates(1)
                        if s == 5 and first:
                            turned_gates(1)
                            copy_gates(0, 0, 1)
                        if s in ((6, 7) if first else (4, 5)) and more:
                            copy_gates(e + 1, 1 - j, s % 2)
                        if s == 5 and j == 1 and more:
                            dequantise2(q + 1)
                        if s == 6 and more:
                            copy13(e + 1, 1 - j)
                        if s == 7 and j == 1 and more:
                            copy2(q + 1, 0)

            pair_c(0)
            with act.Fori(1, E // 2 - 1) as q:
                pair_c(q)
            pair_c(E // 2 - 1, last=True)
            for half in range(2):
                act.wait_ge(ev("experts_summed"), half + 1)
                act.activation(moeT[:, half * HALF:(half + 1) * HALF], ps[:, 6 + half, :], ACT.Copy).then_inc(ev("moeT_ready"), 1)

        @block.vector
        def _(dve):
            n0 = [0]

            def m0(ins):
                n0[0] += 1
                ins.then_inc(s_dve0, 1)

            for h in range(2):
                dve.memset(kz[h], 0.0).then_inc(s_zero, 1)
            dve.wait_ge(s_x, 16)
            for t in range(T):
                m0(dve.bn_stats(stats[:, t, :], x_sb[:, t, :]))
            for t in range(T):
                dve.wait_ge(s_dve0, t + 1)
                m0(dve.bn_aggr(mv[:, t, :], stats[:, t, :]))
            dve.wait_ge(s_small, 16 * 7)
            dve.wait_ge(s_wqf, 16)
            dve.wait_ge(s_wkv, 16)
            m0(dve.tensor_copy(wkk[:, 0:DH], wkv_sb[:, 0:DH]))
            m0(dve.tensor_copy(wkk[:, DH:P], wkv_sb[:, 0:DH]))
            prod = oT[:, 0, :]
            m0(dve.tensor_tensor(prod.rearrange("p (h c) -> p h c", h=HA), wq_full[:].rearrange("p (h c) -> p h c", h=HA),
                                 nk_b[:].unsqueeze(1).to_broadcast([P, HA, DH]), ALU.mult))
            dve.wait_ge(s_dve0, 19)
            m0(dve.tensor_reduce(u_sb[:], prod.rearrange("p (h c) -> p h c", h=HA), AX.X, ALU.add))
            dve.wait_ge(s_mask, 16)
            m0(dve.tensor_scalar(mask_i1[:], mask_u[:], -1.0, -MASKED, ALU.add, ALU.mult))
            m0(dve.tensor_scalar(mask_i0[:], mask_u[:, :, 0:P], -1.0, -MASKED, ALU.add, ALU.mult))
            dve.wait_ge(s_act0, 1)
            m0(dve.reciprocal(rstd[:], std[:]))
            dve.wait_ge(s_dve0, 23)
            for t in range(T):
                m0(dve.tensor_scalar(xh[:, t, :], x_sb[:, t, :], mv[:, t, 0:1], rstd[:, t:t + 1], ALU.subtract, ALU.mult))
            dve.wait_ge(s_pe0, 12)
            m0(dve.tensor_tensor(v_sb[:], ps[:, 4:6, :].rearrange("p b (t c) -> p (b t) c", c=P)[:, :, DH:P],
                                 vn_b[:].unsqueeze(1).to_broadcast([P, T, DH]), ALU.subtract))
            dve.wait_ge(s_pe0, 13)
            dve.wait_ge(s_small, 16 * 7)
            m0(dve.scalar_tensor_tensor(out=snull[:], in0=ps[:, 6, 0:T * HA].rearrange("p (t h) -> p t h", h=HA),
                                        scalar=-float(DH) ** -0.5, in1=nb_b[:].unsqueeze(1).to_broadcast([P, T, HA]),
                                        op0=ALU.mult, op1=ALU.subtract))
            dve.wait_ge(s_dve0, 33)

            def null_scores(hp, i, bh):
                return snull[:].rearrange("p (b i) h -> p b i h", i=2)[:, 2 * bh:2 * bh + 2, i, bass.ts(hp, 2)]

            def add(hp, u):
                i, bh, W = unit(u)
                dve.wait_ge(s_scored, hp * 4 + u + 1)
                dve.wait_ge(s_bias1 if i else s_bias0, hp * 16 + 16)
                if not isinstance(hp, int) or hp:
                    dve.wait_ge(s_turn, hp * 4 + u - 3)
                dve.tensor_copy(px[u][:, :, W].rearrange("p (h b) -> p b h", b=2), null_scores(hp, i, bh))
                k = u % 2
                for hd in range(2):
                    for b2 in range(2):
                        n = 2 * hd + b2
                        ins = dve.tensor_tensor_reduce(px[u][:, n, 0:W], ps[:, 2 * k + hd, b2 * W:(b2 + 1) * W], bias_sb[i][:, hd, :],
                                                       -1.0, -MASKED, ALU.add, ALU.min, lowest[u][:, n:n + 1])
                ins.then_inc(s_added, 1)

            def rowmax(hp, u):
                i, bh, W = unit(u)
                dve.wait_ge(s_added, hp * 4 + u + 1)
                dve.tensor_tensor(negm[u][:].rearrange("p (h b) -> p b h", b=2), lowest[u][:].rearrange("p (h b) -> p b h", b=2),
                                  null_scores(hp, i, bh), ALU.min).then_inc(s_max, 1)

            def invert(hp, u):
                dve.wait_ge(s_exp, hp * 4 + u + 1)
                dve.reciprocal(rec[u][:], sums[u][:]).then_inc(s_rec, 1)

            def turned_copy(hp, u):
                dve.wait_ge(s_turn, hp * 4 + u + 1)
                if not (isinstance(hp, int) and hp * 4 + u < 2):
                    dve.wait_ge(s_pv, hp * 4 + u - 1)
                o = 4 if u < 2 else 0
                dve.tensor_copy(pt[u % 2][:, o:o + 4, :], ps[:, 5, :].rearrange("p (k c) -> p k c", k=4)).then_inc(s_ptd, 1)

            def turned_copy_d(hp, u):
                if u != 2:
                    turned_copy(hp, u)

            def pair(hp, last=False):
                for u in range(4):
                    after(turned_copy_d, hp, u, 3)
                    if not last:
                        weight_step(hp, 3 * u)
                    add(hp, u)
                    if not last:
                        weight_step(hp, 3 * u + 1)
                    after(invert, hp, u, 1)
                    rowmax(hp, u)
                    if not last:
                        weight_step(hp, 3 * u + 2)

            def levels(st, done, count, step):
                step(dve.tensor_tensor(st(2), st(0), st(1), ALU.subtract))
                step(dve.tensor_scalar(st(2), st(2), 1e-5, 1.0 / QMAX, ALU.max, ALU.mult))
                dve.reciprocal(st(3), st(2)).then_inc(done, 1)
                dve.wait_ge(done, count)
                step(dve.tensor_tensor(st(4), st(1), st(3), ALU.mult))
                step(dve.tensor_scalar(st(4), st(4), MAGIC, MAGIC, ALU.add, ALU.min))
                step(dve.tensor_scalar(st(4), st(4), MAGIC - QMAX, None, ALU.max))
                return dve.tensor_scalar(st(5), st(4), -MAGIC, QMAX, ALU.add, ALU.add)


            def weight_step(hp, i):
                if isinstance(hp, int):
                    at, n, dst = slice(0, HB), HB, wint[:]
                else:
                    at, n = bass.ts(hp + (HB // 2 - 1), 2), 2
                    dst = wraw[:, at, :]
                w = wraw[:, at, :]
                rows = [q_stat[:, r, at] for r in range(6)]
                top, low, scale, inverse, first, last = rows

                def wide(row):
                    return row.unsqueeze(2).to_broadcast([P, n, D])

                if i:
                    dve.wait_ge(ev("w_chain"), hp * W_STEPS + i)
                elif isinstance(hp, int):
                    dve.wait_ge(ev("b_in"), 16 * 9)
                if i == 0:
                    ins = dve.tensor_reduce(top, w, AX.X, ALU.max)
                elif i == 1:
                    ins = dve.tensor_reduce(low, w, AX.X, ALU.min)
                elif i == 2:
                    ins = dve.tensor_tensor(scale, top, low, ALU.subtract)
                elif i == 3:
                    ins = dve.tensor_scalar(scale, scale, 1e-5, 1.0 / QMAX, ALU.max, ALU.mult)
                elif i == 4:
                    ins = dve.reciprocal(inverse, scale)
                elif i == 5:
                    ins = dve.tensor_tensor(first, low, inverse, ALU.mult)
                elif i == 6:
                    ins = dve.tensor_scalar(first, first, MAGIC, MAGIC, ALU.add, ALU.min)
                elif i == 7:
                    ins = dve.tensor_scalar(first, first, MAGIC - QMAX, None, ALU.max)
                elif i == 8:
                    ins = dve.tensor_scalar(last, first, -MAGIC, QMAX, ALU.add, ALU.add)
                elif i == 9:
                    ins = dve.tensor_tensor(w, w, wide(inverse), ALU.mult)
                elif i == 10:
                    ins = dve.scalar_tensor_tensor(out=w, in0=w, scalar=MAGIC, in1=wide(first), op0=ALU.add, op1=ALU.max)
                elif i == 11:
                    ins = dve.scalar_tensor_tensor(out=dst, in0=w, scalar=-MAGIC, in1=wide(last), op0=ALU.add, op1=ALU.min)
                ins.then_inc(ev("w_chain"), 1)

            pair(0)
            with dve.Fori(1, PAIRS_A - 1) as hp:
                pair(hp)
            pair(PAIRS_A - 1, last=True)
            invert(PAIRS_A - 1, 3)
            for u in range(1, 4):
                turned_copy_d(PAIRS_A - 1, u)
            chain = [0]

            def link(ins):
                chain[0] += 1
                ins.then_inc(ev("dve_chain"), 1)
                dve.wait_ge(ev("dve_chain"), chain[0])

            def normalise_rms(name, half):
                dve.wait_ge(ev(name + "_root"), half + 1)
                hs = slice(half * 4, half * 4 + 4)
                link(dve.reciprocal(rstd[:, hs], std[:, hs]))
                for t in range(half * 4, half * 4 + 4):
                    dve.tensor_scalar(xh[:, t, :], y_sb[:, t, :], rstd[:, t:t + 1], None, ALU.mult).then_inc(ev(name + "_scaled"), 1)

            for half in range(2):
                hs = slice(half * 4, half * 4 + 4)
                for t in range(half * 4, half * 4 + 4):
                    dve.wait_ge(s_wod, t // 2 * 2 + 2)
                    src = ps[:, t // 2, (t % 2) * P:(t % 2 + 1) * P]
                    link(dve.bn_stats(stats[:, t, :], src))
                    ins = dve.bn_aggr(mv[:, t, :], stats[:, t, :])
                ins.then_inc(ev("ln2_stats"), 1)
                dve.wait_ge(ev("ln2_root"), half + 1)
                link(dve.reciprocal(rstd[:, hs], std[:, hs]))
                for t in range(half * 4, half * 4 + 4):
                    src = ps[:, t // 2, (t % 2) * P:(t % 2 + 1) * P]
                    ins = dve.tensor_scalar(xh[:, t, :], src, mv[:, t, 0:1], rstd[:, t:t + 1], ALU.subtract, ALU.mult)
                link(ins)
                dve.tensor_tensor(y_sb[:, hs, :], xh[:, hs, :], gout_b[:].unsqueeze(1).to_broadcast([P, 4, D]),
                                  ALU.mult).then_inc(ev("rms1_y"), 1)
                normalise_rms("rms1", half)

            def kvf(kv, half):
                return kv_sb[:, half * 4:half * 4 + 4, :, :].rearrange("p t (g k) c -> p t g k c", k=KVH)[:, :, :, kv, :]

            def kv_st(kv, half, wide=False):
                def st(row):
                    a = kv_stat[:, row, kv, half, :]
                    return a.rearrange("p (t g) -> p t g", g=2).unsqueeze(3).to_broadcast([P, 4, 2, D]) if wide else a
                return st

            def kv_max(kv, half, step):
                o = order(kv, half)
                if o:
                    dve.wait_ge(ev("kv_copied"), o)
                else:
                    dve.wait_ge(ev("kv_product"), 1)
                src = kvf(kv, half) if o else kv_psum(kv, half)
                dve.tensor_reduce(kv_st(kv, half)(0).rearrange("p (t g) -> p t g", g=2), src, AX.X, ALU.max)

            def kv_min(kv, half, step):
                src = kvf(kv, half) if order(kv, half) else kv_psum(kv, half)
                step(dve.tensor_reduce(kv_st(kv, half)(1).rearrange("p (t g) -> p t g", g=2), src, AX.X, ALU.min))
                levels(kv_st(kv, half), ev("kv_inverse"), order(kv, half) + 1, step)

            def kv_low(kv, half, step):
                dve.wait_ge(ev("kv_scaled"), order(kv, half) + 1)
                w = kvf(kv, half)
                step(dve.scalar_tensor_tensor(out=w, in0=w, scalar=MAGIC, in1=kv_st(kv, half, True)(4), op0=ALU.add, op1=ALU.max))

            def kv_ints(kv, half, step):
                w = kvf(kv, half)
                dve.scalar_tensor_tensor(out=w, in0=w, scalar=-MAGIC, in1=kv_st(kv, half, True)(5),
                                         op0=ALU.add, op1=ALU.min).then_inc(ev("kv_ints"), 1)

            def rope_q(p, hd, k):
                f = p * 2 + hd
                h = 2 * (p % PAIRS_B) + hd
                dst, scale = ((qa, q_stat[:, 2, h:h + 1]), (qb, sq_swap[:, h:h + 1]))[k]
                dve.wait_ge(ev("q_product_b"), 2 * f + k + 1)
                if f >= 2:
                    dve.wait_ge(ev("q_summed"), f - 1)
                if f == 0 and k:
                    dve.wait_ge(ev("scales_swapped"), 32)
                bank = 6 + k if p < 2 else 7
                dve.scalar_tensor_tensor(out=dst[f % 2][:].rearrange("p (b c) -> p b c", b=2),
                                         in0=ps[:, bank, :].rearrange("p (b c) -> p b c", b=2), scalar=scale,
                                         in1=cs_feat[:, k, :].unsqueeze(1).to_broadcast([P, 2, N]),
                                         op0=ALU.mult, op1=ALU.mult).then_inc(ev("q_rotated"), 1)

            def rowmax_b(n):
                i, half, hp, W, u = unit_b(n)
                dve.wait_ge(ev("scored_b"), n + 1)
                if i:
                    src = ps[:, 0:2, :].rearrange("p h (b c) -> p h b c", b=2)
                else:
                    src = ps[:, 2, :].rearrange("p (h b c) -> p h b c", h=2, b=2)
                dve.tensor_reduce(negm[u][:].rearrange("p (h b) -> p h b", h=2), src,
                                  AX.X, ALU.max, negate=True).then_inc(ev("max_b"), 1)

            def invert_b(n):
                u = n % 4
                dve.wait_ge(ev("exp_b"), n + 1)
                dve.reciprocal(rec[u][:], sums[u][:]).then_inc(ev("inverted_b"), 1)

            def turned_copy_b(n):
                if 5 in banks_b(n):
                    dve.wait_ge(ev("turned_b"), n + 1)
                    if n >= 2:
                        dve.wait_ge(ev("mixed_b"), n - 1)
                    o = 0 if n % 2 else 4
                    dve.tensor_copy(pt[n % 2][:, o:o + 4, :], ps[:, 5, :].rearrange("p (k c) -> p k c", k=4)).then_inc(ev("copied_dve_b"), 1)

            def max13(n, k, step):
                dve.wait_ge(w13_in[k], (n * 16 + (2 - k) * 16))
                if positive(n * 8 - 8):
                    dve.wait_ge(ev("gate_ready"), n * 8 - 8)
                dve.tensor_reduce(st13[k][:, 0, :], w13[k], AX.X, ALU.max)

            def min13(n, k, step):
                step(dve.tensor_reduce(st13[k][:, 1, :], w13[k], AX.X, ALU.min))
                levels(lambda row: st13[k][:, row, :], ev("inverse13"), n + 1, step)

            def max2(n, k, step):
                dve.wait_ge(ev("w2_in"), n * 16 + 16)
                if positive(n):
                    dve.wait_ge(ev("w2_dequantised"), n)
                dve.tensor_reduce(st2[:, 0, :], w2r, AX.X, ALU.max)

            def min2(n, k, step):
                step(dve.tensor_reduce(st2[:, 1, :], w2r, AX.X, ALU.min))
                levels(lambda row: st2[:, row, :], ev("inverse2"), n + 1, step)

            def low13(n, k, step):
                dve.wait_ge(ev("scaled13"), n + 1)
                step(dve.scalar_tensor_tensor(out=w13[k], in0=w13[k], scalar=MAGIC, in1=st13[k][:, 4, :].unsqueeze(2).to_broadcast([FP, 2 * FC, D]),
                                              op0=ALU.add, op1=ALU.max))

            def ints13(n, k, step):
                if positive(n):
                    dve.wait_ge(ev("w13_turned"), n)
                dve.scalar_tensor_tensor(out=i13[:], in0=w13[k], scalar=-MAGIC, in1=st13[k][:, 5, :].unsqueeze(2).to_broadcast([FP, 2 * FC, D]),
                                         op0=ALU.add, op1=ALU.min).then_inc(ev("ints13"), 1)

            def low2(n, k, step):
                dve.wait_ge(ev("scaled2"), n + 1)
                step(dve.scalar_tensor_tensor(out=w2r, in0=w2r, scalar=MAGIC, in1=st2[:, 4, :].unsqueeze(2).to_broadcast([P, G2, D]),
                                              op0=ALU.add, op1=ALU.max))

            def ints2(n, k, step):
                dve.scalar_tensor_tensor(out=w2r, in0=w2r, scalar=-MAGIC, in1=st2[:, 5, :].unsqueeze(2).to_broadcast([P, G2, D]),
                                         op0=ALU.add, op1=ALU.min).then_inc(ev("ints2"), 1)

            kv_max(0, 0, link)
            kv_min(0, 0, link)
            rope_q(0, 0, 0)
            kv_low(0, 0, link)
            kv_ints(0, 0, link)
            rope_q(0, 0, 1)
            rope_q(0, 1, 0)
            rope_q(0, 1, 1)
            kv_max(1, 0, link)
            kv_min(1, 0, link)
            for hd in range(2):
                for k in range(2):
                    rope_q(1, hd, k)
            kv_low(1, 0, link)
            kv_ints(1, 0, link)

            def add_o(half, bank):
                dve.wait_ge(ev("o_product"), half * 4 + 4)
                y = y_sb[:, half * 4:half * 4 + 4, :]
                dve.tensor_tensor(y, ps[:, bank, :].rearrange("p (t d) -> p t d", d=D), y, ALU.add).then_inc(ev("rms2_y"), 1)

            between = {0: [(kv_max, 0, 1)], 1: [(kv_min, 0, 1)], 2: [(kv_low, 0, 1)], 3: [(kv_ints, 0, 1)], 4: [(kv_max, 1, 1)],
                       5: [(kv_min, 1, 1)], 6: [(kv_low, 1, 1)], 7: [(kv_ints, 1, 1)],
                       8: [(max13, 0, 0)], 9: [(min13, 0, 0)], 11: [(low13, 0, 0)], 12: [(ints13, 0, 0)],
                       14: [(max2, 0, 0)], 15: [(min2, 0, 0)]}
            for n in range(UNITS_B):
                if n >= 3:
                    turned_copy_b(n - 3)
                more = n // 2 + 2 < 2 * PAIRS_B
                if more:
                    rope_q(n // 2 + 2, n % 2, 0)
                rowmax_b(n)
                if more:
                    rope_q(n // 2 + 2, n % 2, 1)
                if n:
                    invert_b(n - 1)
                for work, a, b in between.get(n, []):
                    work(a, b, link)
            last = UNITS_B - 1
            invert_b(last)
            add_o(0, 3)
            turned_copy_b(last - 2)
            turned_copy_b(last - 1)
            normalise_rms("rms2", 0)
            turned_copy_b(last)
            low2(0, 0, link)
            ints2(0, 0, link)
            max13(1, 1, link)
            dve.memset(zrow[:], 0.0).then_inc(ev("zeros"), 1)

            def route(half, part):
                hs = slice(half * 4, half * 4 + 4)
                l, g, r = lg[:, hs, :], rw[:, hs, :], rank[:, hs, :]
                more, same = cmp[:, hs], cmq[:, hs]
                parts = rw3[:, hs]
                if part == 0:
                    dve.wait_ge(ev("logits"), half + 1)
                    dve.tensor_copy(l, ps[:, 7, 0:4 * E].rearrange("p (t e) -> p t e", e=E)).then_inc(ev("logits_copied"), 1)
                    dve.wait_ge(ev("logits_copied"), half + 1)
                    link(dve.tensor_reduce(lgm[:, hs], l, AX.X, ALU.max, negate=True))
                    dve.tensor_tensor(l, l, lgm[:, hs].unsqueeze(2).to_broadcast([P, 4, E]), ALU.add).then_inc(ev("logits_shifted"), 1)
                if part == 1:
                    dve.wait_ge(ev("gates_exp"), half + 1)
                    dve.wait_ge(ev("b_const"), 2)
                    mine = l.unsqueeze(3).to_broadcast([P, 4, E, E])
                    other = l.unsqueeze(2).to_broadcast([P, 4, E, E])
                    dve.tensor_tensor(more, other, mine, ALU.is_gt)
                    link(dve.tensor_tensor(same, other, mine, ALU.is_equal))
                    link(dve.tensor_tensor(same, same, below[:].unsqueeze(1).to_broadcast([P, 4, E, E]), ALU.mult))
                    link(dve.tensor_tensor(more, more, same, ALU.add))
                    link(dve.tensor_reduce(r, more, AX.X, ALU.add))
                    link(dve.scalar_tensor_tensor(out=g, in0=r, scalar=2.0, in1=l, op0=ALU.is_lt, op1=ALU.mult))
                if part == 2:
                    link(dve.tensor_reduce(rsm[:, hs], g, AX.X, ALU.add))
                    link(dve.reciprocal(rsm[:, hs], rsm[:, hs]))
                    link(dve.tensor_tensor(g, g, rsm[:, hs].unsqueeze(2).to_broadcast([P, 4, E]), ALU.mult))
                    link(dve.tensor_copy(parts[:, :, :, 0], g))
                    link(dve.tensor_tensor(rw_r[0][:, hs], g, parts[:, :, :, 0], ALU.subtract))
                    link(dve.tensor_copy(parts[:, :, :, 1], rw_r[0][:, hs]))
                    link(dve.tensor_tensor(rw_r[1][:, hs], rw_r[0][:, hs], parts[:, :, :, 1], ALU.subtract))
                    dve.tensor_copy(parts[:, :, :, 2], rw_r[1][:, hs]).then_inc(ev("rw_split"), 1)

            route(0, 0)
            min13(1, 1, link)
            route(0, 1)
            route(0, 2)
            add_o(1, 6)
            normalise_rms("rms2", 1)

            def scale_up(q, j, s):
                n = q * 16 + j * 8 + s
                half, c = s // FC, s % FC
                dve.wait_ge(ev("up_product"), n + 1)
                if c == 0:
                    dve.wait_ge(ev("rwb_ready"), q * 4 + j * 2 + half + 1)
                if positive(n - NBUF + 1):
                    dve.wait_ge(ev("up_ready"), n - NBUF + 1)
                dve.scalar_tensor_tensor(out=ups[s % NBUF], in0=ps[0:FP, 2 * (s % 2) + 1, :],
                                         scalar=st13[j][:, 2, FC + c:FC + c + 1], in1=rwb[j][:, half * HALF:(half + 1) * HALF],
                                         op0=ALU.mult, op1=ALU.mult).then_inc(ev("up_scaled"), 1)

            LINKS_C = 21
            LINKS_13 = 6

            def pair_c(q, last=False):
                k = [0]

                def step(ins):
                    k[0] += 1
                    ins.then_inc(ev("c_chain"), 1)
                    base = q * LINKS_C - LINKS_13 if not isinstance(q, int) or q else 0
                    dve.wait_ge(ev("c_chain"), base + k[0])

                for j in range(2):
                    n = q * 2 + j + 1
                    for s in range(8):
                        scale_up(q, j, s)
                        if isinstance(q, int) and (q, j) == (0, 0) and s in (1, 2, 3):
                            route(1, s - 1)
                        first = isinstance(q, int) and (q, j) == (0, 0)
                        if not (last and j == 1):
                            work = ({0: low13, 4: ints13} if first else {0: max13, 1: min13, 4: low13, 5: ints13}).get(s)
                            if work:
                                work(n, 1 - j, step)
                        if not last:
                            work = {(0, 6): max2, (0, 7): min2, (1, 2): low2, (1, 3): ints2}.get((j, s))
                            if work:
                                work(q + 1, 0, step)
                assert last or k[0] == (LINKS_C if not isinstance(q, int) else LINKS_C - LINKS_13), k[0]

            pair_c(0)
            with dve.Fori(1, E // 2 - 1) as q:
                pair_c(q)
            pair_c(E // 2 - 1, last=True)
            dve.wait_ge(ev("hx_ready"), 1)
            for t in range(T):
                dve.wait_ge(ev("moe_turned"), t + 1)
                moe = ps[:, t % 4, 0:D].rearrange("p (a r) -> p r a", a=2)
                dve.tensor_tensor(hx[:, t, :].rearrange("p (r a) -> p r a", a=2), moe,
                                  hx[:, t, :].rearrange("p (r a) -> p r a", a=2), ALU.add).then_inc(ev("result"), 1)

        @block.tensor
        def _(pe):
            pe.wait_ge(s_ident, 2)
            for t in range(T):
                pe.wait_ge(s_dve0, 24 + t)
                pe.transpose(ps[:, t // 4, (t % 4) * P:(t % 4) * P + P], xh[:, t, :], identf[:]).then_inc(s_pe0, 1)
            pe.wait_ge(s_act0, 2)
            for half in range(2):
                pe.matmul(ps[:, 2 + half, :], wkk[:], xnT[:, half * HALF:(half + 1) * HALF], start=True, stop=True).then_inc(s_pe0, 1)
            pe.wait_ge(s_wkv, 16)
            for t in range(T):
                ins = pe.matmul(ps[:, 4 + t // 4, (t % 4) * P:(t % 4) * P + P], xnT[:, t * P:(t + 1) * P], wkv_sb[:],
                                start=True, stop=True)
                if t % 4 == 3:
                    ins.then_inc(s_pe0, 1)
            for t in range(T):
                ins = pe.matmul(ps[:, 6, t * HA:(t + 1) * HA], xnT[:, t * P:(t + 1) * P], u_sb[:], start=True, stop=True)
            ins.then_inc(s_pe0, 1)

            def queries(hp, half):
                pe.wait_ge(s_wqp, hp * 16 + 16)
                if not (isinstance(hp, int) and hp == 0 and half == 0):
                    pe.wait_ge(s_qev, hp * 2 + half)
                pe.matmul(ps[:, 7, :], wq_p[:], xnT[:, half * HALF:(half + 1) * HALF], start=True, stop=True).then_inc(s_q, 1)

            def scores(hp, u):
                i, bh, W = unit(u)
                k = u % 2
                pe.wait_ge(s_qev, hp * 2 + bh + 1)
                if not (isinstance(hp, int) and hp * 4 + u < 2):
                    pe.wait_ge(s_added, hp * 4 + u - 1)
                for hd in range(2):
                    for b2 in range(2):
                        b = 2 * bh + b2
                        t = 2 * b + i
                        dst = ps[:, 2 * k + hd, b2 * W:(b2 + 1) * W]
                        pe.matmul(dst, qT[:, t * P:(t + 1) * P], kz[hd][:, b * N:b * N + W], start=True, stop=False)
                        m = mask_i1[:, b, :] if i else mask_i0[:, b, :]
                        ins = pe.matmul(dst, identb[:], m, start=False, stop=True)
                ins.then_inc(s_scored, 1)

            def turn(hp, u):
                i, bh, W = unit(u)
                pe.wait_ge(s_norm, hp * 4 + u + 1)
                n = hp * 3 + min(u, 2)
                if not (isinstance(hp, int) and hp * 3 + min(u, 2) == 0):
                    if 4 in pt_banks(u):
                        pe.wait_ge(s_pta, n)
                    if 5 in pt_banks(u):
                        pe.wait_ge(s_ptd, n)
                for hd in range(2):
                    for b2 in range(2):
                        for jt in range(i + 1):
                            n = blk(i, hd, b2, jt)
                            bank = pt_banks(u)[n // 4]
                            ins = pe.transpose(ps[:, bank, (n % 4) * P:(n % 4 + 1) * P],
                                               px[u][:, hd * 2 + b2, jt * P:(jt + 1) * P], identf[:])
                ins.then_inc(s_turn, 1)

            def mix(hp, u):
                i, bh, W = unit(u)
                n = hp * 3 + min(u, 2) + 1
                if 4 in pt_banks(u):
                    pe.wait_ge(s_pta, n)
                if 5 in pt_banks(u):
                    pe.wait_ge(s_ptd, n)
                if not (isinstance(hp, int) and hp * 4 + u == 0):
                    pe.wait_ge(s_oev, hp * 4 + u)
                for b2 in range(2):
                    for jt in range(i + 1):
                        for hd in range(2):
                            t = 2 * (2 * bh + b2) + jt
                            ins = pe.matmul(ps[hd * DH:(hd + 1) * DH, 6, b2 * P:(b2 + 1) * P], v_sb[:, t, :],
                                            pt[u % 2][:, blk(i, hd, b2, jt), :], start=(jt == 0), stop=(jt == i))
                ins.then_inc(s_pv, 1)

            def pair(hp, last=False):
                for u in range(4):
                    after(turn, hp, u, 3)
                    scores(hp, u)
                    after(mix, hp, u, 3)
                    if not last and u >= 2:
                        queries(hp + 1, u - 2)

            queries(0, 0)
            queries(0, 1)
            pe.wait_ge(s_pool0, 7)
            pe.wait_ge(s_act0, 4)
            pe.wait_ge(s_dve0, 33)
            pair(0)
            with pe.Fori(1, PAIRS_A - 1) as hp:
                pair(hp)
            pair(PAIRS_A - 1, last=True)
            for u in range(1, 4):
                turn(PAIRS_A - 1, u)
                mix(PAIRS_A - 1, u)
            pe.wait_ge(ev("w_chain"), W_STEPS)
            for h in range(HB):
                ins = pe.transpose(ps[:, 4, :].bitcast(BF16)[:, h * P:(h + 1) * P], wint[:, h, :], identb[:])
            ins.then_inc(ev("wq_turned"), 1)
            pe.wait_ge(ev("w_dequantised"), GB - HB)
            for g in range(2 * KVH):
                ins = pe.transpose(ps[:, 5, g * P:(g + 1) * P], wraw[:, HB + g, :], identf[:])
            ins.then_inc(ev("wkv_turned"), 1)
            pe.wait_ge(s_oev, PAIRS_A * 4)
            for h in range(HB):
                ins = pe.transpose(ps[:, 6 + h // 4, (h % 4) * P:(h % 4 + 1) * P], wraw[:, HB + 2 * KVH + h, :], identf[:])
            ins.then_inc(ev("wo_turned"), 1)
            pe.wait_ge(s_wo, 16)
            for t in range(T):
                for hp in range(PAIRS_A):
                    ins = pe.matmul(ps[:, t // 2, (t % 2) * P:(t % 2 + 1) * P], oT[:, hp, t * P:(t + 1) * P], wo_sb[:, hp, :],
                                    start=(hp == 0), stop=(hp == PAIRS_A - 1))
                ins.then_inc(s_wod, 1)


            def turn_x(name, bank, half):
                for t in range(4):
                    pe.wait_ge(ev(name + "_scaled"), half * 4 + t + 1)
                    ins = pe.transpose(ps[:, bank, t * P:(t + 1) * P], xh[:, half * 4 + t, :], identf[:])
                ins.then_inc(ev(name + "_turned"), 1)

            wkv_heads = wkvT[:].rearrange("p (g k c) -> p k g c", g=2, k=KVH)
            for half in range(2):
                pe.wait_ge(ev("woT_ready"), 1)
                turn_x("rms1", 6 + half, half)
                for kv in range(KVH):
                    pe.wait_ge(ev("xn1_ready"), 2 * half + 1 if kv == 0 or half == 0 else 4)
                    for t in range(4):
                        ins = pe.matmul(kv_psum(kv, half)[:, t], xnT[:, (half * 4 + t) * P:(half * 4 + t + 1) * P],
                                        wkv_heads[:, kv], start=True, stop=True)
                    ins.then_inc(ev("kv_product"), 1)

            def turn_keys(kv, half):
                pe.wait_ge(ev("k_ready"), order(kv, half) + 1)
                for t in range(4):
                    ins = pe.transpose(ps[:, key_bank(order(kv, half)), t * P:(t + 1) * P], k_rot[:, half * 4 + t, kv, :], identf[:])
                ins.then_inc(ev("k_turned"), 1)

            def queries_b(p, hd, k):
                f, h = p * 2 + hd, 2 * (p % PAIRS_B) + hd
                bank = 6 + k if p < 2 else 7
                n = 2 * f + k
                if p < 2:
                    n = n - 1
                if n > 0:
                    pe.wait_ge(ev("q_rotated"), n)
                half = p // PAIRS_B
                cols, w = slice(half * HALF, (half + 1) * HALF), (wqT, wqrT)[k]
                pe.matmul(ps[:, bank, :], w[:, h, :], x_hi[:, cols], start=True, stop=False)
                pe.matmul(ps[:, bank, :], w[:, h, :], x_lo[:, cols], start=False, stop=True).then_inc(ev("q_product_b"), 1)

            def scores_b(n):
                i, half, hp, W, u = unit_b(n)
                kv = hp * KVH // PAIRS_B
                pe.wait_ge(ev("q_summed"), 2 * (n // 2) + 2)
                if n >= 2:
                    pe.wait_ge(ev("exp_b"), n - 1)
                if hp * KVH == PAIRS_B * kv and i:
                    pe.wait_ge(ev("kT_ready"), order(kv, half) + 1)
                for hd in range(2):
                    for b2 in range(2):
                        b, t = 2 * half + b2, 2 * b2 + i
                        bank, c0 = (hd, b2 * W) if i else (2, (2 * hd + b2) * W)
                        pe.matmul(ps[:, bank, c0:c0 + W], qrT[n // 2 % 3][:, hd, t * P:(t + 1) * P],
                                  kT[:, kv, b * N:b * N + W], start=True, stop=False)
                        ins = pe.matmul(ps[:, bank, c0 + W - P:c0 + W], identb[:], causal[:], start=False, stop=True)
                ins.then_inc(ev("scored_b"), 1)

            def turn_b(n):
                i, half, hp, W, u = unit_b(n)
                pe.wait_ge(ev("normalised_b"), n + 1)
                for bank, copied in ((4, "copied_act_b"), (5, "copied_dve_b")):
                    if bank in banks_b(n) and copies_before(n, bank):
                        pe.wait_ge(ev(copied), copies_before(n, bank))
                for hd in range(2):
                    for b2 in range(2):
                        for jt in range(i + 1):
                            k = blk(i, hd, b2, jt)
                            ins = pe.transpose(ps[:, banks_b(n)[k // 4], (k % 4) * P:(k % 4 + 1) * P],
                                               px[u][:, hd * 2 + b2, jt * P:(jt + 1) * P], identf[:])
                ins.then_inc(ev("turned_b"), 1)

            def mix_b(n):
                i, half, hp, W, u = unit_b(n)
                kv = hp * KVH // PAIRS_B
                for bank, copied in ((4, "copied_act_b"), (5, "copied_dve_b")):
                    if bank in banks_b(n):
                        pe.wait_ge(ev(copied), copies_before(n, bank) + 1)
                if n:
                    pe.wait_ge(ev("mix_copied_b"), n)
                probs = pt[n % 2][:, 0:4 * (i + 1), :].rearrange("p (h b j) c -> p h b j c", h=2, b=2)
                mixed = ps[:, 6, :].rearrange("p (h b c) -> p h b c", h=2, b=2)
                for b2 in range(2):
                    for jt in range(i + 1):
                        t = 2 * (2 * half + b2) + jt
                        ins = pe.matmul(mixed[:, :, b2, :], kv_sb[:, t, KVH + kv, :], probs[:, :, b2, jt, :],
                                        start=(jt == 0), stop=(jt == i))
                ins.then_inc(ev("mixed_b"), 1)

            def o_tile(t, bank):
                for h in range(HB):
                    ins = pe.matmul(ps[:, bank, (t % 4) * P:(t % 4 + 1) * P], oT[:, h, t * P:(t + 1) * P], woT[:, h, :],
                                    start=(h == 0), stop=(h == HB - 1))
                ins.then_inc(ev("o_product"), 1)

            pe.wait_ge(ev("x_split"), 1)
            pe.wait_ge(ev("wqT_ready"), 3)
            pe.wait_ge(ev("kv_copied"), 3)
            for f in range(4):
                for k in range(2):
                    queries_b(f // 2, f % 2, k)
            turn_keys(0, 0)
            pe.wait_ge(ev("q_rotated"), 8)
            pe.wait_ge(ev("x_split"), 2)
            pe.wait_ge(ev("b_const"), 2)
            for n in range(UNITS_B):
                if n >= 3:
                    turn_b(n - 3)
                more = n // 2 + 2 < 2 * PAIRS_B
                if more:
                    queries_b(n // 2 + 2, n % 2, 0)
                scores_b(n)
                if more:
                    queries_b(n // 2 + 2, n % 2, 1)
                if n >= 3:
                    mix_b(n - 3)
                if n in (3, 7, 11):
                    if n > 3:
                        pe.wait_ge(ev("kT_ready"), 2 if n == 7 else 3)
                    turn_keys(*{3: (1, 0), 7: (0, 1), 11: (1, 1)}[n])
                if n >= UNITS_B - 4:
                    pe.wait_ge(ev("mix_copied_b"), UNITS_B // 2)
                    pe.wait_ge(ev("kT_ready"), 4)
                    o_tile(n - UNITS_B + 4, 3)
            last = UNITS_B - 1
            turn_b(last - 2)
            mix_b(last - 2)
            turn_b(last - 1)
            mix_b(last - 1)
            pe.transpose(ps[:, 7, WG0:WG0 + E], wg[:], identf[0:E, 0:E]).then_inc(ev("wg_turned"), 1)
            pe.wait_ge(ev("exp_b"), UNITS_B)
            turn_x("rms2", 0, 0)
            turn_b(last)
            mix_b(last)
            pe.wait_ge(ev("mix_copied_b"), 4 * PAIRS_B)

            def turn13(e):
                pe.wait_ge(ev("ints13"), e + 1)
                if positive(e):
                    pe.wait_ge(ev("w13T_ready"), e)
                for g in range(2 * FC):
                    ins = pe.transpose(ps[:, 4, :].bitcast(BF16)[:, g * FP:(g + 1) * FP], i13[:, g, :], identb[0:FP, 0:FP])
                ins.then_inc(ev("w13_turned"), 1)

            def turn2(q, part):
                pe.wait_ge(ev("w2_dequantised"), q + 1)
                if part:
                    pe.wait_ge(ev("w2T_ready"), q * 2 + 1)
                if isinstance(q, int) and q == 0:
                    if part:
                        pe.wait_ge(ev("rwb_ready"), 1)
                else:
                    pe.wait_ge(ev("rwb_ready"), q * 4 + 2)
                w = w2r.rearrange("r g c -> r (g c)").rearrange("r (a c f) -> r a c f", a=2, c=FC)
                for c in range(2):
                    for a in range(2):
                        n = c * 2 + a
                        ins = pe.transpose(ps[0:FP, 5, n * P:(n + 1) * P], w[:, a, 2 * part + c, :], identf[:])
                ins.then_inc(ev("w2_turned"), 1)

            def spread(q, j, half):
                if positive(q * 4 + j * 2 + half):
                    pe.wait_ge(ev("rwb_ready"), q * 4 + j * 2 + half)
                if j == 1:
                    pe.wait_ge(ev("w2T_ready"), q * 2 + 2)
                pe.matmul(ps[0:FP, 5, :], pick[:, bass.ts(q * 2 + j, 1), :].rearrange("p e f -> p (e f)"),
                          rwT[:, half * HALF:(half + 1) * HALF],
                          start=True, stop=True).then_inc(ev("rw_spread"), 1)

            turn13(0)

            def logits(half):
                for t in range(4):
                    n = 4 * half + t
                    ins = pe.matmul(ps[:, 7, t * E:(t + 1) * E], xnT[:, n * P:(n + 1) * P], wgT[:], start=True, stop=True)
                ins.then_inc(ev("logits"), 1)

            def zero_sums(half):
                pe.matmul(ps[:, 6 + half, :], zrow[:], finite, start=True, stop=False, skip_group_check=True)

            def turn_gates(half):
                pe.wait_ge(ev("rw_split"), half + 1)
                pe.wait_ge(ev("w2T_ready"), half + 1)
                if half:
                    pe.wait_ge(ev("rwb_ready"), 1)
                for t in range(4):
                    ins = pe.transpose(ps[0:3 * E, 5, :].bitcast(BF16)[:, t * P:(t + 1) * P],
                                       rw3[:, 4 * half + t].rearrange("p e s -> p (e s)"), identb[:])
                ins.then_inc(ev("rw_turned"), 1)
                pe.wait_ge(ev("rwT_ready"), half + 1)

            pe.wait_ge(ev("hn_ready"), 1)
            pe.wait_ge(ev("wgT_ready"), 1)
            logits(0)
            for t in range(4, T):
                if t == 6:
                    turn2(0, 0)
                o_tile(t, 6)
            turn_gates(0)
            pe.wait_ge(ev("pick_ready"), 1)
            spread(0, 0, 0)
            pe.wait_ge(ev("hn_split"), 1)
            pe.wait_ge(ev("zeros"), 1)

            def hidden(q, j, s):
                n = q * 16 + j * 8 + s
                half, c = s // FC, s % FC
                cols = slice(half * HALF, (half + 1) * HALF)
                k = s % 2
                if s == 0:
                    pe.wait_ge(ev("w13T_ready"), q * 2 + j + 1)
                if positive(n - 1):
                    pe.wait_ge(ev("gate_ready"), n - 1)
                pe.matmul(ps[0:FP, 2 * k, :], w13T[j][:, c, :], x_hi[:, cols], start=True, stop=False)
                pe.matmul(ps[0:FP, 2 * k, :], w13T[j][:, c, :], x_lo[:, cols], start=False, stop=True).then_inc(ev("gate_product"), 1)
                if positive(n - 1):
                    pe.wait_ge(ev("up_scaled"), n - 1)
                pe.matmul(ps[0:FP, 2 * k + 1, :], w13T[j][:, FC + c, :], x_hi[:, cols], start=True, stop=False)
                pe.matmul(ps[0:FP, 2 * k + 1, :], w13T[j][:, FC + c, :], x_lo[:, cols], start=False, stop=True).then_inc(ev("up_product"), 1)

            def down(q, j, s):
                half, c = s // FC, s % FC
                if j == 0 and s in (0, 2):
                    pe.wait_ge(ev("w2T_ready"), q * 2 + 1 + s // 2)
                pe.wait_ge(ev("up_ready"), q * 16 + j * 8 + s + 1)
                pe.matmul(ps[:, 6 + half, :], w2T[:, c, j, :], up[s % NBUF], start=False, stop=False,
                          skip_group_check=True).then_inc(ev("down"), 1)

            def pair_c(q, last=False):
                for j in range(2):
                    more = not (last and j == 1)
                    for s in range(8):
                        hidden(q, j, s)
                        if s >= 2:
                            down(q, j, s - 2)
                        elif j:
                            down(q, 0, s + 6)
                        elif not isinstance(q, int) or q:
                            down(q - 1, 1, s + 6)
                        first = isinstance(q, int) and (q, j) == (0, 0)
                        if first and s == 1:
                            pe.wait_ge(ev("hn_ready"), 4)
                            logits(1)
                        if s == 1 and j == 0:
                            turn2(q, 1)
                        if first and s == 0:
                            pe.wait_ge(ev("logits_copied"), 1)
                            turn_x("rms2", 7, 1)
                        if first and s == 1:
                            pe.wait_ge(ev("rms2_y"), 2)
                            zero_sums(0)
                        if first and s == 3:
                            pe.wait_ge(ev("hn_split"), 2)
                        if first and s == 4:
                            pe.wait_ge(ev("logits_copied"), 2)
                            zero_sums(1)
                        if first and s == 5:
                            turn_gates(1)
                            spread(0, 0, 1)
                        if s in ((6, 7) if first else (4, 5)) and more:
                            spread(*((q, 1) if j == 0 else (q + 1, 0)), s % 2)
                        if s == 6 and more:
                            turn13(q * 2 + j + 1)
                        if s == 7 and j == 1 and more:
                            turn2(q + 1, 0)

            pair_c(0)
            with pe.Fori(1, E // 2 - 1) as q:
                pair_c(q)
            pair_c(E // 2 - 1, last=True)
            down(E // 2 - 1, 1, 6)
            down(E // 2 - 1, 1, 7)
            for half in range(2):
                pe.matmul(ps[:, 6 + half, :], zrow[:], finite, start=False, stop=True,
                          skip_group_check=True).then_inc(ev("experts_summed"), 1)
            for t in range(T):
                pe.wait_ge(ev("moeT_ready"), t // 4 + 1)
                if t >= 4:
                    pe.wait_ge(ev("result"), t - 3)
                pe.transpose(ps[:, t % 4, 0:D], moeT[:, t * P:(t + 1) * P], identf[:]).then_inc(ev("moe_turned"), 1)


_NAMES = ["x", "fside_16xSxS_0", "cond_64", "mask_BxS_bk0", "L0_cond_g_in", "L0_cond_null_attn_bias", "L0_cond_Wq",
          "L0_cond_Wkv", "L0_cond_Wo", "L0_cond_g_out", "L0_ffn_w_q", "L0_ffn_w_k", "L0_ffn_w_v", "L0_ffn_w_o",
          "L0_ffn_g1", "L0_ffn_g2", "L0_ffn_w_gate", "L0_ffn_w1", "L0_ffn_w3", "L0_ffn_w2"]


def rope_tables(S, HD):
    inv = 1.0 / np.float32(1000000.0) ** (np.arange(0, HD, 2, dtype=np.float32) / np.float32(HD))
    freqs = np.arange(S, dtype=np.float32)[:, None] * inv[None, :].astype(np.float32)
    emb = np.concatenate([freqs, freqs], -1).astype(np.float32)
    sign = np.where(np.arange(HD) < HD // 2, -1.0, 1.0).astype(np.float32)
    tok = np.stack([np.cos(emb), np.sin(emb) * sign], 1).astype(np.float32)
    return np.ascontiguousarray(tok), np.ascontiguousarray(tok.transpose(2, 1, 0))


def kernel(**inputs):
    import concourse.bacc as bacc
    from concourse.bass_utils import run_bass_kernel_spmd

    nc = bacc.Bacc("TRN2", target_bir_lowering=False, num_devices=1)
    arrays, args = {}, []

    def give(name, a):
        arrays[name] = a
        args.append(nc.dram_tensor(name, a.shape, mybir.dt.from_np(a.dtype), kind="ExternalInput").ap())

    for name in _NAMES:
        give(f"in_{name}", np.ascontiguousarray(inputs[name]))
    tok, feat = rope_tables(256, 128)
    give("in_rope_tok", tok)
    give("in_rope_feat", feat)
    args.append(nc.dram_tensor("out_0", inputs["x"].shape, F32, kind="ExternalOutput").ap())
    build(nc, *args)
    r = run_bass_kernel_spmd(nc, [arrays], core_ids=[0])
    return r.results[0]["out_0"]
```
